# Optimizing a Trainium2 kernel written in Bass

```python
import numpy as np
import jax
import jax.numpy as jnp

def _softmax(x, axis=-1):
    return jax.nn.softmax(x, axis=axis)
def _gelu(x):
    return jax.nn.gelu(x, approximate=True)
def _silu(x):
    return jax.nn.silu(x)
def _sigmoid(x):
    return jax.nn.sigmoid(x)
def _layernorm(x, axis=-1, eps=1e-5):
    m = jnp.mean(x, axis=axis, keepdims=True)
    v = jnp.var(x, axis=axis, keepdims=True)
    return (x - m) / jnp.sqrt(v + eps)
def _scatter_add(tgt, idx, src, axis=0):
    return tgt.at[idx].add(src)
def _segment_sum(src, seg, n):
    return jax.ops.segment_sum(src, seg, n)

kernel_name = 'mk_conv_preact_d4_conv_nchw384_5d5402'

def setup_inputs(seed: int = 0):
    np.random.seed(seed)
    _w = jnp.asarray
    def _rec_inputs():
        import jax
        import jax.numpy as jnp
        _gk = jax.random.key(seed)
        x = -0.0005963 + 1.001 * jax.random.normal(jax.random.fold_in(_gk, 1), (8, 384, 32, 32), jnp.float32)
        return x
    x = _rec_inputs()
    def _L0_conv_setup():
        import jax, jax.numpy as jnp
        import numpy as np
        DIM = 384
        HEADS = 8
        key = jax.random.key(seed)
        k_x, k_qkv, k_pw, k_pb = jax.random.split(key, 4)
        x = jax.random.normal(k_x, (8, DIM, 32, 32), dtype=jnp.float32)
        w_qkv = jax.random.normal(k_qkv, (3 * DIM, DIM), dtype=jnp.float32) * DIM ** (-0.5)
        w_proj = jax.random.normal(k_pw, (DIM, DIM), dtype=jnp.float32) * DIM ** (-0.5)
        b_proj = jax.random.normal(k_pb, (DIM,), dtype=jnp.float32) * 0.02
        return {'x': x, 'w_qkv': w_qkv, 'w_proj': w_proj, 'b_proj': b_proj}
    _L0_conv_all = _L0_conv_setup()
    _L0_conv_in = {k: v for k, v in _L0_conv_all.items() if k in ('w_qkv', 'w_proj', 'b_proj', )}
    del _L0_conv_all

    def _L1_conv_setup():
        import jax, jax.numpy as jnp
        import numpy as np

        def conv2d(x, w, b=None, pad=0):
            out = jax.lax.conv_general_dilated(x, w, window_strides=(1, 1), padding=[(pad, pad), (pad, pad)], dimension_numbers=('NCHW', 'OIHW', 'NCHW'))
            return out if b is None else out + b[None, :, None, None]

        def deform_depthwise(x, offsets, w, K, pad):
            B, C, H, W = x.shape
            K2 = K * K
            off = offsets.reshape(B, K2, 2, H, W).transpose(1, 0, 2, 3, 4)
            wk = w.reshape(C, K2).T
            ky = jnp.repeat(jnp.arange(K), K).astype(x.dtype)
            kx = jnp.tile(jnp.arange(K), K).astype(x.dtype)
            gy = jnp.arange(H, dtype=x.dtype)[:, None] - pad
            gx = jnp.arange(W, dtype=x.dtype)[None, :] - pad
            xf = x.reshape(B, C, H * W)

            def sample(py, px):
                y0 = jnp.floor(py)
                x0 = jnp.floor(px)
                dy = py - y0
                dx = px - x0

                def corner(yi, xi, wgt):
                    valid = (yi >= 0) & (yi <= H - 1) & (xi >= 0) & (xi <= W - 1)
                    yc = jnp.clip(yi, 0, H - 1).astype(jnp.int32)
                    xc = jnp.clip(xi, 0, W - 1).astype(jnp.int32)
                    idx = (yc * W + xc).reshape(B, 1, H * W)
                    v = jnp.take_along_axis(xf, idx, axis=2).reshape(B, C, H, W)
                    return v * (wgt * valid.astype(x.dtype))[:, None]
                return corner(y0, x0, (1 - dy) * (1 - dx)) + corner(y0, x0 + 1, (1 - dy) * dx) + corner(y0 + 1, x0, dy * (1 - dx)) + corner(y0 + 1, x0 + 1, dy * dx)

            def body(acc, inp):
                o_k, w_k, ky_k, kx_k = inp
                py = gy[None] + ky_k + o_k[:, 0]
                px = gx[None] + kx_k + o_k[:, 1]
                return (acc + sample(py, px) * w_k[None, :, None, None], None)
            acc, _ = jax.lax.scan(body, jnp.zeros_like(x), (off, wk, ky, kx))
            return acc

        def deform_block(x, ow, ob, dw, pw, pb, K):
            pad = K // 2
            offsets = conv2d(x, ow, ob, pad)
            out = deform_depthwise(x, offsets, dw, K, pad)
            return conv2d(out, pw, pb, 0)

        def se_weight(x, fc1_w, fc2_w):

            def branch(p):
                return conv2d(jax.nn.relu(conv2d(p, fc1_w)), fc2_w)
            avg = jnp.mean(x, axis=(2, 3), keepdims=True)
            mx = jnp.max(x, axis=(2, 3), keepdims=True)
            return jax.nn.sigmoid(branch(avg) + branch(mx))
        key = jax.random.key(seed)
        ks = jax.random.split(key, 20)
        B, Cin, H, W = (8, 384, 96, 96)
        Cs = Cin // 3
        d = {'x': jax.random.normal(ks[0], (B, Cin, H, W), dtype=jnp.float32)}
        i = 1
        for K in (3, 5, 7):
            d[f'offset_w{K}'] = jax.random.normal(ks[i], (2 * K * K, Cs, K, K)) * 0.01
            i += 1
            d[f'offset_b{K}'] = jax.random.normal(ks[i], (2 * K * K,)) * 0.01
            i += 1
            d[f'dw_w{K}'] = jax.random.normal(ks[i], (Cs, K, K)) * (1.0 / K)
            i += 1
            d[f'pw_w{K}'] = jax.random.normal(ks[i], (Cs, Cs, 1, 1)) * Cs ** (-0.5)
            i += 1
            d[f'pw_b{K}'] = jnp.zeros((Cs,))
            i += 1
        d['fc1_w'] = jax.random.normal(ks[i], (Cin // 16, Cin, 1, 1)) * 0.05
        i += 1
        d['fc2_w'] = jax.random.normal(ks[i], (Cin, Cin // 16, 1, 1)) * 0.05
        return d
    _L1_conv_all = _L1_conv_setup()
    _L1_conv_in = {k: v for k, v in _L1_conv_all.items() if k in ('offset_w3', 'offset_b3', 'dw_w3', 'pw_w3', 'pw_b3', 'offset_w5', 'offset_b5', 'dw_w5', 'pw_w5', 'pw_b5', 'offset_w7', 'offset_b7', 'dw_w7', 'pw_w7', 'pw_b7', 'fc1_w', 'fc2_w', )}
    del _L1_conv_all

    def _L2_conv_setup():
        import jax, jax.numpy as jnp
        import numpy as np
        EPS = 1e-12
        key = jax.random.key(seed)
        k1, k2, k3 = jax.random.split(key, 3)
        b, c, H, W = (16, 384, 48, 48)
        heads = 8
        x = jax.random.normal(k1, (b, c, H, W), dtype=jnp.float32)
        w_qkv = jax.random.normal(k2, (c, 3 * c), dtype=jnp.float32) / np.sqrt(c)
        temperature = jnp.ones((1, heads, 1, 1), dtype=jnp.float32)
        w_out = jax.random.normal(k3, (c, c), dtype=jnp.float32) / np.sqrt(c)
        b_out = jnp.zeros((c,), dtype=jnp.float32)
        return {'x': x, 'w_qkv': w_qkv, 'temperature': temperature, 'w_out': w_out, 'b_out': b_out}
    _L2_conv_all = _L2_conv_setup()
    _L2_conv_in = {k: v for k, v in _L2_conv_all.items() if k in ('w_qkv', 'temperature', 'w_out', 'b_out', )}
    del _L2_conv_all

    def _L3_conv_setup():
        import jax, jax.numpy as jnp
        import numpy as np
        from jax import lax
        C = 384
        B, H, W = (16, 56, 56)
        EPS = 1e-05
        KS = [5, 7, 7, 3, 3, 3]
        DIL = [1, 1, 2, 3, 4, 5]

        def _dwconv(x, w, dilation):
            k = w.shape[-1]
            p = (dilation * (k - 1) + 1) // 2
            return lax.conv_general_dilated(x, w, window_strides=(1, 1), padding=[(p, p), (p, p)], rhs_dilation=(dilation, dilation), dimension_numbers=('NCHW', 'OIHW', 'NCHW'), feature_group_count=x.shape[1])

        def _bn(x, p):
            g, b, m, v = (p[0], p[1], p[2], p[3])
            scale = (g * lax.rsqrt(v + EPS)).reshape(1, -1, 1, 1)
            shift = (b - m * g * lax.rsqrt(v + EPS)).reshape(1, -1, 1, 1)
            return x * scale + shift
        key = jax.random.key(seed)
        ks = jax.random.split(key, 10)
        inp = {'x': jax.random.normal(ks[0], (B, C, H, W), jnp.float32), 'lk_w': jax.random.normal(ks[1], (C, 1, 13, 13), jnp.float32) * 0.05, 'obn': jax.random.uniform(ks[2], (4, C), jnp.float32), 'w5': jax.random.normal(ks[3], (C, 1, 5, 5), jnp.float32) * 0.05, 'w7a': jax.random.normal(ks[4], (C, 1, 7, 7), jnp.float32) * 0.05, 'w7b': jax.random.normal(ks[5], (C, 1, 7, 7), jnp.float32) * 0.05, 'w3a': jax.random.normal(ks[6], (C, 1, 3, 3), jnp.float32) * 0.05, 'w3b': jax.random.normal(ks[7], (C, 1, 3, 3), jnp.float32) * 0.05, 'w3c': jax.random.normal(ks[8], (C, 1, 3, 3), jnp.float32) * 0.05, 'br_bn': jax.random.uniform(ks[9], (6, 4, C), jnp.float32)}
        return inp
    _L3_conv_all = _L3_conv_setup()
    _L3_conv_in = {k: v for k, v in _L3_conv_all.items() if k in ('lk_w', 'obn', 'w5', 'w7a', 'w7b', 'w3a', 'w3b', 'w3c', 'br_bn', )}
    del _L3_conv_all

    return {
        "x": x,
        "L0_conv_w_qkv": _L0_conv_in["w_qkv"],
        "L0_conv_w_proj": _L0_conv_in["w_proj"],
        "L0_conv_b_proj": _L0_conv_in["b_proj"],
        "L1_conv_offset_w3": _L1_conv_in["offset_w3"],
        "L1_conv_offset_b3": _L1_conv_in["offset_b3"],
        "L1_conv_dw_w3": _L1_conv_in["dw_w3"],
        "L1_conv_pw_w3": _L1_conv_in["pw_w3"],
        "L1_conv_pw_b3": _L1_conv_in["pw_b3"],
        "L1_conv_offset_w5": _L1_conv_in["offset_w5"],
        "L1_conv_offset_b5": _L1_conv_in["offset_b5"],
        "L1_conv_dw_w5": _L1_conv_in["dw_w5"],
        "L1_conv_pw_w5": _L1_conv_in["pw_w5"],
        "L1_conv_pw_b5": _L1_conv_in["pw_b5"],
        "L1_conv_offset_w7": _L1_conv_in["offset_w7"],
        "L1_conv_offset_b7": _L1_conv_in["offset_b7"],
        "L1_conv_dw_w7": _L1_conv_in["dw_w7"],
        "L1_conv_pw_w7": _L1_conv_in["pw_w7"],
        "L1_conv_pw_b7": _L1_conv_in["pw_b7"],
        "L1_conv_fc1_w": _L1_conv_in["fc1_w"],
        "L1_conv_fc2_w": _L1_conv_in["fc2_w"],
        "L2_conv_w_qkv": _L2_conv_in["w_qkv"],
        "L2_conv_temperature": _L2_conv_in["temperature"],
        "L2_conv_w_out": _L2_conv_in["w_out"],
        "L2_conv_b_out": _L2_conv_in["b_out"],
        "L3_conv_lk_w": _L3_conv_in["lk_w"],
        "L3_conv_obn": _L3_conv_in["obn"],
        "L3_conv_w5": _L3_conv_in["w5"],
        "L3_conv_w7a": _L3_conv_in["w7a"],
        "L3_conv_w7b": _L3_conv_in["w7b"],
        "L3_conv_w3a": _L3_conv_in["w3a"],
        "L3_conv_w3b": _L3_conv_in["w3b"],
        "L3_conv_w3c": _L3_conv_in["w3c"],
        "L3_conv_br_bn": _L3_conv_in["br_bn"],
    }

def reference(x, L0_conv_w_qkv, L0_conv_w_proj, L0_conv_b_proj, L1_conv_offset_w3, L1_conv_offset_b3, L1_conv_dw_w3, L1_conv_pw_w3, L1_conv_pw_b3, L1_conv_offset_w5, L1_conv_offset_b5, L1_conv_dw_w5, L1_conv_pw_w5, L1_conv_pw_b5, L1_conv_offset_w7, L1_conv_offset_b7, L1_conv_dw_w7, L1_conv_pw_w7, L1_conv_pw_b7, L1_conv_fc1_w, L1_conv_fc2_w, L2_conv_w_qkv, L2_conv_temperature, L2_conv_w_out, L2_conv_b_out, L3_conv_lk_w, L3_conv_obn, L3_conv_w5, L3_conv_w7a, L3_conv_w7b, L3_conv_w3a, L3_conv_w3b, L3_conv_w3c, L3_conv_br_bn):
    import jax
    import jax.numpy as jnp
    def _L0_conv_ref(x, w_qkv, w_proj, b_proj):
        import jax, jax.numpy as jnp
        import numpy as np
        DIM = 384
        HEADS = 8
        B, C, H, W = x.shape
        h = HEADS
        d = C // h
        scale = d ** (-0.5)
        qkv = jnp.einsum('oc,bchw->bohw', w_qkv, x)
        q, k, v = jnp.split(qkv, 3, axis=1)

        def to_heads(y):
            return y.reshape(B, h, d, H * W).transpose(0, 1, 3, 2)
        q, k, v = (to_heads(q), to_heads(k), to_heads(v))
        att = jnp.einsum('bhxd,bhyd->bhxy', q * scale, k)
        att = jax.nn.softmax(att, axis=-1)
        out = jnp.einsum('bhxy,bhyd->bhxd', att, v)
        out = out.transpose(0, 1, 3, 2).reshape(B, C, H, W)
        out = jnp.einsum('oc,bchw->bohw', w_proj, out) + b_proj[None, :, None, None]
        return out

    def _L1_conv_ref(x, offset_w3, offset_b3, dw_w3, pw_w3, pw_b3, offset_w5, offset_b5, dw_w5, pw_w5, pw_b5, offset_w7, offset_b7, dw_w7, pw_w7, pw_b7, fc1_w, fc2_w):
        import jax, jax.numpy as jnp
        import numpy as np

        def conv2d(x, w, b=None, pad=0):
            out = jax.lax.conv_general_dilated(x, w, window_strides=(1, 1), padding=[(pad, pad), (pad, pad)], dimension_numbers=('NCHW', 'OIHW', 'NCHW'))
            return out if b is None else out + b[None, :, None, None]

        def deform_depthwise(x, offsets, w, K, pad):
            B, C, H, W = x.shape
            K2 = K * K
            off = offsets.reshape(B, K2, 2, H, W).transpose(1, 0, 2, 3, 4)
            wk = w.reshape(C, K2).T
            ky = jnp.repeat(jnp.arange(K), K).astype(x.dtype)
            kx = jnp.tile(jnp.arange(K), K).astype(x.dtype)
            gy = jnp.arange(H, dtype=x.dtype)[:, None] - pad
            gx = jnp.arange(W, dtype=x.dtype)[None, :] - pad
            xf = x.reshape(B, C, H * W)

            def sample(py, px):
                y0 = jnp.floor(py)
                x0 = jnp.floor(px)
                dy = py - y0
                dx = px - x0

                def corner(yi, xi, wgt):
                    valid = (yi >= 0) & (yi <= H - 1) & (xi >= 0) & (xi <= W - 1)
                    yc = jnp.clip(yi, 0, H - 1).astype(jnp.int32)
                    xc = jnp.clip(xi, 0, W - 1).astype(jnp.int32)
                    idx = (yc * W + xc).reshape(B, 1, H * W)
                    v = jnp.take_along_axis(xf, idx, axis=2).reshape(B, C, H, W)
                    return v * (wgt * valid.astype(x.dtype))[:, None]
                return corner(y0, x0, (1 - dy) * (1 - dx)) + corner(y0, x0 + 1, (1 - dy) * dx) + corner(y0 + 1, x0, dy * (1 - dx)) + corner(y0 + 1, x0 + 1, dy * dx)

            def body(acc, inp):
                o_k, w_k, ky_k, kx_k = inp
                py = gy[None] + ky_k + o_k[:, 0]
                px = gx[None] + kx_k + o_k[:, 1]
                return (acc + sample(py, px) * w_k[None, :, None, None], None)
            acc, _ = jax.lax.scan(body, jnp.zeros_like(x), (off, wk, ky, kx))
            return acc

        def deform_block(x, ow, ob, dw, pw, pb, K):
            pad = K // 2
            offsets = conv2d(x, ow, ob, pad)
            out = deform_depthwise(x, offsets, dw, K, pad)
            return conv2d(out, pw, pb, 0)

        def se_weight(x, fc1_w, fc2_w):

            def branch(p):
                return conv2d(jax.nn.relu(conv2d(p, fc1_w)), fc2_w)
            avg = jnp.mean(x, axis=(2, 3), keepdims=True)
            mx = jnp.max(x, axis=(2, 3), keepdims=True)
            return jax.nn.sigmoid(branch(avg) + branch(mx))
        c3, c5, c7 = jnp.split(x, 3, axis=1)
        out3 = deform_block(c3, offset_w3, offset_b3, dw_w3, pw_w3, pw_b3, 3)
        out5 = deform_block(c5, offset_w5, offset_b5, dw_w5, pw_w5, pw_b5, 5)
        out7 = deform_block(c7, offset_w7, offset_b7, dw_w7, pw_w7, pw_b7, 7)
        out = jnp.concatenate([out3, out5, out7], axis=1)
        return out * se_weight(out, fc1_w, fc2_w)

    def _L2_conv_ref(x, w_qkv, temperature, w_out, b_out):
        import jax, jax.numpy as jnp
        import numpy as np
        EPS = 1e-12
        b, c, H, W = x.shape
        h = temperature.shape[1]
        d = c // h
        n = H * W
        xt = x.reshape(b, c, n).transpose(0, 2, 1)
        qkv = xt @ w_qkv
        q, k, v = jnp.split(qkv, 3, axis=-1)
        q = q.reshape(b, n, h, d).transpose(0, 2, 1, 3)
        k = k.reshape(b, n, h, d).transpose(0, 2, 3, 1)
        v = v.reshape(b, n, h, d).transpose(0, 2, 1, 3)
        q = q / jnp.maximum(jnp.sqrt(jnp.sum(q * q, axis=-2, keepdims=True)), EPS)
        k = k / jnp.maximum(jnp.sqrt(jnp.sum(k * k, axis=-1, keepdims=True)), EPS)
        k = k * temperature
        attn = jnp.einsum('bhpn,bhnq->bhpq', k, q)
        attn = jax.nn.softmax(attn, axis=-1)
        out = jnp.einsum('bhnp,bhpq->bhnq', v, attn)
        out = out.transpose(0, 2, 1, 3).reshape(b, n, c)
        out = out @ w_out + b_out
        out = out.transpose(0, 2, 1).reshape(b, c, H, W)
        return out

    def _L3_conv_ref(x, lk_w, obn, w5, w7a, w7b, w3a, w3b, w3c, br_bn):
        import jax, jax.numpy as jnp
        import numpy as np
        from jax import lax
        C = 384
        B, H, W = (16, 56, 56)
        EPS = 1e-05
        KS = [5, 7, 7, 3, 3, 3]
        DIL = [1, 1, 2, 3, 4, 5]

        def _dwconv(x, w, dilation):
            k = w.shape[-1]
            p = (dilation * (k - 1) + 1) // 2
            return lax.conv_general_dilated(x, w, window_strides=(1, 1), padding=[(p, p), (p, p)], rhs_dilation=(dilation, dilation), dimension_numbers=('NCHW', 'OIHW', 'NCHW'), feature_group_count=x.shape[1])

        def _bn(x, p):
            g, b, m, v = (p[0], p[1], p[2], p[3])
            scale = (g * lax.rsqrt(v + EPS)).reshape(1, -1, 1, 1)
            shift = (b - m * g * lax.rsqrt(v + EPS)).reshape(1, -1, 1, 1)
            return x * scale + shift
        out = _bn(_dwconv(x, lk_w, 1), obn)
        ws = [w5, w7a, w7b, w3a, w3b, w3c]
        for i, (w, r) in enumerate(zip(ws, DIL)):
            out = out + _bn(_dwconv(x, w, r), br_bn[i])
        return out

    def _gn(v, G=32, eps=1e-5):
        B_, C_, H_, W_ = v.shape
        g = v.reshape(B_, G, C_ // G, H_, W_)
        m = jnp.mean(g, axis=(2, 3, 4), keepdims=True)
        s = jnp.var(g, axis=(2, 3, 4), keepdims=True)
        return ((g - m) / jnp.sqrt(s + eps)).reshape(v.shape)

    def _ln_c(v, eps=1e-6):
        m = jnp.mean(v, axis=1, keepdims=True)
        s = jnp.var(v, axis=1, keepdims=True)
        return (v - m) / jnp.sqrt(s + eps)

    def _ln_t(v, eps=1e-5):
        m = jnp.mean(v, axis=-1, keepdims=True)
        s = jnp.var(v, axis=-1, keepdims=True)
        return (v - m) / jnp.sqrt(s + eps)

    def _to_tokens(v):
        B_, C_, H_, W_ = v.shape
        return v.reshape(B_, C_, H_ * W_).transpose(0, 2, 1)
    def _from_tokens(t, like):
        B_, C_, H_, W_ = like.shape
        return t.transpose(0, 2, 1).reshape(B_, C_, H_, W_)

    x = x + _L0_conv_ref(_gn(x), L0_conv_w_qkv, L0_conv_w_proj, L0_conv_b_proj)
    x = x + _L1_conv_ref(_gn(x), L1_conv_offset_w3, L1_conv_offset_b3, L1_conv_dw_w3, L1_conv_pw_w3, L1_conv_pw_b3, L1_conv_offset_w5, L1_conv_offset_b5, L1_conv_dw_w5, L1_conv_pw_w5, L1_conv_pw_b5, L1_conv_offset_w7, L1_conv_offset_b7, L1_conv_dw_w7, L1_conv_pw_w7, L1_conv_pw_b7, L1_conv_fc1_w, L1_conv_fc2_w)
    x = x + _L2_conv_ref(_gn(x), L2_conv_w_qkv, L2_conv_temperature, L2_conv_w_out, L2_conv_b_out)
    x = x + _L3_conv_ref(_gn(x), L3_conv_lk_w, L3_conv_obn, L3_conv_w5, L3_conv_w7a, L3_conv_w7b, L3_conv_w3a, L3_conv_w3b, L3_conv_w3c, L3_conv_br_bn)
    return x


_drawn_inputs = setup_inputs


def setup_inputs(seed=0):
    import zlib

    import numpy as np

    out = dict(_drawn_inputs(seed))
    spreads = {'L1_conv_pw_b3': (0.0, 0.687),
     'L1_conv_pw_b5': (0.0, 0.674),
     'L1_conv_pw_b7': (0.0, 0.732),
     'L2_conv_temperature': (1.0, 0.6),
     'L2_conv_b_out': (0.0, 0.1)}
    factors = {'L0_conv_b_proj': 5.782,
     'L1_conv_offset_b3': 34.823,
     'L1_conv_offset_b5': 8.0,
     'L1_conv_offset_b7': 25.498,
     'L1_conv_fc1_w': 3.364}
    for name, (base, spread) in spreads.items():
        noise = np.random.default_rng([zlib.crc32(name.encode()), seed]).standard_normal(out[name].shape)
        drawn = base * np.exp(spread * noise) if base else spread * noise
        out[name] = jnp.asarray(drawn.astype(out[name].dtype))
    for name, factor in factors.items():
        out[name] = (out[name] * factor).astype(out[name].dtype)
    return out
```

```python
from contextlib import ExitStack

import concourse.bass as bass
from concourse import mybir
from concourse.alu_op_type import AluOpType as ALU

F32 = mybir.dt.float32
F16 = mybir.dt.float16
BF16 = mybir.dt.bfloat16
I32 = mybir.dt.int32
ACT = mybir.ActivationFunctionType
AX = mybir.AxisListType.X

P = 128
B = 8
C = 384
G3 = C // P
H = W = 32
N = H * W
HALF = N // 2
GROUPS = 32
CPG = C // GROUPS
HEADS = 8
D = C // HEADS
PAIRS = HEADS // 2
TP = 64 + D
NT = N // P
ROWB = P // W


def ds(start, size):
    return bass.DynSlice(start, size)


class Arena:

    def __init__(self, nc, tag):
        self.nc, self.tag, self.stack, self.sems = nc, tag, ExitStack(), []

    def __enter__(self):
        self.stack.__enter__()
        return self

    def __exit__(self, *e):
        if self.sems and e[0] is None:
            clear(self.nc, self.sems)
        return self.stack.__exit__(*e)

    def sb(self, name, shape, dt=F32):
        return self.stack.enter_context(self.nc.sbuf_tensor(f"{self.tag}_{name}", shape, dt))

    def ps(self, name, shape, dt=F32):
        return self.stack.enter_context(self.nc.psum_tensor(f"{self.tag}_{name}", shape, dt))

    def sem(self, name):
        self.sems.append(self.stack.enter_context(self.nc.semaphore(f"{self.tag}_{name}")))
        return self.sems[-1]


def clear(nc, sems):
    with nc.Block() as block:

        @block.sync
        def _(e):
            for sem in sems:
                e.sem_clear(sem)


def at(i, per, k):
    return i * per + max(k, 0)


def hold(sh, e, sem, value):
    e.wait_ge(sem, value)
    e.sem_inc(sh["tick"], 1)


class Chain:

    def __init__(self, sh, eng, sem, i=None, per=0):
        self.sh = sh
        self.eng, self.sem, self.i, self.per, self.n = eng, sem, i, per, 0

    def __call__(self, ins):
        ins.then_inc(self.sem, 1)
        self.n += 1
        if self.i is None:
            self.eng.wait_ge(self.sem, self.n)
        else:
            hold(self.sh, self.eng, self.sem, self.i * self.per + self.n)

    def end(self):
        assert self.i is None or self.n == self.per, (self.n, self.per)


def load_shared(nc, sh, consts):
    with Arena(nc, "ld") as a, nc.Block() as block:
        s = a.sem("s")

        @block.sync
        def _(e):
            e.dma_start(sh["ident"][:], consts["ident"]).then_inc(s, 16)
            e.dma_start(sh["gmat"][:], consts["gmat"].rearrange("g p n -> p g n")).then_inc(s, 16)
            e.dma_start(sh["gmatT"][:], consts["gmatT"]).then_inc(s, 16)
            e.wait_ge(s, 48)


def norm_params(nc, sh, tag):
    with Arena(nc, tag) as a:
        mv = a.sb("mv", [P, G3, B, 2])
        sq = a.sb("sq", [P, G3, B])
        grp = a.sb("grp", [GROUPS, B, 2])
        gsq = a.sb("gsq", [GROUPS, B])
        bank = a.ps("bank", [P, 1 + G3, B * 2])
        p_grp = bank[0:GROUPS, 0, :]
        p_ch = bank[:, 1:1 + G3, :]
        s_d, s_dc, s_pe, s_a = a.sem("d"), a.sem("dc"), a.sem("pe"), a.sem("a")
        with nc.Block() as block:

            @block.vector
            def _(e):
                link = Chain(sh, e, s_dc)
                for g in range(G3):
                    for b in range(B):
                        last = e.bn_aggr(mv[:, g, b, :], sh["stat"][:, g, b, :, :].rearrange("p a s -> p (a s)"))
                link(last)
                link(e.tensor_tensor(sq[:], mv[:, :, :, 0], mv[:, :, :, 0], ALU.mult))
                e.tensor_tensor(mv[:, :, :, 1], mv[:, :, :, 1], sq[:], ALU.add).then_inc(s_d, 1)
                e.wait_ge(s_pe, 1)
                link(e.tensor_scalar(grp[:].rearrange("p b s -> p (b s)"), p_grp, 1.0 / CPG, None, ALU.mult))
                link(e.tensor_tensor(gsq[:], grp[:, :, 0], grp[:, :, 0], ALU.mult))
                link(e.tensor_tensor(gsq[:], grp[:, :, 1], gsq[:], ALU.subtract))
                e.tensor_scalar(gsq[:], gsq[:], 1e-5, None, ALU.add).then_inc(s_d, 1)
                e.wait_ge(s_a, 1)
                e.reciprocal(grp[:, :, 1], gsq[:]).then_inc(s_d, 1)
                e.wait_ge(s_pe, 2)
                e.tensor_copy(sh["gn"][:].rearrange("p g b s -> p g (b s)"), p_ch).then_inc(s_d, 1)
                e.wait_ge(s_d, 4)

            @block.scalar
            def _(e):
                e.wait_ge(s_d, 2)
                e.activation(gsq[:], gsq[:], ACT.Sqrt).then_inc(s_a, 1)

            @block.tensor
            def _(e):
                e.wait_ge(s_d, 1)
                for g in range(G3):
                    last = e.matmul(p_grp, sh["gmat"][:, g, :], mv[:, g, :, :].rearrange("p b s -> p (b s)"),
                                    start=(g == 0), stop=(g == G3 - 1))
                last.then_inc(s_pe, 1)
                e.wait_ge(s_d, 3)
                for g in range(G3):
                    last = e.matmul(p_ch[:, g, :], sh["gmatT"][:, g, :], grp[:].rearrange("p b s -> p (b s)"),
                                    start=True, stop=True)
                last.then_inc(s_pe, 1)


def layer0(nc, sh, x, w_qk, w_v, w_proj, b_proj, y):
    xv = x.rearrange("b (g p) n -> p b g n", p=P)
    yv = y.rearrange("b (g p) n -> p b g n", p=P)
    NTILE = 2 * NT
    with Arena(nc, "a") as a:
        xs = a.sb("xs", [P, B, G3, N])
        h = a.sb("h", [P, G3, N])
        wqk = a.sb("wqk", [P, G3, 2, TP])
        wv = a.sb("wv", [P, G3, C])
        wp = a.sb("wp", [TP, PAIRS, C])
        bp = a.sb("bp", [P, G3])
        q = a.sb("q", [TP, N])
        k = a.sb("k", [TP, N])
        v = a.sb("v", [P, 2, NT, TP])
        att = a.sb("att", [P, 2, N])
        attT = a.sb("attT", [P, 2, NT, HALF])
        nmax = a.sb("nmax", [P, 2])
        rden = a.sb("rden", [P, HALF])
        o = a.sb("o", [TP, PAIRS, N])
        p_s = [a.ps(f"p_s{i}", [P, 2, HALF]) for i in range(2)]
        p_t = a.ps("p_t", [P, NT, P])
        p_o = a.ps("p_o", [P, HALF])
        s_x = [a.sem(f"x{b}") for b in range(B)]
        s_w, s_wqk, s_y = a.sem("w"), a.sem("wqk"), a.sem("y")
        s_st, s_z, s_h, s_pj, s_q, s_k, s_v = (a.sem(n) for n in ("st", "z", "h", "pj", "q", "k", "v"))
        s_s, s_m, s_e, s_t, s_ta, s_tv = (a.sem(n) for n in ("s", "m", "e", "t", "ta", "tv"))
        s_o, s_on, s_rd, s_f, s_fo = (a.sem(n) for n in ("o", "on", "rd", "f", "fo"))

        with nc.Block() as block:

            @block.sync
            def _(e):
                for b in range(B):
                    e.dma_start(xs[:, b, :, :], xv[:, b, :, :]).then_inc(s_x[b], 16)
                e.dma_start(wv[:], w_v.rearrange("(g p) n -> p g n", p=P)).then_inc(s_w, 16)
                e.dma_start(wp[:], w_proj).then_inc(s_w, 16)
                e.dma_start(bp[:], b_proj.rearrange("(g p) -> p g", p=P), allow_slow_non_contiguous=True).then_inc(s_w, 16)
                e.wait_ge(s_w, 48)

            @block.gpsimd
            def _(e):
                e.memset(v[:], 0.0).then_inc(s_z, 1)
                e.memset(o[:], 0.0).then_inc(s_z, 1)
                e.wait_ge(s_z, 2)
                e.memset(v[:, 0, :, 64:TP], 1.0).then_inc(s_z, 1)
                e.memset(v[:, 1, :, 0:D], 1.0).then_inc(s_z, 1)
                e.wait_ge(s_z, 4)

            @block.vector
            def _(e):
                for b in range(B):
                    e.wait_ge(s_x[b], 16)
                    for g in range(G3):
                        for n in range(2):
                            last = e.bn_stats(sh["stat"][:, g, b, n, :], xs[:, b, g, n * HALF:(n + 1) * HALF])
                last.then_inc(s_st, 1)
                e.wait_ge(s_st, 1)

        norm_params(nc, sh, "n0")
        with nc.Block() as block:

            @block.sync
            def _(e):
                with e.Fori(0, B) as b:
                    with e.Fori(0, PAIRS) as t:
                        i = b * PAIRS + t
                        e.wait_ge(s_pj, i * 3)
                        e.dma_start(wqk[:], w_qk[ds(t, 1)].rearrange("o (g p) s n -> p (o g) s n", p=P)).then_inc(s_wqk, 16)
                    e.wait_ge(s_fo, at(b, 6, 6))
                    e.dma_start(yv[:, ds(b, 1), :, :], xs[:, ds(b, 1), :, :]).then_inc(s_y, 16)
                e.wait_ge(s_y, 16 * B)

            @block.tensor
            def _(e):
                with e.Fori(0, B) as b:
                    with e.Fori(0, PAIRS) as t:
                        i = b * PAIRS + t
                        e.wait_ge(s_h, b + 1)
                        e.wait_ge(s_wqk, (i + 1) * 16)
                        e.wait_ge(s_e, i * NTILE)
                        for s in range(2):
                            for n in range(2):
                                for g in range(G3):
                                    last = e.matmul(p_s[s][0:TP, n, :], wqk[:, g, s, :], h[:, g, n * HALF:(n + 1) * HALF],
                                                    start=(g == 0), stop=(g == G3 - 1))
                            last.then_inc(s_pj, 1)
                        e.wait_ge(s_ta, i * NTILE)
                        e.wait_ge(s_tv, i * NTILE)
                        for c in range(NT):
                            for g in range(G3):
                                last = e.matmul(p_t[:, c, 0:2 * D], h[:, g, c * P:(c + 1) * P], wv[:, g, ds(t * (2 * D), 2 * D)],
                                                start=(g == 0), stop=(g == G3 - 1))
                        last.then_inc(s_pj, 1)
                        e.wait_ge(s_q, i + 1)
                        e.wait_ge(s_k, i + 1)

                        def scores(m):
                            e.wait_ge(s_e, at(i, NTILE, m - 1))
                            r, c = 64 * (m // NT), m % NT
                            for n in range(2):
                                last = e.matmul(p_s[m % 2][:, n, :], q[r:r + D, c * P:(c + 1) * P],
                                                k[r:r + D, n * HALF:(n + 1) * HALF], start=True, stop=True)
                            last.then_inc(s_s, 1)

                        def turn(m):
                            e.wait_ge(s_e, at(i, NTILE, m + 1))
                            if m == 0:
                                e.wait_ge(s_v, (i + 1) * 4)
                            e.wait_ge(s_ta, at(i, NTILE, m))
                            e.wait_ge(s_tv, at(i, NTILE, m))
                            for c in range(NT):
                                last = e.transpose(p_t[:, c, :], att[:, m % 2, c * P:(c + 1) * P], sh["ident"][:])
                            last.then_inc(s_t, 1)

                        def weigh(j):
                            e.wait_ge(s_ta, at(i, NTILE, 4 * j + 4))
                            e.wait_ge(s_tv, at(i, NTILE, 4 * j + 4))
                            if j == 0:
                                e.wait_ge(s_v, (i + 1) * 4)
                            e.wait_ge(s_on, at(i, 4, j))
                            for c in range(NT):
                                last = e.matmul(p_o[0:TP, :], v[:, j // 2, c, :], attT[:, j % 2, c, :],
                                                start=(c == 0), stop=(c == NT - 1))
                            last.then_inc(s_o, 1)

                        scores(0)
                        for m in range(NTILE):
                            if m + 1 < NTILE:
                                scores(m + 1)
                            turn(m)
                            if m % 4 == 0 and m:
                                weigh(m // 4 - 1)
                        weigh(3)
                    e.wait_ge(s_e, (b + 1) * (PAIRS * NTILE))
                    e.wait_ge(s_on, (b + 1) * (PAIRS * 4))
                    for m in range(2 * G3):
                        g, n = m // 2, m % 2
                        e.wait_ge(s_fo, at(b, 6, m - 3))
                        for t in range(PAIRS):
                            last = e.matmul(p_s[m // 2 % 2][:, m % 2, :], wp[:, t, g * P:(g + 1) * P],
                                            o[:, t, n * HALF:(n + 1) * HALF], start=(t == 0), stop=(t == PAIRS - 1))
                        last.then_inc(s_f, 1)

            @block.scalar
            def _(e):
                with e.Fori(0, B) as b:
                    with e.Fori(0, PAIRS) as t:
                        i = b * PAIRS + t
                        e.wait_ge(s_pj, i * 3 + 1)
                        e.activation(q[:], p_s[0][0:TP, :, :].rearrange("p a n -> p (a n)"), ACT.Copy,
                                     scale=float(D) ** -0.5).then_inc(s_q, 1)

                        def exps(m):
                            e.wait_ge(s_m, at(i, NTILE, m + 1))
                            e.wait_ge(s_t, at(i, NTILE, m - 1))
                            e.activation(att[:, m % 2, :], p_s[m % 2][:].rearrange("p a n -> p (a n)"), ACT.Exp,
                                         bias=nmax[:, m % 2:m % 2 + 1]).then_inc(s_e, 1)

                        exps(0)
                        for m in range(NTILE):
                            if m + 1 < NTILE:
                                exps(m + 1)
                            e.wait_ge(s_t, at(i, NTILE, m + 1))
                            if m % 4 == 0:
                                e.wait_ge(s_o, at(i, 4, m // 4 - 1))
                            e.copy(attT[:, m // 4 % 2, 0:4, (m % 4) * P:(m % 4 + 1) * P], p_t[:, 0:4, :]).then_inc(s_ta, 1)

            @block.vector
            def _(e):
                with e.Fori(0, B) as b:
                    e.wait_ge(s_pj, b * (3 * PAIRS))
                    for g in range(G3):
                        last = e.tensor_scalar(h[:, g, :], xs[:, ds(b, 1), g, :].rearrange("p o n -> p (o n)"),
                                               sh["gn"][:, g, ds(b, 1), 0:1].rearrange("p o s -> p (o s)"),
                                               sh["gn"][:, g, ds(b, 1), 1:2].rearrange("p o s -> p (o s)"),
                                               ALU.subtract, ALU.mult)
                    last.then_inc(s_h, 1)
                    with e.Fori(0, PAIRS) as t:
                        i = b * PAIRS + t
                        e.wait_ge(s_pj, i * 3 + 2)
                        e.tensor_copy(k[:], p_s[1][0:TP, :, :].rearrange("p a n -> p (a n)")).then_inc(s_k, 1)
                        e.wait_ge(s_pj, i * 3 + 3)
                        e.wait_ge(s_o, i * 4)
                        for s in range(2):
                            for u in range(2):
                                e.tensor_copy(v[:, s, 4 * u:4 * u + 4, 64 * s:64 * s + D],
                                              p_t[:, 4 * u:4 * u + 4, s * D:(s + 1) * D]).then_inc(s_v, 1)

                        def maxima(m):
                            e.wait_ge(s_s, at(i, NTILE, m + 1))
                            e.wait_ge(s_e, at(i, NTILE, m - 1))
                            e.tensor_reduce(nmax[:, m % 2:m % 2 + 1], p_s[m % 2][:].rearrange("p a n -> p (a n)"), AX, ALU.max,
                                            negate=True).then_inc(s_m, 1)

                        def normed(j):
                            e.wait_ge(s_o, at(i, 4, j + 1))
                            r, z = (0, 64) if j < 2 else (64, 0)
                            e.reciprocal(rden[r:r + D, :], p_o[z:z + D, :]).then_inc(s_rd, 1)
                            e.wait_ge(s_rd, at(i, 4, j + 1))
                            e.tensor_tensor(o[r:r + D, ds(t, 1), (j % 2) * HALF:(j % 2 + 1) * HALF],
                                            p_o[r:r + D, :].unsqueeze(1), rden[r:r + D, :].unsqueeze(1), ALU.mult).then_inc(s_on, 1)

                        maxima(0)
                        for m in range(NTILE):
                            if m + 1 < NTILE:
                                maxima(m + 1)
                            e.wait_ge(s_t, at(i, NTILE, m + 1))
                            if m % 4 == 0:
                                e.wait_ge(s_o, at(i, 4, m // 4 - 1))
                            e.tensor_copy(attT[:, m // 4 % 2, 4:8, (m % 4) * P:(m % 4 + 1) * P], p_t[:, 4:8, :]).then_inc(s_tv, 1)
                            if m % 4 == 1 and m > 1:
                                normed(m // 4 - 1)
                        normed(3)
                    for m in range(2 * G3):
                        g, n = m // 2, m % 2
                        e.wait_ge(s_f, at(b, 6, m + 1))
                        part = xs[:, ds(b, 1), g, n * HALF:(n + 1) * HALF].rearrange("p o n -> p (o n)")
                        e.scalar_tensor_tensor(part, p_s[m // 2 % 2][:, m % 2, :], bp[:, g:g + 1], part,
                                               ALU.add, ALU.add).then_inc(s_fo, 1)
                    e.wait_ge(s_fo, at(b, 6, 6))
                    for m in range(2 * G3):
                        g, n = m // 2, m % 2
                        last = e.bn_stats(sh["stat"][:, g, ds(b, 1), n, :].rearrange("p o s -> p (o s)"),
                                          xs[:, ds(b, 1), g, n * HALF:(n + 1) * HALF].rearrange("p o n -> p (o n)"))
                    last.then_inc(s_st, 1)
                e.wait_ge(s_st, B + 1)


def normalise(e, sh, h, xs, b):
    for g in range(G3):
        last = e.tensor_scalar(h[:, g, :], xs[:, g, :], one(sh["gn"][:, g, ds(b, 1), 0:1]), one(sh["gn"][:, g, ds(b, 1), 1:2]),
                               ALU.subtract, ALU.mult)
    return last


def one(ap):
    return ap.rearrange("p o n -> p (o n)")


def layer2(nc, sh, x, w_qk, w_vT, w_out, temp, b_out, y):
    xv = x.rearrange("b (g p) n -> p b g n", p=P)
    yv = y.rearrange("b (g p) n -> p b g n", p=P)
    norm_params(nc, sh, "n2")
    with Arena(nc, "c") as a:
        xs = a.sb("xs", [P, 2, G3, N])
        h = a.sb("h", [P, G3, N])
        w = a.sb("w", [P, G3, 2, C])
        wvT = a.sb("wvT", [TP, PAIRS, C])
        wo = a.sb("wo", [D, HEADS, C])
        tmp = a.sb("temp", [D, HEADS])
        bo = a.sb("bo", [P, G3])
        ones = a.sb("ones", [P, D])
        kq = a.sb("kq", [P, NT, HEADS, TP])
        dk = a.sb("dk", [D, HEADS, D])
        dq = a.sb("dq", [P, HEADS, D])
        rk = a.sb("rk", [D, HEADS])
        rq = a.sb("rq", [D, HEADS, D])
        at2 = a.sb("att", [D, HEADS, D])
        mx = a.sb("mx", [D, HEADS])
        attT = a.sb("attT", [D, HEADS, D])
        m = a.sb("m", [TP, PAIRS, C])
        f = a.sb("f", [P, G3, C])
        xo = a.sb("xo", [P, G3, N])
        p_a = [a.ps(f"p_a{i}", [P, 512]) for i in range(4)]
        p_g = a.ps("p_g", [P, 2, 512])
        p_m = a.ps("p_m", [P, 2, 512])
        gram = p_g[:, :, 0:4 * TP].rearrange("p u (h c) -> p u h c", h=4)
        s_w, s_x, s_y, s_z = (a.sem(n) for n in ("w", "x", "y", "z"))
        s_h, s_a, s_ae, s_g, s_dq, s_qq, s_c, s_sq, s_ex = (a.sem(n) for n in ("h", "a", "ae", "g", "dq", "qq", "c", "sq", "ex"))
        s_sub, s_an, s_tt, s_te, s_m, s_me, s_f, s_fe, s_o, s_oe, s_st = (
            a.sem(n) for n in ("sub", "an", "tt", "te", "m", "me", "f", "fe", "o", "oe", "st"))
        with nc.Block() as block:

            @block.sync
            def _(e):
                e.dma_start(w[:], w_qk.rearrange("(g p) s n -> p g s n", p=P)).then_inc(s_w, 16)
                e.dma_start(wvT[:], w_vT).then_inc(s_w, 16)
                e.dma_start(wo[:], w_out).then_inc(s_w, 16)
                e.dma_start(tmp[:], temp.partition_broadcast(D)).then_inc(s_w, 16)
                e.dma_start(bo[:], b_out.rearrange("(g p) -> p g", p=P), allow_slow_non_contiguous=True).then_inc(s_w, 16)
                e.wait_ge(s_w, 80)

            @block.gpsimd
            def _(e):
                e.memset(kq[:], 0.0).then_inc(s_z, 1)
                e.memset(ones[:], 1.0).then_inc(s_z, 1)
                e.memset(m[:], 0.0).then_inc(s_z, 1)
                e.wait_ge(s_z, 3)

        with nc.Block() as block:

            @block.sync
            def _(e):
                with e.Fori(0, B // 2) as b2:
                    for u in range(2):
                        b = b2 * 2 + u
                        e.wait_ge(s_oe, at(b2, 12, 6 * u))
                        e.dma_start(xs[:, u, :, :].unsqueeze(1), xv[:, ds(b, 1), :, :]).then_inc(s_x, 16)
                    for u in range(2):
                        b = b2 * 2 + u
                        e.wait_ge(s_oe, b * 6 + 6)
                        e.dma_start(yv[:, ds(b, 1), :, :], xo[:].unsqueeze(1)).then_inc(s_y, 16)
                e.wait_ge(s_y, 16 * B)

            @block.vector
            def _(e):
                with e.Fori(0, B // 2) as b2:
                    for u in range(2):
                        b = b2 * 2 + u
                        link = Chain(sh, e, s_c, b, 5)
                        e.wait_ge(s_x, b * 16 + 16)
                        e.wait_ge(s_o, at(b, 6, 0))
                        normalise(e, sh, h, xs[:, u, :, :], b).then_inc(s_h, 1)
                        e.wait_ge(s_g, b + 1)
                        idk = sh["ident"][0:D, 0:D].unsqueeze(1).broadcast_to([D, 4, D])
                        idq = sh["ident"][64:TP, 64:TP].unsqueeze(1).broadcast_to([D, 4, D])
                        for v in range(2):
                            e.tensor_tensor(dq[64:TP, 4 * v:4 * v + 4, :], gram[64:TP, v, :, 64:TP], idq, ALU.mult).then_inc(s_dq, 1)
                        for v in range(2):
                            last = e.tensor_tensor(dk[:, 4 * v:4 * v + 4, :], gram[0:D, v, :, 0:D], idk, ALU.mult)
                        link(last)
                        e.tensor_reduce(rk[:], dk[:], AX, ALU.add).then_inc(s_dq, 1)
                        e.wait_ge(s_sq, b * 2 + 1)
                        e.tensor_scalar(rk[:], rk[:], 1e-12, None, ALU.max)
                        e.wait_ge(s_sq, b * 2 + 2)
                        link(e.tensor_scalar(rq[:], rq[:], 1e-12, None, ALU.max))
                        e.reciprocal(rk[:], rk[:])
                        link(e.reciprocal(rq[:], rq[:]))
                        e.tensor_tensor(rk[:], rk[:], tmp[:], ALU.mult)
                        for v in range(2):
                            last = e.tensor_tensor(at2[:, 4 * v:4 * v + 4, :], gram[0:D, v, :, 64:TP], rq[:, 4 * v:4 * v + 4, :], ALU.mult)
                        link(last)
                        link(e.tensor_tensor(at2[:], at2[:], rk[:].unsqueeze(2).broadcast_to([D, HEADS, D]), ALU.mult))
                        e.tensor_reduce(mx[:], at2[:], AX, ALU.max).then_inc(s_sub, 1)
                        e.wait_ge(s_sub, b * 4 + 1)
                        e.tensor_tensor(at2[:], at2[:], mx[:].unsqueeze(2).broadcast_to([D, HEADS, D]), ALU.subtract).then_inc(s_sub, 1)
                        e.wait_ge(s_ex, b + 1)
                        e.tensor_reduce(mx[:], at2[:], AX, ALU.add).then_inc(s_sub, 1)
                        e.wait_ge(s_sub, b * 4 + 3)
                        e.reciprocal(mx[:], mx[:]).then_inc(s_sub, 1)
                        e.wait_ge(s_sub, b * 4 + 4)
                        e.tensor_tensor(at2[:], at2[:], mx[:].unsqueeze(2).broadcast_to([D, HEADS, D]), ALU.mult).then_inc(s_an, 1)
                        e.wait_ge(s_tt, b + 1)
                        e.tensor_copy(attT[:].rearrange("p h d -> p (h d)"), p_m[0:D, 0, 0:C]).then_inc(s_te, 1)
                        for v in range(PAIRS):
                            e.wait_ge(s_m, b * 4 + v + 1)
                            for r in (0, 64):
                                last = e.tensor_copy(m[r:r + D, v, :], p_m[r:r + D, v % 2, 0:C])
                            last.then_inc(s_me, 1)
                        for g in range(G3):
                            e.wait_ge(s_f, b * 3 + g + 1)
                            e.tensor_copy(f[:, g, :], p_a[g][:, 0:C]).then_inc(s_fe, 1)
                        e.wait_ge(s_y, b * 16)
                        for i in range(2 * G3):
                            g, n = i // 2, i % 2
                            e.wait_ge(s_o, b * 6 + i + 1)
                            e.scalar_tensor_tensor(xo[:, g, n * HALF:(n + 1) * HALF], p_a[i % 4][:], bo[:, g:g + 1],
                                                   xs[:, u, g, n * HALF:(n + 1) * HALF], ALU.add, ALU.add).then_inc(s_oe, 1)
                        e.wait_ge(s_oe, b * 6 + 6)
                        for i in range(2 * G3):
                            g, n = i // 2, i % 2
                            last = e.bn_stats(one(sh["stat"][:, g, ds(b, 1), n, :]), xo[:, g, n * HALF:(n + 1) * HALF])
                        last.then_inc(s_st, 1)
                        link.end()
                e.wait_ge(s_st, B)

            @block.scalar
            def _(e):
                with e.Fori(0, B) as b:
                    for i in range(2 * NT):
                        c, s = i // 2, i % 2
                        e.wait_ge(s_a, b * (2 * NT) + i + 1)
                        if i == 0:
                            e.wait_ge(s_g, b)
                        e.copy(kq[:, c, :, 64 * s:64 * s + D], p_a[i % 4][:, 0:C].rearrange("p (h d) -> p h d", h=HEADS)).then_inc(s_ae, 1)
                    e.wait_ge(s_dq, b * 3 + 3)
                    e.activation(rk[:], rk[:], ACT.Sqrt).then_inc(s_sq, 1)
                    e.wait_ge(s_qq, b + 1)
                    e.activation(rq[:].rearrange("p h d -> p (h d)"), p_m[0:D, 0, 0:C], ACT.Sqrt).then_inc(s_sq, 1)
                    e.wait_ge(s_sub, b * 4 + 2)
                    e.activation(at2[:], at2[:], ACT.Exp).then_inc(s_ex, 1)

            @block.tensor
            def _(e):
                with e.Fori(0, B) as b:
                    for i in range(2 * NT):
                        c, s = i // 2, i % 2
                        if i == 0:
                            e.wait_ge(s_h, b + 1)
                            e.wait_ge(s_oe, b * 6)
                        if i >= 4:
                            e.wait_ge(s_ae, b * (2 * NT) + i - 3)
                        for g in range(G3):
                            last = e.matmul(p_a[i % 4][:, 0:C], h[:, g, c * P:(c + 1) * P], w[:, g, s, :], start=(g == 0), stop=(g == G3 - 1))
                        last.then_inc(s_a, 1)
                    e.wait_ge(s_ae, b * (2 * NT) + 2 * NT)
                    for hd in range(HEADS):
                        for c in range(NT):
                            last = e.matmul(gram[0:TP, hd // 4, hd % 4, :], kq[:, c, hd, :], kq[:, c, hd, :], start=(c == 0), stop=(c == NT - 1))
                    last.then_inc(s_g, 1)
                    hold(sh, e, s_dq, b * 3 + 2)
                    e.matmul(p_m[0:D, 0, 0:C], ones[64:TP, :], dq[64:TP, :, :].rearrange("p h d -> p (h d)"), start=True, stop=True).then_inc(s_qq, 1)
                    hold(sh, e, s_an, b + 1)
                    for hd in range(HEADS):
                        last = e.transpose(p_m[0:D, 0, hd * D:(hd + 1) * D], at2[:, hd, :], sh["ident"][0:D, 0:D])
                    last.then_inc(s_tt, 1)
                    hold(sh, e, s_te, b + 1)
                    for v in range(PAIRS):
                        if v >= 2:
                            hold(sh, e, s_me, b * 4 + v - 1)
                        for u in range(2):
                            last = e.matmul(p_m[64 * u:64 * u + D, v % 2, 0:C], attT[:, 2 * v + u, :], wo[:, 2 * v + u, :], start=True, stop=True)
                        last.then_inc(s_m, 1)
                    e.wait_ge(s_me, b * 4 + 4)
                    for g in range(G3):
                        for v in range(PAIRS):
                            last = e.matmul(p_a[g][:, 0:C], wvT[:, v, g * P:(g + 1) * P], m[:, v, :], start=(v == 0), stop=(v == PAIRS - 1))
                        last.then_inc(s_f, 1)
                    e.wait_ge(s_fe, b * 3 + 3)
                    for i in range(2 * G3):
                        o, n = i // 2, i % 2
                        if i >= 4:
                            e.wait_ge(s_oe, b * 6 + i - 3)
                        for g in range(G3):
                            last = e.matmul(p_a[i % 4][:], f[:, g, o * P:(o + 1) * P], h[:, g, n * HALF:(n + 1) * HALF], start=(g == 0), stop=(g == G3 - 1))
                        last.then_inc(s_o, 1)


KB = 13
REACH = KB // 2
SHAPES = [(13, 1), (5, 1), (7, 1), (7, 2), (3, 3), (3, 4), (3, 5)]
CONVS = len(SHAPES)
TAPS3 = [k * k for k, _ in SHAPES]
PITCH = W + REACH
KROWS = 24
BANDS = 5
TLEN = BANDS * ROWB * PITCH
CH4 = 4


def layer3(nc, sh, x, weights, bn, y):
    xv = x.rearrange("b (g p) n -> p g b n", p=P)
    yv = y.rearrange("b (g p) n -> p g b n", p=P)
    NTAP = sum(TAPS3)
    wm_dram = nc.dram_tensor("merged_kernels", [C, KROWS * PITCH], F32).ap()
    norm_params(nc, sh, "n3")
    with Arena(nc, "d") as a:
        wr = a.sb("wr", [P, G3, NTAP])
        bnp = a.sb("bnp", [P, G3, CONVS, 4])
        dev = a.sb("dev", [P, G3, CONVS])
        scale = a.sb("scale", [P, G3, CONVS])
        shift = a.sb("shift", [P, G3, CONVS])
        sft = a.sb("sft", [P, G3])
        wm = a.sb("wm", [P, G3, KROWS, PITCH])
        xs = a.sb("xs", [P, B, N])
        h = a.sb("h", [P, 2, N])
        xT = a.sb("xT", [P, P, B * NT])
        yT = a.sb("yT", [P, B * NT, P])
        win = a.sb("win", [P, 2, CH4, TLEN])
        toe = a.sb("toe", [P, 4, CH4, BANDS * ROWB, W])
        xo = a.sb("xo", [P, 2, N])
        p_t = [a.ps(f"p_t{i}", [P, NT, P]) for i in range(2)]
        p_c = [a.ps(f"p_c{i}", [P, 8, B * NT]) for i in range(2)]
        s_w, s_wm, s_c, s_v = (a.sem(n) for n in ("w", "wm", "c", "v"))
        with nc.Block() as block:

            @block.sync
            def _(e):
                off = 0
                for i, wi in enumerate(weights):
                    e.dma_start(wr[:, :, off:off + TAPS3[i]], wi.rearrange("(g p) t -> p g t", p=P)).then_inc(s_w, 16)
                    off += TAPS3[i]
                e.dma_start(bnp[:], bn.rearrange("(g p) i f -> p g i f", p=P)).then_inc(s_w, 16)
                e.wait_ge(s_wm, 1)
                e.dma_start(wm_dram.rearrange("(g p) n -> p g n", p=P), wm[:].rearrange("p g r c -> p g (r c)")).then_inc(s_w, 16)
                e.wait_ge(s_w, 16 * (CONVS + 2))

            @block.scalar
            def _(e):
                e.wait_ge(s_v, 1)
                e.activation(dev[:], dev[:], ACT.Sqrt).then_inc(s_v, 1)

            @block.vector
            def _(e):
                link = Chain(sh, e, s_c)
                link(e.memset(wm[:], 0.0))
                e.wait_ge(s_w, 16 * (CONVS + 1))
                e.tensor_scalar(dev[:], bnp[:, :, :, 3], 1e-5, None, ALU.add).then_inc(s_v, 1)
                e.wait_ge(s_v, 2)
                link(e.reciprocal(dev[:], dev[:]))
                link(e.tensor_tensor(scale[:], bnp[:, :, :, 0], dev[:], ALU.mult))
                link(e.tensor_tensor(shift[:], bnp[:, :, :, 2], scale[:], ALU.mult))
                link(e.tensor_tensor(shift[:], bnp[:, :, :, 1], shift[:], ALU.subtract))
                link(e.tensor_reduce(sft[:], shift[:], AX, ALU.add))
                off = 0
                for i, (k, d) in enumerate(SHAPES):
                    first = REACH - d * (k - 1) // 2
                    span = d * (k - 1) + 1
                    for g in range(G3):
                        into = wm[:, g, REACH + first:REACH + first + span:d, first:first + span:d]
                        last = e.scalar_tensor_tensor(into, wr[:, g, off:off + k * k].rearrange("p (a b) -> p a b", a=k),
                                                      scale[:, g, i:i + 1], into, ALU.mult, ALU.add)
                    if i + 1 < CONVS:
                        link(last)
                    off += k * k
                last.then_inc(s_wm, 1)
                e.wait_ge(s_wm, 1)

        s_x, s_h, s_t, s_te, s_p, s_pe, s_b, s_o = (a.sem(n) for n in ("x", "h", "t", "te", "p", "pe", "b", "o"))
        s_y = [a.sem(f"y{u}") for u in range(2)]
        s_win = [a.sem(f"win{q}") for q in range(2)]
        s_toe = [a.sem(f"toe{q}") for q in range(4)]
        CB = P // (4 * CH4)
        win_m = win[:].rearrange("p q c (r w) -> p q c r w", w=PITCH)
        xT_m = xT[:].rearrange("p c (b i) -> p c b i", b=B)
        with nc.Block() as block:

            @block.sync
            def _(e):
                with e.Fori(0, G3 * CB) as i:
                    for q in range(4):
                        e.wait_ge(s_toe[(q - 2) % 4], i + 1)
                        for r in range(ROWB):
                            src = bass.AP(wm_dram.tensor, REACH * 2 + 1 + r * PITCH, [[KROWS * PITCH, C], [1, W], [1, TLEN - PITCH + W]])
                            e.dma_start(win[r * W:(r + 1) * W, q % 2, :, 0:TLEN - PITCH + W],
                                        src[ds(i * (4 * CH4) + q * CH4, CH4)].rearrange("c w n -> w c n")).then_inc(s_win[q % 2], 16)

            def pack(e, copy, i, q):
                e.wait_ge(s_win[q % 2], (i * 2 + q // 2 + 1) * (16 * ROWB))
                hold(sh, e, s_p, i * 4 + q + 1)
                copy(toe[:, q, :, :, :], win_m[:, q % 2, :, :, 0:W]).then_inc(s_toe[q], 1)

            @block.gpsimd
            def _(e):
                with e.Fori(0, G3 * CB) as i:
                    pack(e, e.tensor_copy, i, 1)

            @block.scalar
            def _(e):
                with e.Fori(0, G3) as g:
                    e.wait_ge(s_o, g * B)
                    e.dma_start(xs[:].unsqueeze(1), xv[:, ds(g, 1), :, :]).then_inc(s_x, 16)
                    with e.Fori(0, B // 2) as b2:
                        for u in range(2):
                            n = g * B + b2 * 2 + u
                            e.wait_ge(s_t, n + 1)
                            if u == 0:
                                e.copy(xT_m[:, :, ds(b2 * 2, 1), :].rearrange("p c o i -> p c (o i)"), p_t[0][:].rearrange("p i c -> p c i")).then_inc(s_te, 1)
                    with e.Fori(0, CB) as j:
                        i = g * CB + j
                        pack(e, e.copy, i, 2)
                        e.wait_ge(s_p, i * 4 + 2 + 4)
                        e.copy(yT[:, :, ds(j * 16, 8)], p_c[0][:].rearrange("p c n -> p n c")).then_inc(s_pe, 1)
                    with e.Fori(0, B // 2) as b2:
                        for u in range(2):
                            n = g * B + b2 * 2 + u
                            e.wait_ge(s_o, n + 1)
                            e.dma_start(yv[:, ds(g, 1), ds(b2 * 2 + u, 1), :], xo[:, u:u + 1, :].unsqueeze(1)).then_inc(s_y[u], 16)
                for u in range(2):
                    e.wait_ge(s_y[u], 16 * (B // 2) * G3)

            @block.vector
            def _(e):
                with e.Fori(0, G3) as g:
                    with e.Fori(0, B // 2) as b2:
                        for u in range(2):
                            n = g * B + b2 * 2 + u
                            b = b2 * 2 + u
                            e.wait_ge(s_x, g * 16 + 16)
                            gn = sh["gn"][:, ds(g, 1), ds(b, 1), :].rearrange("p g b s -> p (g b s)")
                            e.tensor_scalar(h[:, u, :], one(xs[:, ds(b, 1), :]), gn[:, 0:1], gn[:, 1:2], ALU.subtract, ALU.mult).then_inc(s_h, 1)
                            e.wait_ge(s_t, n + 1)
                            if u == 1:
                                e.tensor_copy(xT_m[:, :, ds(b, 1), :].rearrange("p c o i -> p c (o i)"), p_t[1][:].rearrange("p i c -> p c i")).then_inc(s_te, 1)
                    with e.Fori(0, CB) as j:
                        i = g * CB + j
                        pack(e, e.tensor_copy, i, 0)
                        pack(e, e.tensor_copy, i, 3)
                        e.wait_ge(s_p, i * 4 + 4 + 4)
                        e.tensor_copy(yT[:, :, ds(j * 16 + 8, 8)], p_c[1][:].rearrange("p c n -> p n c")).then_inc(s_pe, 1)
                    for b in range(B):
                        e.wait_ge(s_b, g * B + b + 1)
                        e.wait_ge(s_y[b % 2], (g * (B // 2) + b // 2) * 16)
                        e.scalar_tensor_tensor(xo[:, b % 2, :], p_t[b % 2][:].rearrange("p i w -> p (i w)").rearrange("p (i w) -> p i w", i=NT)[:, :, ::-1],
                                               sft[:, ds(g, 1)], xs[:, b, :].rearrange("p (i w) -> p i w", i=NT), ALU.add, ALU.add).then_inc(s_o, 1)

            @block.tensor
            def _(e):
                e.sem_inc(s_p, 4)
                for q in (2, 3):
                    e.sem_inc(s_toe[q], 1)
                with e.Fori(0, G3) as g:
                    with e.Fori(0, B // 2) as b2:
                        for u in range(2):
                            n = g * B + b2 * 2 + u
                            e.wait_ge(s_h, n + 1)
                            e.wait_ge(s_te, g * B + b2 * 2)
                            for i in range(NT):
                                last = e.transpose(p_t[u][:, i, :], h[:, u, i * P:(i + 1) * P], sh["ident"][:])
                            last.then_inc(s_t, 1)
                    with e.Fori(0, CB) as j:
                        i = g * CB + j
                        for q in range(4):
                            e.wait_ge(s_toe[q], i + 1 + (q == 2 or q == 3))
                            if q == 0:
                                e.wait_ge(s_te, g * B + B)
                            if q % 2 == 0:
                                e.wait_ge(s_pe, i * 2)
                            for c in range(CH4):
                                ch = j * 16 + (q * CH4 + c)
                                for d in (0, -1, 1, -2, 2):
                                    lo, hi = max(0, -d), min(NT, NT - d)
                                    rows = ROWB * (d + 2)
                                    last = e.matmul(p_c[q // 2][:, (q % 2) * CH4 + c, :].rearrange("p (b i) -> p b i", b=B)[:, :, lo:hi],
                                                    toe[:, q, c, rows:rows + ROWB, :].rearrange("p r w -> p (r w)"),
                                                    xT_m[:, ds(ch, 1), :, lo + d:hi + d].rearrange("p o b i -> p (o b) i"),
                                                    start=(d == 0), stop=(d == 2), skip_group_check=True)
                            last.then_inc(s_p, 1)
                    for b in range(B):
                        if b == 0:
                            e.wait_ge(s_pe, (g + 1) * (2 * CB))
                        if b >= 2:
                            e.wait_ge(s_o, g * B + b - 1)
                        for i in range(NT):
                            last = e.transpose(p_t[b % 2][:, i, :], yT[:, b * NT + i, :], sh["ident"][:])
                        last.then_inc(s_b, 1)


KS = (3, 5, 7)
NEAR = ROWB
CHUNKS = NT + 2
FAR_STEP = 3 * ROWB
FAR = 3
TOP = FAR * FAR_STEP + 2 * ROWB
ROWS = 2 * TOP + H
PARTS = 2
SLOTS = {3: (0, 1, 2), 5: (0, 1, 2, 0, 1), 7: (0, 1, 2, 0, 1, 2, 1)}
NB = 3
BACK = 4
HID = C // 16


def last_use(K, kx):
    seq = SLOTS[K]
    return next(n for n in range(1, 2 * K) if seq[(kx - n) % K] == seq[kx])


def nth_use(K, kx):
    seq = SLOTS[K]
    return seq.count(seq[kx]), seq[:kx + 1].count(seq[kx])


def tiles_of(j):
    return max(0, j - 2), min(NT - 1, j) + 1


class Taps:

    def __init__(self, a, tag):
        self.s_stack, self.s_y = (a.sem(f"{tag}_{n}") for n in ("stack", "y"))
        self.s_hk, self.s_row, self.s_col, self.s_acc = (a.sem(f"{tag}_{n}") for n in ("hk", "row", "col", "act"))
        self.s_py = [a.sem(f"{tag}_py{i}") for i in range(NB)]
        self.s_px = [a.sem(f"{tag}_px{i}") for i in range(NB)]
        self.s_hi, self.s_rep, self.s_s, self.s_m = (a.sem(f"{tag}_{n}") for n in ("hi", "rep", "s", "m"))
        self.all = [self.s_stack, self.s_y, self.s_hk, self.s_row, self.s_col, self.s_acc, self.s_hi, self.s_rep, self.s_s, self.s_m, *self.s_py, *self.s_px]


ITEMS = 2 * CHUNKS


def credit(sh, block, tp):
    for engine in (block.sync, block.scalar, block.gpsimd):

        @engine
        def _(e):
            e.sem_inc(sh["tick"], 1)

    @block.vector
    def _(e):
        e.sem_inc(tp.s_stack, BACK)
        e.sem_inc(tp.s_s, BACK * ITEMS)

    @block.tensor
    def _(e):
        e.sem_inc(tp.s_rep, BACK * ITEMS)
        e.sem_inc(tp.s_m, BACK * ITEMS)


def deform(nc, sh, block, K, tp, bf, loop, zero_first):
    def near(T, n, per):
        return (T - n + 1 + BACK) * per

    @block.sync
    def _(e):
        for it, ky, row in loop(e):
            e.wait_ge(tp.s_y, it * K)
            for s in range(2):
                e.dma_start(bf["hk"][:, s, :, :], bf["hTd"][s, ds((row + ky) * W, CHUNKS * P), :].rearrange("(j p) c -> p j c", p=P)).then_inc(tp.s_hk, 16)
            e.dma_start(bf["wk"][:, 0:K, :], bf["dw"][ds(ky * K, K), :].partition_broadcast(P)).then_inc(tp.s_hk, 16)
            for kx in range(K):
                T, b, back = it * K + kx, SLOTS[K][kx], last_use(K, kx)
                m = (ky * K + kx) * 2
                e.wait_ge(tp.s_stack, near(T, back, 1))
                for s in range(2):
                    e.dma_start(bf["py"][64 * s:64 * s + 64, b, :], bf["posd"][s, ds(m, 1), :].partition_broadcast(64).rearrange("p o n -> p (o n)")).then_inc(tp.s_py[b], 16)
                e.wait_ge(tp.s_s, near(T, back, ITEMS))
                e.dma_start(bf["px"][:, b, :, :], bf["posd"][:, ds(m + 1, 1), :].rearrange("s o n -> (s o) n").partition_broadcast(P)).then_inc(tp.s_px[b], 16)

    @block.scalar
    def _(e):
        for it, ky, row in loop(e):
            for kx in range(K):
                b = SLOTS[K][kx]
                uses, nth = nth_use(K, kx)
                T = it * K + kx
                for buf, sem, by, done in ((bf["py"][:, b, :], tp.s_py[b], 32, tp.s_row),
                                           (bf["px"][:, b, :, :].rearrange("p s n -> p (s n)"), tp.s_px[b], 16, tp.s_col)):
                    e.wait_ge(sem, (it * uses + nth) * by)
                    e.activation(buf, buf, ACT.Abs, bias=bf["minus"][:]).then_inc(tp.s_acc, 1)
                    e.wait_ge(tp.s_acc, T * 2 + (1 if done is tp.s_row else 2))
                    e.activation(buf, buf, ACT.Relu, bias=1.0, scale=-1.0).then_inc(done, 1)

    @block.gpsimd
    def _(e):
        for it, ky, row in loop(e):
            for kx in range(K):
                b = SLOTS[K][kx]
                T = it * K + kx
                if kx == 0:
                    e.wait_ge(tp.s_hk, (it + 1) * 48)
                hold(sh, e, tp.s_m, near(T, last_use(K, kx), ITEMS))
                e.tensor_tensor(bf["y"][:, b, :, :], bf["hk"][:].rearrange("p s j c -> p (s j) c"),
                                bf["wk"][:, kx, :].unsqueeze(1).broadcast_to([P, ITEMS, P]), ALU.mult).then_inc(tp.s_y, 1)

    @block.vector
    def _(e):
        for it, ky, row in loop(e):
            def split(kx):
                T, b = it * K + kx, SLOTS[K][kx]
                e.wait_ge(tp.s_row, T + 1)
                e.tensor_copy(bf["hi"][:], bf["py"][:, b, :]).then_inc(tp.s_hi, 1)
                e.wait_ge(tp.s_hi, T + 1)
                e.wait_ge(tp.s_rep, near(T, last_use(K, kx), ITEMS))
                e.scalar_tensor_tensor(bf["stack"][:, b, :], bf["hi"][:], bf["low"][:], bf["py"][:, b, :], ALU.mult, ALU.subtract).then_inc(tp.s_stack, 1)

            split(0)
            for kx in range(K):
                T, b = it * K + kx, SLOTS[K][kx]
                for i in range(ITEMS):
                    s, j = divmod(i, CHUNKS)
                    lo, hi = tiles_of(j)
                    n = (hi - lo) * P
                    if i == 0:
                        e.wait_ge(tp.s_col, T + 1)
                    if i == CHUNKS and kx + 1 < K:
                        split(kx + 1)
                    e.wait_ge(tp.s_rep, (T + BACK) * ITEMS + i + 1)
                    e.wait_ge(tp.s_m, (T + BACK) * ITEMS + i + 1 - bf["NS"])
                    e.tensor_tensor(bf["S"][:, i % bf["NS"], 0:n], bf["p_r"][i % 4][:, 0:n],
                                    bf["px"][:, b, s, lo * P:hi * P], ALU.mult).then_inc(tp.s_s, 1)

    @block.tensor
    def _(e):
        if zero_first:
            for s in range(2):
                for n in range(2):
                    e.matmul(bf["acc"][s][:, n, :], bf["zero"][:, 0:P], bf["zero"][:], start=True, stop=False, skip_group_check=True)
        for it, ky, row in loop(e):
            def spread(k):
                kx, i = divmod(k, ITEMS)
                s, j = divmod(i, CHUNKS)
                T, b = it * K + kx, SLOTS[K][kx]
                lo, hi = tiles_of(j)
                if i == 0:
                    e.wait_ge(tp.s_stack, T + 1 + BACK)
                e.wait_ge(tp.s_s, (T + BACK) * ITEMS + i + 1 - 4)
                e.matmul(bf["p_r"][i % 4][:, 0:(hi - lo) * P], bf["E"][:, s, ds((row + ky + j * ROWB) * W, P)],
                         bf["stack"][:, b, lo * P:hi * P], start=True, stop=True).then_inc(tp.s_rep, 1)

            def product(k):
                kx, i = divmod(k, ITEMS)
                s, j = divmod(i, CHUNKS)
                T, b = it * K + kx, SLOTS[K][kx]
                lo, hi = tiles_of(j)
                if i == 0:
                    e.wait_ge(tp.s_y, T + 1)
                e.wait_ge(tp.s_s, (T + BACK) * ITEMS + i + 1)
                for n in range(2):
                    a, z = max(lo, n * NT // 2), min(hi, (n + 1) * NT // 2)
                    if a < z:
                        last = e.matmul(bf["acc"][s][:, n, (a - n * NT // 2) * P:(z - n * NT // 2) * P], bf["y"][:, b, i, :],
                                        bf["S"][:, i % bf["NS"], (a - lo) * P:(z - lo) * P], start=False, stop=False, skip_group_check=True)
                last.then_inc(tp.s_m, 1)

            AHEAD = 3
            for k in range(AHEAD):
                spread(k)
            for k in range(K * ITEMS):
                if k + AHEAD < K * ITEMS:
                    spread(k + AHEAD)
                product(k)


def layer1(nc, sh, x, t, y):
    xv = x.rearrange("b (g p) n -> p b g n", p=P)
    yv = y.rearrange("b (g p) n -> p b g n", p=P)
    M7 = 2 * KS[-1] ** 2
    posd = nc.dram_tensor("sampling_positions", [2, M7, N], F32).ap()
    hTd = nc.dram_tensor("turned_image", [2, ROWS * W, P], F32).ap()
    PADT = TOP * W // P
    norm_params(nc, sh, "n1")
    with Arena(nc, "b") as a:
        E = a.sb("E", [P, 2, ROWS * W], F16)
        zero = a.sb("zero", [P, HALF], F16)
        minus = a.sb("minus", [P, 1])
        low = a.sb("low", [P, 1])
        ymask = a.sb("ymask", [M7, 1])
        pw = a.sb("pw", [P, G3, P])
        pb = a.sb("pb", [P, G3])
        ob = a.sb("ob", [M7, G3])
        f1 = a.sb("f1", [P, G3, HID])
        f2 = a.sb("f2", [HID, G3, P])
        dcv = a.sb("dcv", [P, G3, 2, N])
        far = a.sb("far", [1, 1 + 2 * FAR * KS[-1]], I32)
        ps = [a.ps(f"p{i}", [P, 2, HALF]) for i in range(4)]
        acc = ps[0:2]
        p_r = [ps[2 + i // 2][:, i % 2, :] for i in range(4)]
        taps = [Taps(a, f"t{g}") for g in range(G3)]
        tfar = Taps(a, "far")
        s_i, s_iv, s_hv, s_iz = (a.sem(n) for n in ("i", "iv", "hv", "iz"))
        with Arena(nc, "bi") as ai, nc.Block() as block:
            ef = ai.sb("ef", [P, 2, H * W])
            zt = ai.sb("zt", [P, PADT, P])

            @block.sync
            def _(e):
                e.dma_start(ef[:], t["b_E"].rearrange("s p n -> p s n")).then_inc(s_i, 16)
                for dst, src in ((minus[:], t["b_minus"]), (low[:], t["b_low"]), (ymask[:], t["b_ymask"]),
                                 (pw[:], t["b_pw"].rearrange("g c o -> c g o")), (f1[:], t["b_f1"].rearrange("g c o -> c g o")), (f2[:], t["b_f2"]),
                                 (pb[:], t["b_pb"]), (ob[:], t["b_ob"])):
                    e.dma_start(dst, src, allow_slow_non_contiguous=True).then_inc(s_i, 16)
                e.wait_ge(s_iv, 2)
                for s in range(2):
                    for r0 in (0, (TOP + H) * W):
                        e.dma_start(hTd[s, r0:r0 + TOP * W, :].rearrange("(j p) c -> p j c", p=P), zt[:]).then_inc(s_iz, 16)
                e.wait_ge(s_iz, 16 * 4)
                e.wait_ge(s_i, 16 * 9)

            @block.gpsimd
            def _(e):
                e.memset(zt[:], 0.0).then_inc(s_iv, 1)
                e.memset(zero[:], 0.0).then_inc(s_iv, 1)

            @block.vector
            def _(e):
                e.memset(E[:], 0.0).then_inc(s_hv, 1)
                e.wait_ge(s_hv, 1)
                e.wait_ge(s_i, 16 * 9)
                e.tensor_copy(E[:, :, TOP * W:(TOP + H) * W], ef[:]).then_inc(s_hv, 1)
                e.wait_ge(s_hv, 2)

        for tp in taps:
            with nc.Block() as block:
                credit(sh, block, tp)

        SA = {n: [a.sem(f"{n}{g}") for g in range(G3)] for n in ("x", "w", "g", "h", "hp", "tr", "cv", "po", "tt", "fl", "st", "ev", "pw", "dc")}
        SC = {n: a.sem(f"c{n}") for n in ("x", "r", "v", "p", "a", "o", "y")}
        with nc.Fori(0, B // 2) as pr:
            for g, K in enumerate(KS):
                M, R = 2 * K * K, K // 2
                with Arena(nc, f"o{g}") as ao, nc.Block() as block:
                    PW = W + 2 * R
                    ow = ao.sb("ow", [P, K * K, M])
                    grid = ao.sb("grid", [M, N])
                    xs = ao.sb("xs", [P, 2, N])
                    h = ao.sb("h", [P, 2, N])
                    hp = ao.sb("hp", [P, 2, PW, PW])
                    hT = ao.sb("hT", [P, 2, NT, P])
                    pos = ao.sb("pos", [M, 2, N])
                    off = ao.sb("off", [M, 2, N])
                    mx = ao.sb("mx", [M, 2, 2])
                    mxm = ao.sb("mxm", [M, 2])
                    fm = ao.sb("fm", [1, 2, K])
                    S = {n: v[g] for n, v in SA.items()}

                    @block.sync
                    def _(e):
                        e.dma_start(xs[:], xv[:, ds(pr * 2, 2), g, :]).then_inc(S["x"], 16)
                        e.dma_start(ow[:], t[f"b_ow{g}"]).then_inc(S["w"], 16)
                        e.dma_start(grid[:], t[f"b_grid{g}"]).then_inc(S["g"], 16)
                        e.wait_ge(S["tr"], pr * 3 + 3)
                        for s in range(2):
                            e.dma_start(hTd[s, TOP * W:(TOP + H) * W, :].rearrange("(j p) c -> p j c", p=P), hT[:, s, :, :]).then_inc(S["st"], 16)
                        e.wait_ge(S["po"], pr * 8 + 8)
                        e.dma_start(posd[:, 0:M, :].rearrange("s m n -> m s n"), pos[:]).then_inc(S["st"], 16)
                        hold(sh, e, S["st"], (pr + 1) * 48)

                    @block.gpsimd
                    def _(e):
                        e.memset(hp[:], 0.0).then_inc(S["hp"], 1)

                    @block.scalar
                    def _(e):
                        e.wait_ge(S["hp"], pr * 2 + 1)
                        e.wait_ge(S["h"], pr * 2 + 2)
                        for s in range(2):
                            last = e.copy(hp[:, s, R:R + H, R:R + W], h[:, s, :].rearrange("p (a b) -> p a b", a=H))
                        last.then_inc(S["hp"], 1)
                        e.wait_ge(S["tr"], pr * 3 + 1)
                        for s in range(2):
                            e.copy(hT[:, s, :, :], ps[2 + s][:].rearrange("p a (b c) -> p (a b) c", c=P)).then_inc(S["tr"], 1)

                    @block.vector
                    def _(e):
                        e.wait_ge(S["x"], (pr + 1) * 16)
                        for s in range(2):
                            gn = sh["gn"][:, g, ds(pr * 2 + s, 1), :].rearrange("p b s -> p (b s)")
                            e.tensor_scalar(h[:, s, :], xs[:, s, :], gn[:, 0:1], gn[:, 1:2], ALU.subtract, ALU.mult).then_inc(S["h"], 1)
                        e.wait_ge(S["g"], (pr + 1) * 16)
                        for s in range(2):
                            for n in range(2):
                                e.wait_ge(S["cv"], pr * 4 + s * 2 + n + 1)
                                part = slice(n * HALF, (n + 1) * HALF)
                                e.tensor_scalar(off[:, s, part], acc[s][0:M, n, :], ob[0:M, g:g + 1], None, ALU.add).then_inc(S["po"], 1)
                        e.wait_ge(S["po"], pr * 8 + 4)
                        e.tensor_reduce(mx[:, 0, :], off[:], AX, ALU.min, negate=True).then_inc(S["po"], 1)
                        e.tensor_reduce(mx[:, 1, :], off[:], AX, ALU.max).then_inc(S["po"], 1)
                        for s in range(2):
                            e.tensor_tensor(pos[:, s, :], off[:, s, :], grid[:], ALU.add).then_inc(S["po"], 1)
                        e.wait_ge(S["po"], pr * 8 + 8)
                        link = Chain(sh, e, S["fl"], pr, 5)
                        link(e.tensor_reduce(mxm[:], mx[:], AX, ALU.max))
                        link(e.tensor_scalar(mxm[:], mxm[:], ymask[0:M, :], None, ALU.mult))
                        e.wait_ge(S["tt"], pr + 1)
                        for way in range(2):
                            last = e.tensor_reduce(fm[:, way, :], ps[2][0:1, way, 0:M].rearrange("p (ky m) -> p ky m", ky=K), AX, ALU.max)
                        link(last)
                        for f in range(2 * FAR):
                            steps = FAR - 1 - f if f < FAR else f - FAR
                            last = e.tensor_scalar(far[:, 1 + f * KS[-1]:1 + f * KS[-1] + K], fm[:, int(f >= FAR), :],
                                                   float(NEAR + steps * FAR_STEP), None, ALU.is_gt)
                        link(last)
                        n = 1 + (FAR - 1) * KS[-1]
                        link(e.tensor_reduce(far[:, 0:1], far[:, n:n + 2 * KS[-1]].rearrange("p (f k) -> p f k", f=2)[:, :, 0:K],
                                             mybir.AxisListType.XY, ALU.max))
                        link.end()

                    @block.tensor
                    def _(e):
                        e.wait_ge(S["h"], pr * 2 + 2)
                        for s in range(2):
                            for i in range(NT):
                                last = e.transpose(ps[2 + s][:, i // 4, i % 4 * P:(i % 4 + 1) * P], h[:, s, i * P:(i + 1) * P], sh["ident"][:])
                        last.then_inc(S["tr"], 1)
                        e.wait_ge(S["w"], (pr + 1) * 16)
                        e.wait_ge(S["hp"], pr * 2 + 2)
                        for s in range(2):
                            for n in range(2):
                                for k in range(K * K):
                                    dy, dx = divmod(k, K)
                                    last = e.matmul(acc[s][0:M, n, :].rearrange("p (a b) -> p a b", b=W), ow[:, k, :],
                                                    hp[:, s, n * 16 + dy:n * 16 + dy + 16, dx:dx + W], start=(k == 0), stop=(k == K * K - 1))
                                last.then_inc(S["cv"], 1)
                        e.wait_ge(S["tr"], pr * 3 + 3)
                        hold(sh, e, S["fl"], pr * 5 + 2)
                        for way in range(2):
                            last = e.matmul(ps[2][0:1, way, 0:M], mxm[:, way:way + 1], sh["ident"][0:M, 0:M], start=True, stop=True)
                        last.then_inc(S["tt"], 1)

                with Arena(nc, f"m{g}") as am:
                    bf = {"hk": am.sb("hk", [P, 2, CHUNKS, P]), "wk": am.sb("wk", [P, K, P]), "py": am.sb("py", [P, NB, N]),
                          "px": am.sb("px", [P, NB, 2, N]), "hi": am.sb("hi", [P, N], F16), "stack": am.sb("stack", [P, NB, N], F16),
                          "y": am.sb("y", [P, NB, ITEMS, P]), "NS": 5, "S": am.sb("S", [P, 5, 3 * P]),
                          "hTd": hTd, "posd": posd, "dw": t[f"b_dw{g}"], "minus": minus, "low": low, "zero": zero, "E": E,
                          "acc": acc, "p_r": p_r}
                    smp = am.sb("smp", [P, 2, N])
                    first = TOP - ROWB - R

                    def near_loop(e):
                        with e.Fori(0, K) as ky:
                            yield pr * K + ky, ky, first

                    with nc.Block() as block:
                        deform(nc, sh, block, K, taps[g], bf, near_loop, True)
                    with nc.If(nc.values_load(far[0:1, 0:1], min_val=0, max_val=1) > 0):
                        with nc.Fori(0, 2 * FAR) as f, nc.Fori(0, K) as ky:
                            which = nc.values_load(far[0:1, ds(1 + f * KS[-1] + ky, 1)], min_val=0, max_val=1)
                            row = first + f * FAR_STEP + f // FAR * FAR_STEP - FAR * FAR_STEP
                            with nc.If(which > 0):
                                with nc.Block() as block:
                                    credit(sh, block, tfar)
                                with nc.Block() as block:
                                    deform(nc, sh, block, K, tfar, bf, lambda e: [(0, ky, row)], False)
                                clear(nc, tfar.all)
                    with nc.Block() as block:
                        S = {n: v[g] for n, v in SA.items()}

                        @block.scalar
                        def _(e):
                            for s in range(2):
                                e.copy(smp[:, s, :], acc[s][:].rearrange("p a n -> p (a n)")).then_inc(S["ev"], 1)
                            for s in range(2):
                                e.wait_ge(S["pw"], pr * 2 + s + 1)
                                e.activation(dcv[:, g, s, :], ps[2 + s][:].rearrange("p a n -> p (a n)"), ACT.Identity, bias=pb[:, g:g + 1]).then_inc(S["dc"], 1)

                        @block.tensor
                        def _(e):
                            for s in range(2):
                                e.wait_ge(S["ev"], pr * 2 + s + 1)
                                for n in range(2):
                                    last = e.matmul(ps[2 + s][:, n, :], pw[:, g, :], smp[:, s, n * HALF:(n + 1) * HALF], start=True, stop=True)
                                last.then_inc(S["pw"], 1)

            with Arena(nc, "se") as ae, nc.Block() as block:
                xs = ae.sb("xs", [P, 2, G3, N])
                pool = ae.sb("pool", [P, G3, 2, 2])
                hid = ae.sb("hid", [HID, 4])
                z = ae.sb("z", [P, G3, 2])
                zz = ae.sb("zz", [P, G3, 4])

                @block.sync
                def _(e):
                    e.dma_start(xs[:], xv[:, ds(pr * 2, 2), :, :]).then_inc(SC["x"], 16)
                    e.wait_ge(SC["o"], pr * 7 + 6)
                    e.dma_start(yv[:, ds(pr * 2, 2), :, :], xs[:]).then_inc(SC["y"], 16)
                    hold(sh, e, SC["y"], (pr + 1) * 16)

                @block.vector
                def _(e):
                    link = Chain(sh, e, SC["r"], pr, 7)
                    for g in range(G3):
                        e.tensor_reduce(pool[:, g, 0, :], dcv[:, g, :, :], AX, ALU.add)
                        last = e.tensor_reduce(pool[:, g, 1, :], dcv[:, g, :, :], AX, ALU.max)
                    link(last)
                    link(e.tensor_scalar(pool[:, :, 0, :], pool[:, :, 0, :], 1.0 / N, None, ALU.mult))
                    e.wait_ge(SC["p"], pr * 2 + 1)
                    link(e.tensor_scalar(hid[:], ps[2][0:HID, 0, 0:4], 0.0, None, ALU.max))
                    e.wait_ge(SC["p"], pr * 2 + 2)
                    link(e.tensor_copy(zz[:], ps[3][:, 0, 0:4 * G3].rearrange("p (g f) -> p g f", f=4)))
                    link(e.tensor_tensor(z[:], zz[:, :, 0:2], zz[:, :, 2:4], ALU.add))
                    e.wait_ge(SC["a"], pr + 1)
                    link(e.tensor_scalar(z[:], z[:], 1.0, None, ALU.add))
                    link(e.reciprocal(z[:], z[:]))
                    e.wait_ge(SC["x"], (pr + 1) * 16)
                    for g in range(G3):
                        for s in range(2):
                            e.scalar_tensor_tensor(xs[:, s, g, :], dcv[:, g, s, :], z[:, g, s:s + 1], xs[:, s, g, :], ALU.mult, ALU.add).then_inc(SC["o"], 1)
                    e.wait_ge(SC["o"], pr * 7 + 6)
                    for g in range(G3):
                        for s in range(2):
                            for n in range(2):
                                last = e.bn_stats(sh["stat"][:, g, ds(pr * 2 + s, 1), n, :].rearrange("p o s -> p (o s)"), xs[:, s, g, n * HALF:(n + 1) * HALF])
                    last.then_inc(SC["o"], 1)
                    hold(sh, e, SC["o"], pr * 7 + 7)
                    link.end()

                @block.scalar
                def _(e):
                    e.wait_ge(SC["r"], pr * 7 + 5)
                    e.activation(z[:], z[:], ACT.Exp, scale=-1.0).then_inc(SC["a"], 1)

                @block.tensor
                def _(e):
                    hold(sh, e, SC["r"], pr * 7 + 2)
                    for g in range(G3):
                        last = e.matmul(ps[2][0:HID, 0, 0:4], f1[:, g, :], pool[:, g, :, :].rearrange("p a s -> p (a s)"), start=(g == 0), stop=(g == G3 - 1))
                    last.then_inc(SC["p"], 1)
                    hold(sh, e, SC["r"], pr * 7 + 3)
                    for g in range(G3):
                        last = e.matmul(ps[3][:, 0, 4 * g:4 * g + 4], f2[:, g, :], hid[:], start=True, stop=True)
                    last.then_inc(SC["p"], 1)


def program(nc, t):
    with ExitStack() as ctx:
        def shared(name, shape, dt=F32):
            return ctx.enter_context(nc.sbuf_tensor(name, shape, dt))

        sh = {
            "tick": ctx.enter_context(nc.semaphore("tick")),
            "ident": shared("ident", [P, P]),
            "gmat": shared("gmat", [P, G3, GROUPS]),
            "gmatT": shared("gmatT", [GROUPS, G3, P]),
            "stat": shared("stat", [P, G3, B, 2, 6]),
            "gn": shared("gn", [P, G3, B, 2]),
        }
        load_shared(nc, sh, t)
        x1, x2, x3 = (nc.dram_tensor(f"x{i}", [B, C, N], F32).ap() for i in (1, 2, 3))
        layer0(nc, sh, t["x"], t["a_wqk"], t["a_wv"], t["a_wp"], t["a_bp"], x1)
        layer1(nc, sh, x1, t, x2)
        layer2(nc, sh, x2, t["c_wqk"], t["c_wvT"], t["c_wo"], t["c_temp"], t["c_bo"], x3)
        layer3(nc, sh, x3, [t[f"d_w{k}"] for k in range(CONVS)], t["d_bn"], t["out"])


def laid_out(i, np):
    f = np.float32
    t = {"x": i["x"].reshape(B, C, N)}
    t["ident"] = np.eye(P, dtype=f)
    member = (np.arange(C)[:, None] // CPG == np.arange(GROUPS)[None, :]).astype(f)
    t["gmat"] = member.reshape(G3, P, GROUPS)
    t["gmatT"] = member.T.reshape(GROUPS, G3, P)
    w = i["L0_conv_w_qkv"].T.reshape(C, 3, PAIRS, 2, D)
    qk = np.zeros((PAIRS, C, 2, 2, 64), f)
    qk[..., 0:D] = w[:, 0:2].transpose(2, 0, 1, 3, 4)
    t["a_wqk"] = qk.reshape(PAIRS, C, 2, 128)[..., 0:TP]
    t["a_wv"] = w[:, 2].reshape(C, C)
    wp = np.zeros((PAIRS, 2, 64, C), f)
    wp[:, :, 0:D] = i["L0_conv_w_proj"].T.reshape(PAIRS, 2, D, C)
    t["a_wp"] = wp.reshape(PAIRS, 128, C)[:, 0:TP].transpose(1, 0, 2)
    t["a_bp"] = i["L0_conv_b_proj"]
    spread = np.zeros((2, 2, PARTS, H, H, W), f)
    for r in range(H):
        for u in range(2):
            spread[u, u, :, r, r, :] = -1.0
    t["b_E"] = spread.reshape(2, P, H * W)
    t["b_minus"] = -(np.arange(P) % H).astype(f)[:, None]
    t["b_low"] = (np.arange(P) // H % PARTS).astype(f)[:, None]
    M7 = 2 * KS[-1] ** 2
    t["b_ymask"] = ((np.arange(M7) + 1) % 2).astype(f)[:, None]
    t["b_pw"] = np.stack([i[f"L1_conv_pw_w{K}"].reshape(P, P).T for K in KS])
    t["b_pb"] = np.stack([i[f"L1_conv_pw_b{K}"] for K in KS], 1)
    ob = np.zeros((M7, G3), f)
    for g, K in enumerate(KS):
        M, R = 2 * K * K, K // 2
        ob[0:M, g] = i[f"L1_conv_offset_b{K}"]
        t[f"b_ow{g}"] = i[f"L1_conv_offset_w{K}"].transpose(1, 2, 3, 0).reshape(P, K * K, M)
        t[f"b_dw{g}"] = i[f"L1_conv_dw_w{K}"].reshape(P, K * K).T
        grid = np.zeros((K, K, 2, H, W), f)
        grid[:, :, 0] = (np.arange(K)[:, None, None, None] - R + np.arange(H)[None, None, :, None])
        grid[:, :, 1] = (np.arange(K)[None, :, None, None] - R + np.arange(W)[None, None, None, :])
        t[f"b_grid{g}"] = grid.reshape(M, N)
    t["b_ob"] = ob
    t["b_f1"] = i["L1_conv_fc1_w"].reshape(HID, G3, P).transpose(1, 2, 0)
    t["b_f2"] = i["L1_conv_fc2_w"].reshape(G3, P, HID).transpose(2, 0, 1)
    w = i["L2_conv_w_qkv"].reshape(C, 3, C)
    t["c_wqk"] = w[:, 1::-1]
    wv = np.zeros((PAIRS, 2, 64, C), f)
    wv[:, :, 0:D] = w[:, 2].T.reshape(PAIRS, 2, D, C)
    t["c_wvT"] = wv.reshape(PAIRS, 128, C)[:, 0:TP].transpose(1, 0, 2)
    t["c_wo"] = i["L2_conv_w_out"].reshape(HEADS, D, C).transpose(1, 0, 2)
    t["c_temp"] = i["L2_conv_temperature"].reshape(HEADS)
    t["c_bo"] = i["L2_conv_b_out"]
    for k, name in enumerate(("lk_w", "w5", "w7a", "w7b", "w3a", "w3b", "w3c")):
        t[f"d_w{k}"] = i[f"L3_conv_{name}"].reshape(C, -1)
    t["d_bn"] = np.concatenate([i["L3_conv_obn"][None], i["L3_conv_br_bn"]]).transpose(2, 0, 1)
    return t


def kernel(**inputs):
    import numpy as np
    import concourse.bacc as bacc
    from concourse.bass_utils import run_bass_kernel_spmd as run

    nc = bacc.Bacc("TRN2", target_bir_lowering=False, num_devices=1)
    arrays, t = {}, {}
    for name, a in laid_out({k: np.asarray(v) for k, v in inputs.items()}, np).items():
        a = np.ascontiguousarray(a)
        arrays[f"in_{name}"] = a
        t[name] = nc.dram_tensor(f"in_{name}", a.shape, mybir.dt.from_np(a.dtype), kind="ExternalInput").ap()
    t["out"] = nc.dram_tensor("out_dram", [B, C, N], F32, kind="ExternalOutput").ap()
    program(nc, t)
    r = run(nc, [arrays], core_ids=[0])
    return r.results[0]["out_dram"].reshape(B, C, H, W)
```

```python
from contextlib import ExitStack

import concourse.bass as bass
from concourse import mybir
from concourse.alu_op_type import AluOpType as ALU

F32 = mybir.dt.float32
F16 = mybir.dt.float16
BF16 = mybir.dt.bfloat16
I32 = mybir.dt.int32
ACT = mybir.ActivationFunctionType
AX = mybir.AxisListType.X

P = 128
B = 8
C = 384
G3 = C // P
H = W = 32
N = H * W
HALF = N // 2
GROUPS = 32
CPG = C // GROUPS
HEADS = 8
D = C // HEADS
PAIRS = HEADS // 2
TP = 64 + D
NT = N // P
ROWB = P // W


def ds(start, size):
    return bass.DynSlice(start, size)


class Arena:

    def __init__(self, nc, tag):
        self.nc, self.tag, self.stack, self.sems = nc, tag, ExitStack(), []
        self.ahead = []

    def __enter__(self):
        self.stack.__enter__()
        return self

    def __exit__(self, *e):
        if self.sems and e[0] is None:
            clear(self.nc, self.sems)
        return self.stack.__exit__(*e)

    def sb(self, name, shape, dt=F32):
        return self.stack.enter_context(self.nc.sbuf_tensor(f"{self.tag}_{name}", shape, dt))

    def ps(self, name, shape, dt=F32):
        return self.stack.enter_context(self.nc.psum_tensor(f"{self.tag}_{name}", shape, dt))

    def sem(self, name):
        self.sems.append(self.stack.enter_context(self.nc.semaphore(f"{self.tag}_{name}")))
        return Sem(self.sems[-1], 0)

    def loop_sem(self, name):
        sem = Sem(self.sem(name).handle, 1)
        self.ahead.append(sem.handle)
        return sem

    def open(self):
        with self.nc.Block() as block:

            @block.sync
            def _(e):
                for sem in self.ahead:
                    e.sem_inc(sem, 1)


class Sem:

    def __init__(self, handle, start):
        self.handle, self.start = handle, start


def wait(e, sem, count):
    e.wait_ge(sem.handle, count + sem.start)


def clear(nc, sems):
    with nc.Block() as block:

        @block.sync
        def _(e):
            for sem in sems:
                e.sem_clear(sem)


def at(i, per, k):
    return i * per + max(k, 0)


def hold(sh, e, sem, value):
    wait(e, sem, value)
    e.sem_inc(sh["tick"], 1)


class Chain:

    def __init__(self, sh, eng, sem, i=None, per=0):
        self.sh = sh
        self.eng, self.sem, self.i, self.per, self.n = eng, sem, i, per, 0

    def __call__(self, ins):
        ins.then_inc(self.sem.handle, 1)
        self.n += 1
        if self.i is None:
            wait(self.eng, self.sem, self.n)
        else:
            hold(self.sh, self.eng, self.sem, self.i * self.per + self.n)

    def end(self):
        assert self.i is None or self.n == self.per, (self.n, self.per)


def load_shared(nc, sh, consts):
    with Arena(nc, "ld") as a, nc.Block() as block:
        s = a.sem("s")

        @block.sync
        def _(e):
            e.dma_start(sh["ident"][:], consts["ident"]).then_inc(s.handle, 16)
            e.dma_start(sh["gmat"][:], consts["gmat"].rearrange("g p n -> p g n")).then_inc(s.handle, 16)
            e.dma_start(sh["gmatT"][:], consts["gmatT"]).then_inc(s.handle, 16)
            wait(e, s, 48)


def norm_params(nc, sh, tag):
    with Arena(nc, tag) as a:
        mv = a.sb("mv", [P, G3, B, 2])
        sq = a.sb("sq", [P, G3, B])
        grp = a.sb("grp", [GROUPS, B, 2])
        gsq = a.sb("gsq", [GROUPS, B])
        bank = a.ps("bank", [P, 1 + G3, B * 2])
        p_grp = bank[0:GROUPS, 0, :]
        p_ch = bank[:, 1:1 + G3, :]
        s_d, s_dc, s_pe, s_a = a.sem("d"), a.sem("dc"), a.sem("pe"), a.sem("a")
        with nc.Block() as block:

            @block.vector
            def _(e):
                link = Chain(sh, e, s_dc)
                for g in range(G3):
                    for b in range(B):
                        last = e.bn_aggr(mv[:, g, b, :], sh["stat"][:, g, b, :, :].rearrange("p a s -> p (a s)"))
                link(last)
                link(e.tensor_tensor(sq[:], mv[:, :, :, 0], mv[:, :, :, 0], ALU.mult))
                e.tensor_tensor(mv[:, :, :, 1], mv[:, :, :, 1], sq[:], ALU.add).then_inc(s_d.handle, 1)
                wait(e, s_pe, 1)
                link(e.tensor_scalar(grp[:].rearrange("p b s -> p (b s)"), p_grp, 1.0 / CPG, None, ALU.mult))
                link(e.tensor_tensor(gsq[:], grp[:, :, 0], grp[:, :, 0], ALU.mult))
                link(e.tensor_tensor(gsq[:], grp[:, :, 1], gsq[:], ALU.subtract))
                e.tensor_scalar(gsq[:], gsq[:], 1e-5, None, ALU.add).then_inc(s_d.handle, 1)
                wait(e, s_a, 1)
                e.reciprocal(grp[:, :, 1], gsq[:]).then_inc(s_d.handle, 1)
                wait(e, s_pe, 2)
                e.tensor_copy(sh["gn"][:].rearrange("p g b s -> p g (b s)"), p_ch).then_inc(s_d.handle, 1)
                wait(e, s_d, 4)

            @block.scalar
            def _(e):
                wait(e, s_d, 2)
                e.activation(gsq[:], gsq[:], ACT.Sqrt).then_inc(s_a.handle, 1)

            @block.tensor
            def _(e):
                wait(e, s_d, 1)
                for g in range(G3):
                    last = e.matmul(p_grp, sh["gmat"][:, g, :], mv[:, g, :, :].rearrange("p b s -> p (b s)"),
                                    start=(g == 0), stop=(g == G3 - 1))
                last.then_inc(s_pe.handle, 1)
                wait(e, s_d, 3)
                for g in range(G3):
                    last = e.matmul(p_ch[:, g, :], sh["gmatT"][:, g, :], grp[:].rearrange("p b s -> p (b s)"),
                                    start=True, stop=True)
                last.then_inc(s_pe.handle, 1)


def input_stats(nc, sh, x):
    with Arena(nc, "i") as a:
        xs = a.sb("xs", [P, B, G3, N])
        s_x = [a.sem(f"x{b}") for b in range(B)]
        s_st = a.sem("st")
        with nc.Block() as block:

            @block.sync
            def _(e):
                for b in range(B):
                    e.dma_start(xs[:, b, :, :], x.rearrange("b (g p) n -> p b g n", p=P)[:, b, :, :]).then_inc(s_x[b].handle, 16)

            @block.vector
            def _(e):
                for b in range(B):
                    wait(e, s_x[b], 16)
                    for g in range(G3):
                        for n in range(2):
                            last = e.bn_stats(sh["stat"][:, g, b, n, :], xs[:, b, g, n * HALF:(n + 1) * HALF])
                last.then_inc(s_st.handle, 1)
                wait(e, s_st, 1)


def layer0(nc, sh, x, w_qk, w_v, w_proj, b_proj, y):
    input_stats(nc, sh, x)
    norm_params(nc, sh, "n0")
    xv = x.rearrange("b (g p) n -> p b g n", p=P)
    yv = y.rearrange("b (g p) n -> p b g n", p=P)
    TH = NT
    TB = HEADS * TH
    SCALE = float(D) ** -0.5
    RING = 4
    UNITS = 6
    ROWS_OF = (0, 64)
    with Arena(nc, "a") as a:
        xh = a.sb("xh", [P, G3, N])
        xr = a.sb("xr", [P, G3, N])
        h = a.sb("h", [P, G3, N])
        wqk = a.sb("wqk", [P, PAIRS, G3, 2, TP])
        wv = a.sb("wv", [P, G3, C])
        wp = a.sb("wp", [TP, PAIRS, C])
        bp = a.sb("bp", [P, G3])
        idh = a.sb("idh", [P, P], F16)
        q = a.sb("q", [TP, 2, 2, N], F16)
        kh = a.sb("kh", [TP, 2, 2, N], F16)
        kl = a.sb("kl", [TP, 2, 2, N], F16)
        v = a.sb("v", [P, 2, NT, 2, TP], F16)
        att = a.sb("att", [P, RING, N])
        ah = a.sb("ah", [P, RING, N], F16)
        al = a.sb("al", [P, RING, N], F16)
        attT = a.sb("attT", [P, 2, 2, NT, HALF], F16)
        nmax = a.sb("nmax", [P, RING])
        den = a.sb("den", [P, RING])
        rden = a.sb("rden", [P, RING])
        oh = a.sb("oh", [TP, HALF])
        o = a.sb("o", [TP, PAIRS, N])
        p_s = [a.ps(f"p_s{i}", [P, 2, HALF]) for i in range(2)]
        p_t = a.ps("p_t", [P, 2, NT, P], F16)
        p_o = a.ps("p_o", [P, HALF])
        p_j = a.ps("p_j", [P, HALF])
        s_w, s_xh, s_xr, s_y = (a.sem(n) for n in ("w", "xh", "xr", "y"))
        s_z, s_h, s_pj, s_ja, s_jv = (a.loop_sem(n) for n in ("z", "h", "pj", "ja", "jv"))
        s_s, s_m, s_e, s_ri, s_hi, s_lo, s_t, s_ta, s_tv = (a.loop_sem(n) for n in ("s", "m", "e", "ri", "hi", "lo", "t", "ta", "tv"))
        s_o, s_oa, s_on, s_f, s_fo, s_st, s_yd = (a.loop_sem(n) for n in ("o", "oa", "on", "f", "fo", "st", "yd"))
        a.open()
        JA = (2, 2, 4, 4, 1, 1)
        PJA = sum(JA)

        with nc.Block() as block:

            @block.sync
            def _(e):
                e.dma_start(wqk[:], w_qk.rearrange("t (g p) s n -> p t g s n", p=P)).then_inc(s_w.handle, 16)
                e.dma_start(wv[:], w_v.rearrange("(g p) n -> p g n", p=P)).then_inc(s_w.handle, 16)
                e.dma_start(wp[:], w_proj).then_inc(s_w.handle, 16)
                e.dma_start(bp[:], b_proj.rearrange("(g p) -> p g", p=P), allow_slow_non_contiguous=True).then_inc(s_w.handle, 16)
                wait(e, s_w, 64)

            @block.vector
            def _(e):
                e.memset(q[:], 0.0).then_inc(s_z.handle, 1)
                e.memset(kh[:], 0.0).then_inc(s_z.handle, 1)
                e.memset(kl[:], 0.0).then_inc(s_z.handle, 1)
                e.tensor_copy(idh[:], sh["ident"][:]).then_inc(s_z.handle, 1)

            @block.gpsimd
            def _(e):
                e.memset(v[:], 0.0).then_inc(s_z.handle, 1)
                e.memset(o[:], 0.0).then_inc(s_z.handle, 1)

        def project(e, i, t, unit):
            if unit == 0 and t == 0:
                wait(e, s_h, i // PAIRS + 1 if not isinstance(i, int) else 1)
            prev = i * PJA + sum(JA[:unit])
            wait(e, s_ja, prev)
            wait(e, s_jv, prev)
            if unit < 4:
                s, n = divmod(unit, 2)
                for g in range(G3):
                    last = e.matmul(p_j[0:TP, :], wqk[:, t, g, s, :], h[:, g, n * HALF:(n + 1) * HALF], start=(g == 0), stop=(g == G3 - 1))
            else:
                for c in range(4):
                    for g in range(G3):
                        px = (4 * (unit - 4) + c) * P
                        last = e.matmul(p_j[:, c * 2 * D:(c + 1) * 2 * D], h[:, g, px:px + P], wv[:, g, t * 2 * D:(t + 1) * 2 * D],
                                        start=(g == 0), stop=(g == G3 - 1))
            last.then_inc(s_pj.handle, 1)

        def high(e, i, t, unit):
            if unit == 0 and not isinstance(i, int):
                wait(e, s_s, (i - 1) * 16)
            wait(e, s_pj, i * UNITS + unit + 1)
            u, n = t % 2, unit % 2
            cols = slice(n * HALF, (n + 1) * HALF)
            if unit < 2:
                for hd, r in enumerate(ROWS_OF):
                    e.activation(q[r:r + D, u, hd, cols], p_j[r:r + D, :], ACT.Copy, scale=SCALE).then_inc(s_ja.handle, 1)
            elif unit < 4:
                for hd, r in enumerate(ROWS_OF):
                    for to in ROWS_OF:
                        e.copy(kh[to:to + D, u, hd, cols], p_j[r:r + D, :]).then_inc(s_ja.handle, 1)
            else:
                if unit == 4 and not isinstance(i, int):
                    wait(e, s_o, (i - 1) * 4)
                e.copy(v[:, u, 4 * n:4 * n + 4, :, 0:D], p_j[:, 0:8 * D].rearrange("p (c s d) -> p c s d", c=4, s=2)).then_inc(s_ja.handle, 1)

        def low(e, i, t, unit):
            wait(e, s_ja, i * PJA + sum(JA[:unit + 1]))
            u, n = t % 2, unit % 2
            cols = slice(n * HALF, (n + 1) * HALF)
            if unit < 2:
                for hd, r in enumerate(ROWS_OF):
                    z = 64 - r
                    e.scalar_tensor_tensor(q[z:z + D, u, hd, cols], p_j[r:r + D, :], SCALE, q[r:r + D, u, hd, cols],
                                           ALU.mult, ALU.subtract).then_inc(s_jv.handle, 1)
            elif unit < 4:
                for hd, r in enumerate(ROWS_OF):
                    for to in ROWS_OF:
                        e.tensor_tensor(kl[to:to + D, u, hd, cols], p_j[r:r + D, :], kh[r:r + D, u, hd, cols], ALU.subtract).then_inc(s_jv.handle, 1)
            else:
                e.tensor_tensor(v[:, u, 4 * n:4 * n + 4, :, 64:TP], p_j[:, 0:8 * D].rearrange("p (c s d) -> p c s d", c=4, s=2),
                                v[:, u, 4 * n:4 * n + 4, :, 0:D], ALU.subtract).then_inc(s_jv.handle, 1)

        def norm(e, b):
            wait(e, s_xh, (b + 1) * 16)
            wait(e, s_pj, b * (PAIRS * UNITS))
            bb = b % B if not isinstance(b, int) else b
            for g in range(G3):
                gn = sh["gn"][:, g, ds(bb, 1), :].rearrange("p o s -> p (o s)")
                last = e.tensor_scalar(h[:, g, :], xh[:, g, :], gn[:, 0:1], gn[:, 1:2], ALU.subtract, ALU.mult)
            last.then_inc(s_h.handle, 1)

        UNIT_AT = (0, 2, 4, 6, 8, 10)

        def unit_in(m):
            t, r = divmod(m, 16)
            return (t + 1, UNIT_AT.index(r)) if 0 <= t < PAIRS and r in UNIT_AT else None

        with nc.Block() as block:

            @block.sync
            def _(e):
                e.dma_start(xh[:], xv[:, 0, :, :]).then_inc(s_xh.handle, 16)
                with e.Fori(0, B) as b:
                    wait(e, s_yd, b)
                    e.dma_start(xr[:].unsqueeze(1), xv[:, ds(b, 1), :, :]).then_inc(s_xr.handle, 16)
                    hold(sh, e, s_h, b + 1)
                    e.dma_start(xh[:].unsqueeze(1), xv[:, ds((b + 1) % B, 1), :, :]).then_inc(s_xh.handle, 16)
                    wait(e, s_fo, at(b, 6, 6))
                    e.dma_start(yv[:, ds(b, 1), :, :], xr[:].unsqueeze(1)).then_inc(s_y.handle, 16)
                    hold(sh, e, s_st, b + 1)
                    wait(e, s_y, (b + 1) * 16)
                    e.sem_inc(s_yd.handle, 1)
                wait(e, s_xh, 16 * (B + 1))

            @block.tensor
            def _(e):
                for unit in range(UNITS):
                    project(e, 0, 0, unit)
                with e.Fori(0, B) as b:
                    i0 = b * PAIRS

                    def scores(m):
                        hd, c = m // NT, m % NT
                        t = hd // 2
                        if m % 16 == 0:
                            wait(e, s_jv, (i0 + t) * PJA + sum(JA[0:4]))
                        wait(e, s_e, at(b, TB, m - 1))
                        if m < 2:
                            wait(e, s_fo, b * 6)
                        for n in range(2):
                            for k, r in ((kh, 0), (kl, 1)):
                                last = e.matmul(p_s[m % 2][:, n, :], q[:, t % 2, hd % 2, c * P:(c + 1) * P],
                                                k[:, t % 2, hd % 2, n * HALF:(n + 1) * HALF], start=(r == 0), stop=(r == 1))
                        last.then_inc(s_s.handle, 1)

                    def turn(m):
                        wait(e, s_ta, at(b, TB, m))
                        wait(e, s_tv, at(b, TB, m))
                        wait(e, s_lo, at(b, TB, m + 1))
                        for r, part in enumerate((ah, al)):
                            for c in range(NT):
                                last = e.transpose(p_t[:, r, c, :], part[:, m % RING, c * P:(c + 1) * P], idh[:])
                        last.then_inc(s_t.handle, 1)

                    def weigh(j):
                        t, hd = j // 4, j // 2 % 2
                        if j % 4 == 0:
                            wait(e, s_jv, (i0 + t) * PJA + PJA)
                        wait(e, s_on, at(b, 16, j))
                        wait(e, s_ta, at(b, TB, 4 * j + 4))
                        wait(e, s_tv, at(b, TB, 4 * j + 4))
                        for r in range(2):
                            for c in range(NT):
                                last = e.matmul(p_o[0:TP, :], v[:, t % 2, c, hd, :], attT[:, j % 2, r, c, :],
                                                start=(r == 0 and c == 0), stop=(r == 1 and c == NT - 1))
                        last.then_inc(s_o.handle, 1)

                    for m in range(-2, TB + 5):
                        if m + 2 < TB:
                            scores(m + 2)
                        if 0 <= m - 2 < TB:
                            turn(m - 2)
                        if unit_in(m):
                            t, unit = unit_in(m)
                            project(e, i0 + t, t % PAIRS, unit)
                        if m >= 7 and (m - 7) % 4 == 0:
                            weigh((m - 7) // 4)
                    wait(e, s_e, (b + 1) * TB)
                    wait(e, s_on, (b + 1) * 16)
                    for m in range(2 * G3):
                        g, n = m // 2, m % 2
                        wait(e, s_fo, at(b, 6, m - 3))
                        for t in range(PAIRS):
                            last = e.matmul(p_s[m // 2 % 2][:, m % 2, :], wp[:, t, g * P:(g + 1) * P],
                                            o[:, t, n * HALF:(n + 1) * HALF], start=(t == 0), stop=(t == PAIRS - 1))
                        last.then_inc(s_f.handle, 1)

            @block.gpsimd
            def _(e):
                with e.Fori(0, B) as b:
                    for m in range(TB):
                        r = m % RING
                        wait(e, s_t, at(b, TB, m + 1 - RING))
                        hold(sh, e, s_ri, at(b, TB, m + 1))
                        e.tensor_scalar(ah[:, r, :], att[:, r, :], rden[:, r:r + 1], None, ALU.mult).then_inc(s_hi.handle, 1)

            @block.scalar
            def _(e):
                for unit in range(UNITS):
                    high(e, 0, 0, unit)
                with e.Fori(0, B) as b:
                    i0 = b * PAIRS
                    for m in range(-2, TB + 5):
                        if 0 <= m + 1 < TB:
                            k, r = m + 1, (m + 1) % RING
                            wait(e, s_m, at(b, TB, k + 1))
                            wait(e, s_lo, at(b, TB, k + 1 - RING))
                            e.activation(att[:, r, :], p_s[k % 2][:].rearrange("p a n -> p (a n)"), ACT.Exp,
                                         bias=nmax[:, r:r + 1], accum_out=den[:, r:r + 1]).then_inc(s_e.handle, 1)
                        if 0 <= m - 2 < TB:
                            k = m - 2
                            wait(e, s_t, at(b, TB, k + 1))
                            if k % 4 == 0:
                                wait(e, s_o, at(b, 16, k // 4 - 1))
                            e.copy(attT[:, k // 4 % 2, 0, :, (k % 4) * P:(k % 4 + 1) * P], p_t[:, 0, :, :]).then_inc(s_ta.handle, 1)
                        if unit_in(m - 1):
                            t, unit = unit_in(m - 1)
                            high(e, i0 + t, t, unit)
                        if m >= 8 and (m - 8) % 4 == 0:
                            j = (m - 8) // 4
                            r = ROWS_OF[j // 2 % 2]
                            wait(e, s_o, at(b, 16, j + 1))
                            wait(e, s_on, at(b, 16, j))
                            e.copy(oh[r:r + D, :], p_o[0:D, :]).then_inc(s_oa.handle, 1)

            @block.vector
            def _(e):
                norm(e, 0)
                for unit in range(UNITS):
                    low(e, 0, 0, unit)
                with e.Fori(0, B) as b:
                    i0 = b * PAIRS
                    for m in range(-2, TB + 5):
                        if 0 <= m - 1 < TB:
                            k, r = m - 1, (m - 1) % RING
                            wait(e, s_hi, at(b, TB, k + 1))
                            wait(e, s_t, at(b, TB, k + 1 - RING))
                            e.scalar_tensor_tensor(al[:, r, :], att[:, r, :], rden[:, r:r + 1], ah[:, r, :],
                                                   ALU.mult, ALU.subtract).then_inc(s_lo.handle, 1)
                        if m + 2 < TB:
                            k, r = m + 2, (m + 2) % RING
                            wait(e, s_s, at(b, TB, k + 1))
                            wait(e, s_e, at(b, TB, k + 1 - RING))
                            e.tensor_reduce(nmax[:, r:r + 1], p_s[k % 2][:].rearrange("p a n -> p (a n)"), AX, ALU.max,
                                            negate=True).then_inc(s_m.handle, 1)
                        if 0 <= m + 1 < TB:
                            k, r = m + 1, (m + 1) % RING
                            wait(e, s_e, at(b, TB, k + 1))
                            wait(e, s_lo, at(b, TB, k + 1 - RING))
                            e.reciprocal(rden[:, r:r + 1], den[:, r:r + 1]).then_inc(s_ri.handle, 1)
                        if 0 <= m - 2 < TB:
                            k = m - 2
                            wait(e, s_t, at(b, TB, k + 1))
                            if k % 4 == 0:
                                wait(e, s_o, at(b, 16, k // 4 - 1))
                            e.tensor_copy(attT[:, k // 4 % 2, 1, :, (k % 4) * P:(k % 4 + 1) * P], p_t[:, 1, :, :]).then_inc(s_tv.handle, 1)
                        if m == 3 * 16 - 3:
                            norm(e, b + 1)
                        if unit_in(m - 1):
                            t, unit = unit_in(m - 1)
                            low(e, i0 + t, t, unit)
                        if m >= 8 and (m - 8) % 4 == 0:
                            j = (m - 8) // 4
                            r = ROWS_OF[j // 2 % 2]
                            t, n = j // 4, j % 2
                            wait(e, s_oa, at(b, 16, j + 1))
                            e.tensor_tensor(o[r:r + D, t, n * HALF:(n + 1) * HALF], p_o[64:TP, :], oh[r:r + D, :], ALU.add).then_inc(s_on.handle, 1)
                    wait(e, s_xr, (b + 1) * 16)
                    for m in range(2 * G3):
                        g, n = m // 2, m % 2
                        wait(e, s_f, at(b, 6, m + 1))
                        part = xr[:, g, n * HALF:(n + 1) * HALF]
                        e.scalar_tensor_tensor(part, p_s[m // 2 % 2][:, m % 2, :], bp[:, g:g + 1], part, ALU.add, ALU.add).then_inc(s_fo.handle, 1)
                    wait(e, s_fo, at(b, 6, 6))
                    for m in range(2 * G3):
                        g, n = m // 2, m % 2
                        last = e.bn_stats(one(sh["stat"][:, g, ds(b, 1), n, :]), xr[:, g, n * HALF:(n + 1) * HALF])
                    last.then_inc(s_st.handle, 1)


def normalise(e, sh, h, xs, b):
    for g in range(G3):
        last = e.tensor_scalar(h[:, g, :], xs[:, g, :], one(sh["gn"][:, g, ds(b, 1), 0:1]), one(sh["gn"][:, g, ds(b, 1), 1:2]),
                               ALU.subtract, ALU.mult)
    return last


def one(ap):
    return ap.rearrange("p o n -> p (o n)")


def layer2(nc, sh, x, w_qk, w_vT, w_out, temp, b_out, y):
    xv = x.rearrange("b (g p) n -> p b g n", p=P)
    yv = y.rearrange("b (g p) n -> p b g n", p=P)
    norm_params(nc, sh, "n2")
    with Arena(nc, "c") as a:
        xs = a.sb("xs", [P, 2, G3, N])
        h = a.sb("h", [P, G3, N])
        w = a.sb("w", [P, G3, 2, C])
        wvT = a.sb("wvT", [TP, PAIRS, C])
        wo = a.sb("wo", [D, HEADS, C])
        tmp = a.sb("temp", [D, HEADS])
        bo = a.sb("bo", [P, G3])
        ones = a.sb("ones", [P, D])
        kq = a.sb("kq", [P, NT, HEADS, TP])
        dk = a.sb("dk", [D, HEADS, D])
        dq = a.sb("dq", [P, HEADS, D])
        rk = a.sb("rk", [D, HEADS])
        rq = a.sb("rq", [D, HEADS, D])
        at2 = a.sb("att", [D, HEADS, D])
        mx = a.sb("mx", [D, HEADS])
        attT = a.sb("attT", [D, HEADS, D])
        m = a.sb("m", [TP, PAIRS, C])
        f = a.sb("f", [P, G3, C])
        xo = a.sb("xo", [P, G3, N])
        p_a = [a.ps(f"p_a{i}", [P, 512]) for i in range(4)]
        p_g = a.ps("p_g", [P, 2, 512])
        p_m = a.ps("p_m", [P, 2, 512])
        gram = p_g[:, :, 0:4 * TP].rearrange("p u (h c) -> p u h c", h=4)
        s_w, s_x, s_y, s_z = (a.sem(n) for n in ("w", "x", "y", "z"))
        s_h, s_a, s_ae, s_g, s_dq, s_qq, s_c, s_sq, s_ex, s_yd = (a.loop_sem(n) for n in ("h", "a", "ae", "g", "dq", "qq", "c", "sq", "ex", "yd"))
        s_sub, s_an, s_tt, s_te, s_m, s_me, s_f, s_fe, s_o, s_oe, s_st = (
            a.loop_sem(n) for n in ("sub", "an", "tt", "te", "m", "me", "f", "fe", "o", "oe", "st"))
        a.open()
        with nc.Block() as block:

            @block.sync
            def _(e):
                e.dma_start(w[:], w_qk.rearrange("(g p) s n -> p g s n", p=P)).then_inc(s_w.handle, 16)
                e.dma_start(wvT[:], w_vT).then_inc(s_w.handle, 16)
                e.dma_start(wo[:], w_out).then_inc(s_w.handle, 16)
                e.dma_start(tmp[:], temp.partition_broadcast(D)).then_inc(s_w.handle, 16)
                e.dma_start(bo[:], b_out.rearrange("(g p) -> p g", p=P), allow_slow_non_contiguous=True).then_inc(s_w.handle, 16)
                wait(e, s_w, 80)

            @block.gpsimd
            def _(e):
                e.memset(kq[:], 0.0).then_inc(s_z.handle, 1)
                e.memset(ones[:], 1.0).then_inc(s_z.handle, 1)
                e.memset(m[:], 0.0).then_inc(s_z.handle, 1)
                wait(e, s_z, 3)

        with nc.Block() as block:

            @block.sync
            def _(e):
                with e.Fori(0, B // 2) as b2:
                    for u in range(2):
                        b = b2 * 2 + u
                        wait(e, s_oe, at(b2, 12, 6 * u))
                        e.dma_start(xs[:, u, :, :].unsqueeze(1), xv[:, ds(b, 1), :, :]).then_inc(s_x.handle, 16)
                    for u in range(2):
                        b = b2 * 2 + u
                        wait(e, s_oe, b * 6 + 6)
                        e.dma_start(yv[:, ds(b, 1), :, :], xo[:].unsqueeze(1)).then_inc(s_y.handle, 16)
                        wait(e, s_y, (b + 1) * 16)
                        e.sem_inc(s_yd.handle, 1)

            @block.vector
            def _(e):
                with e.Fori(0, B // 2) as b2:
                    for u in range(2):
                        b = b2 * 2 + u
                        link = Chain(sh, e, s_c, b, 5)
                        wait(e, s_x, b * 16 + 16)
                        wait(e, s_o, at(b, 6, 0))
                        normalise(e, sh, h, xs[:, u, :, :], b).then_inc(s_h.handle, 1)
                        wait(e, s_g, b + 1)
                        idk = sh["ident"][0:D, 0:D].unsqueeze(1).broadcast_to([D, 4, D])
                        idq = sh["ident"][64:TP, 64:TP].unsqueeze(1).broadcast_to([D, 4, D])
                        for v in range(2):
                            e.tensor_tensor(dq[64:TP, 4 * v:4 * v + 4, :], gram[64:TP, v, :, 64:TP], idq, ALU.mult).then_inc(s_dq.handle, 1)
                        for v in range(2):
                            last = e.tensor_tensor(dk[:, 4 * v:4 * v + 4, :], gram[0:D, v, :, 0:D], idk, ALU.mult)
                        link(last)
                        e.tensor_reduce(rk[:], dk[:], AX, ALU.add).then_inc(s_dq.handle, 1)
                        wait(e, s_sq, b * 2 + 1)
                        e.tensor_scalar(rk[:], rk[:], 1e-12, None, ALU.max)
                        wait(e, s_sq, b * 2 + 2)
                        link(e.tensor_scalar(rq[:], rq[:], 1e-12, None, ALU.max))
                        e.reciprocal(rk[:], rk[:])
                        link(e.reciprocal(rq[:], rq[:]))
                        e.tensor_tensor(rk[:], rk[:], tmp[:], ALU.mult)
                        for v in range(2):
                            last = e.tensor_tensor(at2[:, 4 * v:4 * v + 4, :], gram[0:D, v, :, 64:TP], rq[:, 4 * v:4 * v + 4, :], ALU.mult)
                        link(last)
                        link(e.tensor_tensor(at2[:], at2[:], rk[:].unsqueeze(2).broadcast_to([D, HEADS, D]), ALU.mult))
                        e.tensor_reduce(mx[:], at2[:], AX, ALU.max).then_inc(s_sub.handle, 1)
                        wait(e, s_sub, b * 4 + 1)
                        e.tensor_tensor(at2[:], at2[:], mx[:].unsqueeze(2).broadcast_to([D, HEADS, D]), ALU.subtract).then_inc(s_sub.handle, 1)
                        wait(e, s_ex, b + 1)
                        e.tensor_reduce(mx[:], at2[:], AX, ALU.add).then_inc(s_sub.handle, 1)
                        wait(e, s_sub, b * 4 + 3)
                        e.reciprocal(mx[:], mx[:]).then_inc(s_sub.handle, 1)
                        wait(e, s_sub, b * 4 + 4)
                        e.tensor_tensor(at2[:], at2[:], mx[:].unsqueeze(2).broadcast_to([D, HEADS, D]), ALU.mult).then_inc(s_an.handle, 1)
                        wait(e, s_tt, b + 1)
                        e.tensor_copy(attT[:].rearrange("p h d -> p (h d)"), p_m[0:D, 0, 0:C]).then_inc(s_te.handle, 1)
                        for v in range(PAIRS):
                            wait(e, s_m, b * 4 + v + 1)
                            for r in (0, 64):
                                last = e.tensor_copy(m[r:r + D, v, :], p_m[r:r + D, v % 2, 0:C])
                            last.then_inc(s_me.handle, 1)
                        for g in range(G3):
                            wait(e, s_f, b * 3 + g + 1)
                            e.tensor_copy(f[:, g, :], p_a[g][:, 0:C]).then_inc(s_fe.handle, 1)
                        wait(e, s_yd, b)
                        for i in range(2 * G3):
                            g, n = i // 2, i % 2
                            wait(e, s_o, b * 6 + i + 1)
                            e.scalar_tensor_tensor(xo[:, g, n * HALF:(n + 1) * HALF], p_a[i % 4][:], bo[:, g:g + 1],
                                                   xs[:, u, g, n * HALF:(n + 1) * HALF], ALU.add, ALU.add).then_inc(s_oe.handle, 1)
                        wait(e, s_oe, b * 6 + 6)
                        for i in range(2 * G3):
                            g, n = i // 2, i % 2
                            last = e.bn_stats(one(sh["stat"][:, g, ds(b, 1), n, :]), xo[:, g, n * HALF:(n + 1) * HALF])
                        last.then_inc(s_st.handle, 1)
                        link.end()
                wait(e, s_st, B)

            @block.scalar
            def _(e):
                with e.Fori(0, B) as b:
                    for i in range(2 * NT):
                        c, s = i // 2, i % 2
                        wait(e, s_a, b * (2 * NT) + i + 1)
                        if i == 0:
                            wait(e, s_g, b)
                        e.copy(kq[:, c, :, 64 * s:64 * s + D], p_a[i % 4][:, 0:C].rearrange("p (h d) -> p h d", h=HEADS)).then_inc(s_ae.handle, 1)
                    wait(e, s_dq, b * 3 + 3)
                    e.activation(rk[:], rk[:], ACT.Sqrt).then_inc(s_sq.handle, 1)
                    wait(e, s_qq, b + 1)
                    e.activation(rq[:].rearrange("p h d -> p (h d)"), p_m[0:D, 0, 0:C], ACT.Sqrt).then_inc(s_sq.handle, 1)
                    wait(e, s_sub, b * 4 + 2)
                    e.activation(at2[:], at2[:], ACT.Exp).then_inc(s_ex.handle, 1)

            @block.tensor
            def _(e):
                with e.Fori(0, B) as b:
                    for i in range(2 * NT):
                        c, s = i // 2, i % 2
                        if i == 0:
                            wait(e, s_h, b + 1)
                            wait(e, s_oe, b * 6)
                        if i >= 4:
                            wait(e, s_ae, b * (2 * NT) + i - 3)
                        for g in range(G3):
                            last = e.matmul(p_a[i % 4][:, 0:C], h[:, g, c * P:(c + 1) * P], w[:, g, s, :], start=(g == 0), stop=(g == G3 - 1))
                        last.then_inc(s_a.handle, 1)
                    wait(e, s_ae, b * (2 * NT) + 2 * NT)
                    for hd in range(HEADS):
                        for c in range(NT):
                            last = e.matmul(gram[0:TP, hd // 4, hd % 4, :], kq[:, c, hd, :], kq[:, c, hd, :], start=(c == 0), stop=(c == NT - 1))
                    last.then_inc(s_g.handle, 1)
                    hold(sh, e, s_dq, b * 3 + 2)
                    e.matmul(p_m[0:D, 0, 0:C], ones[64:TP, :], dq[64:TP, :, :].rearrange("p h d -> p (h d)"), start=True, stop=True).then_inc(s_qq.handle, 1)
                    hold(sh, e, s_an, b + 1)
                    for hd in range(HEADS):
                        last = e.transpose(p_m[0:D, 0, hd * D:(hd + 1) * D], at2[:, hd, :], sh["ident"][0:D, 0:D])
                    last.then_inc(s_tt.handle, 1)
                    hold(sh, e, s_te, b + 1)
                    for v in range(PAIRS):
                        if v >= 2:
                            hold(sh, e, s_me, b * 4 + v - 1)
                        for u in range(2):
                            last = e.matmul(p_m[64 * u:64 * u + D, v % 2, 0:C], attT[:, 2 * v + u, :], wo[:, 2 * v + u, :], start=True, stop=True)
                        last.then_inc(s_m.handle, 1)
                    wait(e, s_me, b * 4 + 4)
                    for g in range(G3):
                        for v in range(PAIRS):
                            last = e.matmul(p_a[g][:, 0:C], wvT[:, v, g * P:(g + 1) * P], m[:, v, :], start=(v == 0), stop=(v == PAIRS - 1))
                        last.then_inc(s_f.handle, 1)
                    wait(e, s_fe, b * 3 + 3)
                    for i in range(2 * G3):
                        o, n = i // 2, i % 2
                        if i >= 4:
                            wait(e, s_oe, b * 6 + i - 3)
                        for g in range(G3):
                            last = e.matmul(p_a[i % 4][:], f[:, g, o * P:(o + 1) * P], h[:, g, n * HALF:(n + 1) * HALF], start=(g == 0), stop=(g == G3 - 1))
                        last.then_inc(s_o.handle, 1)


KB = 13
REACH = KB // 2
SHAPES = [(13, 1), (5, 1), (7, 1), (7, 2), (3, 3), (3, 4), (3, 5)]
CONVS = len(SHAPES)
TAPS3 = [k * k for k, _ in SHAPES]
PITCH = W + REACH
KROWS = 24
BANDS = 5
TLEN = BANDS * ROWB * PITCH
CH4 = 4


def layer3(nc, sh, x, weights, bn, y):
    xv = x.rearrange("b (g p) n -> p g b n", p=P)
    yv = y.rearrange("b (g p) n -> p g b n", p=P)
    NTAP = sum(TAPS3)
    wm_dram = nc.dram_tensor("merged_kernels", [C, KROWS * PITCH], F32).ap()
    norm_params(nc, sh, "n3")
    with Arena(nc, "d") as a:
        wr = a.sb("wr", [P, G3, NTAP])
        bnp = a.sb("bnp", [P, G3, CONVS, 4])
        dev = a.sb("dev", [P, G3, CONVS])
        scale = a.sb("scale", [P, G3, CONVS])
        shift = a.sb("shift", [P, G3, CONVS])
        sft = a.sb("sft", [P, G3])
        wm = a.sb("wm", [P, G3, KROWS, PITCH])
        xs = a.sb("xs", [P, B, N])
        h = a.sb("h", [P, 2, N])
        xT = a.sb("xT", [P, P, B * NT])
        yT = a.sb("yT", [P, B * NT, P])
        win = a.sb("win", [P, 2, CH4, TLEN])
        toe = a.sb("toe", [P, 4, CH4, BANDS * ROWB, W])
        xo = a.sb("xo", [P, 2, N])
        p_t = [a.ps(f"p_t{i}", [P, NT, P]) for i in range(2)]
        p_c = [a.ps(f"p_c{i}", [P, 8, B * NT]) for i in range(2)]
        s_w, s_wm, s_c, s_v = (a.sem(n) for n in ("w", "wm", "c", "v"))
        with nc.Block() as block:

            @block.sync
            def _(e):
                off = 0
                for i, wi in enumerate(weights):
                    e.dma_start(wr[:, :, off:off + TAPS3[i]], wi.rearrange("(g p) t -> p g t", p=P)).then_inc(s_w.handle, 16)
                    off += TAPS3[i]
                e.dma_start(bnp[:], bn.rearrange("(g p) i f -> p g i f", p=P)).then_inc(s_w.handle, 16)
                wait(e, s_wm, 1)
                e.dma_start(wm_dram.rearrange("(g p) n -> p g n", p=P), wm[:].rearrange("p g r c -> p g (r c)")).then_inc(s_w.handle, 16)
                wait(e, s_w, 16 * (CONVS + 2))

            @block.scalar
            def _(e):
                wait(e, s_v, 1)
                e.activation(dev[:], dev[:], ACT.Sqrt).then_inc(s_v.handle, 1)

            @block.vector
            def _(e):
                link = Chain(sh, e, s_c)
                link(e.memset(wm[:], 0.0))
                wait(e, s_w, 16 * (CONVS + 1))
                e.tensor_scalar(dev[:], bnp[:, :, :, 3], 1e-5, None, ALU.add).then_inc(s_v.handle, 1)
                wait(e, s_v, 2)
                link(e.reciprocal(dev[:], dev[:]))
                link(e.tensor_tensor(scale[:], bnp[:, :, :, 0], dev[:], ALU.mult))
                link(e.tensor_tensor(shift[:], bnp[:, :, :, 2], scale[:], ALU.mult))
                link(e.tensor_tensor(shift[:], bnp[:, :, :, 1], shift[:], ALU.subtract))
                link(e.tensor_reduce(sft[:], shift[:], AX, ALU.add))
                off = 0
                for i, (k, d) in enumerate(SHAPES):
                    first = REACH - d * (k - 1) // 2
                    span = d * (k - 1) + 1
                    for g in range(G3):
                        into = wm[:, g, REACH + first:REACH + first + span:d, first:first + span:d]
                        last = e.scalar_tensor_tensor(into, wr[:, g, off:off + k * k].rearrange("p (a b) -> p a b", a=k),
                                                      scale[:, g, i:i + 1], into, ALU.mult, ALU.add)
                    if i + 1 < CONVS:
                        link(last)
                    off += k * k
                last.then_inc(s_wm.handle, 1)
                wait(e, s_wm, 1)

        s_x = a.sem("x")
        s_h, s_t, s_te, s_p, s_pe, s_b, s_o, s_yd = (a.loop_sem(n) for n in ("h", "t", "te", "p", "pe", "b", "o", "yd"))
        s_y = [a.sem(f"y{u}") for u in range(2)]
        s_win = [a.sem(f"win{q}") for q in range(2)]
        s_toe = [a.loop_sem(f"toe{q}") for q in range(4)]
        a.open()
        CB = P // (4 * CH4)
        win_m = win[:].rearrange("p q c (r w) -> p q c r w", w=PITCH)
        xT_m = xT[:].rearrange("p c (b i) -> p c b i", b=B)
        with nc.Block() as block:

            @block.sync
            def _(e):
                with e.Fori(0, G3 * CB) as i:
                    for q in range(4):
                        wait(e, s_toe[(q - 2) % 4], i + 1)
                        for r in range(ROWB):
                            src = bass.AP(wm_dram.tensor, REACH * 2 + 1 + r * PITCH, [[KROWS * PITCH, C], [1, W], [1, TLEN - PITCH + W]])
                            e.dma_start(win[r * W:(r + 1) * W, q % 2, :, 0:TLEN - PITCH + W],
                                        src[ds(i * (4 * CH4) + q * CH4, CH4)].rearrange("c w n -> w c n")).then_inc(s_win[q % 2].handle, 16)

            def pack(e, copy, i, q):
                wait(e, s_win[q % 2], (i * 2 + q // 2 + 1) * (16 * ROWB))
                hold(sh, e, s_p, i * 4 + q + 1)
                copy(toe[:, q, :, :, :], win_m[:, q % 2, :, :, 0:W]).then_inc(s_toe[q].handle, 1)

            @block.gpsimd
            def _(e):
                with e.Fori(0, G3) as g:
                    with e.Fori(0, CB) as j:
                        pack(e, e.tensor_copy, g * CB + j, 1)
                    with e.Fori(0, B // 2) as b2:
                        for u in range(2):
                            wait(e, s_o, g * B + b2 * 2 + u + 1)
                            e.dma_start(yv[:, ds(g, 1), ds(b2 * 2 + u, 1), :], xo[:, u:u + 1, :].unsqueeze(1)).then_inc(s_y[u].handle, 16)
                        for u in range(2):
                            wait(e, s_y[u], (g * (B // 2) + b2 + 1) * 16)
                        e.sem_inc(s_yd.handle, 1)

            @block.scalar
            def _(e):
                with e.Fori(0, G3) as g:
                    wait(e, s_o, g * B)
                    e.dma_start(xs[:].unsqueeze(1), xv[:, ds(g, 1), :, :]).then_inc(s_x.handle, 16)
                    with e.Fori(0, B // 2) as b2:
                        for u in range(2):
                            n = g * B + b2 * 2 + u
                            wait(e, s_t, n + 1)
                            if u == 0:
                                e.copy(xT_m[:, :, ds(b2 * 2, 1), :].rearrange("p c o i -> p c (o i)"), p_t[0][:].rearrange("p i c -> p c i")).then_inc(s_te.handle, 1)
                    with e.Fori(0, CB) as j:
                        i = g * CB + j
                        pack(e, e.copy, i, 2)
                        wait(e, s_p, i * 4 + 2 + 4)
                        e.copy(yT[:, :, ds(j * 16, 8)], p_c[0][:].rearrange("p c n -> p n c")).then_inc(s_pe.handle, 1)

            @block.vector
            def _(e):
                with e.Fori(0, G3) as g:
                    with e.Fori(0, B // 2) as b2:
                        for u in range(2):
                            n = g * B + b2 * 2 + u
                            b = b2 * 2 + u
                            wait(e, s_x, g * 16 + 16)
                            gn = sh["gn"][:, ds(g, 1), ds(b, 1), :].rearrange("p g b s -> p (g b s)")
                            e.tensor_scalar(h[:, u, :], one(xs[:, ds(b, 1), :]), gn[:, 0:1], gn[:, 1:2], ALU.subtract, ALU.mult).then_inc(s_h.handle, 1)
                            wait(e, s_t, n + 1)
                            if u == 1:
                                e.tensor_copy(xT_m[:, :, ds(b, 1), :].rearrange("p c o i -> p c (o i)"), p_t[1][:].rearrange("p i c -> p c i")).then_inc(s_te.handle, 1)
                    with e.Fori(0, CB) as j:
                        i = g * CB + j
                        pack(e, e.tensor_copy, i, 0)
                        pack(e, e.tensor_copy, i, 3)
                        wait(e, s_p, i * 4 + 4 + 4)
                        e.tensor_copy(yT[:, :, ds(j * 16 + 8, 8)], p_c[1][:].rearrange("p c n -> p n c")).then_inc(s_pe.handle, 1)
                    for b in range(B):
                        wait(e, s_b, g * B + b + 1)
                        wait(e, s_yd, g * (B // 2) + b // 2)
                        e.scalar_tensor_tensor(xo[:, b % 2, :], p_t[b % 2][:].rearrange("p i w -> p (i w)").rearrange("p (i w) -> p i w", i=NT)[:, :, ::-1],
                                               sft[:, ds(g, 1)], xs[:, b, :].rearrange("p (i w) -> p i w", i=NT), ALU.add, ALU.add).then_inc(s_o.handle, 1)

            @block.tensor
            def _(e):
                e.sem_inc(s_p.handle, 4)
                for q in (2, 3):
                    e.sem_inc(s_toe[q].handle, 1)
                with e.Fori(0, G3) as g:
                    with e.Fori(0, B // 2) as b2:
                        for u in range(2):
                            n = g * B + b2 * 2 + u
                            wait(e, s_h, n + 1)
                            wait(e, s_te, g * B + b2 * 2)
                            for i in range(NT):
                                last = e.transpose(p_t[u][:, i, :], h[:, u, i * P:(i + 1) * P], sh["ident"][:])
                            last.then_inc(s_t.handle, 1)
                    with e.Fori(0, CB) as j:
                        i = g * CB + j
                        for q in range(4):
                            wait(e, s_toe[q], i + 1 + (q == 2 or q == 3))
                            if q == 0:
                                wait(e, s_te, g * B + B)
                            if q % 2 == 0:
                                wait(e, s_pe, i * 2)
                            for c in range(CH4):
                                ch = j * 16 + (q * CH4 + c)
                                for d in (0, -1, 1, -2, 2):
                                    lo, hi = max(0, -d), min(NT, NT - d)
                                    rows = ROWB * (d + 2)
                                    last = e.matmul(p_c[q // 2][:, (q % 2) * CH4 + c, :].rearrange("p (b i) -> p b i", b=B)[:, :, lo:hi],
                                                    toe[:, q, c, rows:rows + ROWB, :].rearrange("p r w -> p (r w)"),
                                                    xT_m[:, ds(ch, 1), :, lo + d:hi + d].rearrange("p o b i -> p (o b) i"),
                                                    start=(d == 0), stop=(d == 2), skip_group_check=True)
                            last.then_inc(s_p.handle, 1)
                    for b in range(B):
                        if b == 0:
                            wait(e, s_pe, (g + 1) * (2 * CB))
                        if b >= 2:
                            wait(e, s_o, g * B + b - 1)
                        for i in range(NT):
                            last = e.transpose(p_t[b % 2][:, i, :], yT[:, b * NT + i, :], sh["ident"][:])
                        last.then_inc(s_b.handle, 1)


KS = (3, 5, 7)
NEAR = ROWB
CHUNKS = NT + 2
FAR_STEP = 3 * ROWB
FAR = 3
TOP = FAR * FAR_STEP + 2 * ROWB
ROWS = 2 * TOP + H
PARTS = 2
SLOTS = {3: (0, 1, 2), 5: (0, 1, 2, 0, 1), 7: (0, 1, 2, 0, 1, 2, 1)}
NB = 3
BACK = 5
HID = C // 16


def last_use(K, kx):
    seq = SLOTS[K]
    return next(n for n in range(1, 2 * K) if seq[(kx - n) % K] == seq[kx])


def nth_use(K, kx):
    seq = SLOTS[K]
    return seq.count(seq[kx]), seq[:kx + 1].count(seq[kx])


def tiles_of(j):
    return max(0, j - 2), min(NT - 1, j) + 1


class Taps:

    def __init__(self, a, tag):
        self.s_stack, self.s_y = (a.sem(f"{tag}_{n}") for n in ("stack", "y"))
        self.s_hk, self.s_row, self.s_col, self.s_acc = (a.sem(f"{tag}_{n}") for n in ("hk", "row", "col", "act"))
        self.s_py = [a.sem(f"{tag}_py{i}") for i in range(NB)]
        self.s_px = [a.sem(f"{tag}_px{i}") for i in range(NB)]
        self.s_hi, self.s_rep, self.s_s, self.s_m = (a.sem(f"{tag}_{n}") for n in ("hi", "rep", "s", "m"))
        self.all = [self.s_stack, self.s_y, self.s_hk, self.s_row, self.s_col, self.s_acc, self.s_hi, self.s_rep, self.s_s, self.s_m, *self.s_py, *self.s_px]


ITEMS = 2 * CHUNKS


def credit(sh, block, tp):
    @block.gpsimd
    def _(e):
        e.sem_inc(tp.s_y.handle, 1)

    for engine in (block.sync, block.scalar):

        @engine
        def _(e):
            e.sem_inc(sh["tick"], 1)

    @block.vector
    def _(e):
        e.sem_inc(tp.s_stack.handle, BACK)
        e.sem_inc(tp.s_s.handle, BACK * ITEMS)

    @block.tensor
    def _(e):
        e.sem_inc(tp.s_rep.handle, BACK * ITEMS)
        e.sem_inc(tp.s_m.handle, BACK * ITEMS)


def deform(nc, sh, block, K, tp, bf, loop, zero_first):
    def near(T, n, per):
        return (T - n + 1 + BACK) * per

    @block.sync
    def _(e):
        for it, ky, row in loop(e):
            wait(e, tp.s_y, it * K + 1)
            for s in range(2):
                e.dma_start(bf["hk"][:, s, :, :], bf["hTd"][s, ds((row + ky) * W, CHUNKS * P), :].rearrange("(j p) c -> p j c", p=P)).then_inc(tp.s_hk.handle, 16)
            e.dma_start(bf["wk"][:, 0:K, :], bf["dw"][ds(ky * K, K), :].partition_broadcast(P)).then_inc(tp.s_hk.handle, 16)
            for kx in range(K):
                T, b, back = it * K + kx, SLOTS[K][kx], last_use(K, kx)
                m = (ky * K + kx) * 2
                wait(e, tp.s_stack, near(T, back, 1))
                for s in range(2):
                    e.dma_start(bf["py"][64 * s:64 * s + 64, b, :], bf["posd"][s, ds(m, 1), :].partition_broadcast(64).rearrange("p o n -> p (o n)")).then_inc(tp.s_py[b].handle, 16)
                wait(e, tp.s_s, near(T, back, ITEMS))
                e.dma_start(bf["px"][:, b, :, :], bf["posd"][:, ds(m + 1, 1), :].rearrange("s o n -> (s o) n").partition_broadcast(P)).then_inc(tp.s_px[b].handle, 16)

    @block.scalar
    def _(e):
        for it, ky, row in loop(e):
            for kx in range(K):
                b = SLOTS[K][kx]
                uses, nth = nth_use(K, kx)
                T = it * K + kx
                for buf, sem, by, done in ((bf["py"][:, b, :], tp.s_py[b], 32, tp.s_row),
                                           (bf["px"][:, b, :, :].rearrange("p s n -> p (s n)"), tp.s_px[b], 16, tp.s_col)):
                    wait(e, sem, (it * uses + nth) * by)
                    e.activation(buf, buf, ACT.Abs, bias=bf["minus"][:]).then_inc(tp.s_acc.handle, 1)
                    wait(e, tp.s_acc, T * 2 + (1 if done is tp.s_row else 2))
                    e.activation(buf, buf, ACT.Relu, bias=1.0, scale=-1.0).then_inc(done.handle, 1)

    @block.gpsimd
    def _(e):
        for it, ky, row in loop(e):
            for kx in range(K):
                b = SLOTS[K][kx]
                T = it * K + kx
                if kx == 0:
                    wait(e, tp.s_hk, (it + 1) * 48)
                hold(sh, e, tp.s_m, near(T, last_use(K, kx), ITEMS))
                e.tensor_tensor(bf["y"][:, b, :, :], bf["hk"][:].rearrange("p s j c -> p (s j) c"),
                                bf["wk"][:, kx, :].unsqueeze(1).broadcast_to([P, ITEMS, P]), ALU.mult).then_inc(tp.s_y.handle, 1)

    @block.vector
    def _(e):
        for it, ky, row in loop(e):
            def split(kx):
                T, b = it * K + kx, SLOTS[K][kx]
                wait(e, tp.s_row, T + 1)
                e.tensor_copy(bf["hi"][:], bf["py"][:, b, :]).then_inc(tp.s_hi.handle, 1)
                wait(e, tp.s_hi, T + 1)
                wait(e, tp.s_rep, near(T, last_use(K, kx), ITEMS))
                e.scalar_tensor_tensor(bf["stack"][:, b, :], bf["hi"][:], bf["low"][:], bf["py"][:, b, :], ALU.mult, ALU.subtract).then_inc(tp.s_stack.handle, 1)

            split(0)
            for kx in range(K):
                T, b = it * K + kx, SLOTS[K][kx]
                for i in range(ITEMS):
                    s, j = divmod(i, CHUNKS)
                    lo, hi = tiles_of(j)
                    n = (hi - lo) * P
                    if i == 0:
                        wait(e, tp.s_col, T + 1)
                    if i == CHUNKS and kx + 1 < K:
                        split(kx + 1)
                    wait(e, tp.s_rep, (T + BACK) * ITEMS + i + 1)
                    wait(e, tp.s_m, (T + BACK) * ITEMS + i + 1 - bf["NS"])
                    e.tensor_tensor(bf["S"][:, i % bf["NS"], 0:n], bf["p_r"][i % 4][:, 0:n],
                                    bf["px"][:, b, s, lo * P:hi * P], ALU.mult).then_inc(tp.s_s.handle, 1)

    @block.tensor
    def _(e):
        if zero_first:
            for s in range(2):
                for n in range(2):
                    e.matmul(bf["acc"][s][:, n, :], bf["zero"][:, 0:P], bf["zero"][:], start=True, stop=False, skip_group_check=True)
        for it, ky, row in loop(e):
            def spread(k):
                kx, i = divmod(k, ITEMS)
                s, j = divmod(i, CHUNKS)
                T, b = it * K + kx, SLOTS[K][kx]
                lo, hi = tiles_of(j)
                if i == 0:
                    wait(e, tp.s_stack, T + 1 + BACK)
                wait(e, tp.s_s, (T + BACK) * ITEMS + i + 1 - 4)
                e.matmul(bf["p_r"][i % 4][:, 0:(hi - lo) * P], bf["E"][:, s, ds((row + ky + j * ROWB) * W, P)],
                         bf["stack"][:, b, lo * P:hi * P], start=True, stop=True).then_inc(tp.s_rep.handle, 1)

            def product(k):
                kx, i = divmod(k, ITEMS)
                s, j = divmod(i, CHUNKS)
                T, b = it * K + kx, SLOTS[K][kx]
                lo, hi = tiles_of(j)
                if i == 0:
                    wait(e, tp.s_y, T + 2)
                wait(e, tp.s_s, (T + BACK) * ITEMS + i + 1)
                for n in range(2):
                    a, z = max(lo, n * NT // 2), min(hi, (n + 1) * NT // 2)
                    if a < z:
                        last = e.matmul(bf["acc"][s][:, n, (a - n * NT // 2) * P:(z - n * NT // 2) * P], bf["y"][:, b, i, :],
                                        bf["S"][:, i % bf["NS"], (a - lo) * P:(z - lo) * P], start=False, stop=False, skip_group_check=True)
                last.then_inc(tp.s_m.handle, 1)

            AHEAD = 3
            for k in range(AHEAD):
                spread(k)
            for k in range(K * ITEMS):
                if k + AHEAD < K * ITEMS:
                    spread(k + AHEAD)
                product(k)


def layer1(nc, sh, x, t, y):
    xv = x.rearrange("b (g p) n -> p b g n", p=P)
    yv = y.rearrange("b (g p) n -> p b g n", p=P)
    M7 = 2 * KS[-1] ** 2
    posd = nc.dram_tensor("sampling_positions", [2, M7, N], F32).ap()
    hTd = nc.dram_tensor("turned_image", [2, ROWS * W, P], F32).ap()
    PADT = TOP * W // P
    norm_params(nc, sh, "n1")
    with Arena(nc, "b") as a:
        E = a.sb("E", [P, 2, ROWS * W], F16)
        zero = a.sb("zero", [P, HALF], F16)
        minus = a.sb("minus", [P, 1])
        low = a.sb("low", [P, 1])
        ymask = a.sb("ymask", [M7, 1])
        pw = a.sb("pw", [P, G3, P])
        pb = a.sb("pb", [P, G3])
        ob = a.sb("ob", [M7, G3])
        f1 = a.sb("f1", [P, G3, HID])
        f2 = a.sb("f2", [HID, G3, P])
        dcv = a.sb("dcv", [P, G3, 2, N])
        far = a.sb("far", [1, 1 + 2 * FAR * KS[-1]], I32)
        ps = [a.ps(f"p{i}", [P, 2, HALF]) for i in range(4)]
        acc = ps[0:2]
        p_r = [ps[2 + i // 2][:, i % 2, :] for i in range(4)]
        taps = [Taps(a, f"t{g}") for g in range(G3)]
        tfar = Taps(a, "far")
        s_i, s_iv, s_hv, s_iz = (a.sem(n) for n in ("i", "iv", "hv", "iz"))
        with Arena(nc, "bi") as ai, nc.Block() as block:
            ef = ai.sb("ef", [P, 2, H * W])
            zt = ai.sb("zt", [P, PADT, P])

            @block.sync
            def _(e):
                e.dma_start(ef[:], t["b_E"].rearrange("s p n -> p s n")).then_inc(s_i.handle, 16)
                for dst, src in ((minus[:], t["b_minus"]), (low[:], t["b_low"]), (ymask[:], t["b_ymask"]),
                                 (pw[:], t["b_pw"].rearrange("g c o -> c g o")), (f1[:], t["b_f1"].rearrange("g c o -> c g o")), (f2[:], t["b_f2"]),
                                 (pb[:], t["b_pb"]), (ob[:], t["b_ob"])):
                    e.dma_start(dst, src, allow_slow_non_contiguous=True).then_inc(s_i.handle, 16)
                wait(e, s_iv, 2)
                for s in range(2):
                    for r0 in (0, (TOP + H) * W):
                        e.dma_start(hTd[s, r0:r0 + TOP * W, :].rearrange("(j p) c -> p j c", p=P), zt[:]).then_inc(s_iz.handle, 16)
                wait(e, s_iz, 16 * 4)
                wait(e, s_i, 16 * 9)

            @block.gpsimd
            def _(e):
                e.memset(zt[:], 0.0).then_inc(s_iv.handle, 1)
                e.memset(zero[:], 0.0).then_inc(s_iv.handle, 1)

            @block.vector
            def _(e):
                e.memset(E[:], 0.0).then_inc(s_hv.handle, 1)
                wait(e, s_hv, 1)
                wait(e, s_i, 16 * 9)
                e.tensor_copy(E[:, :, TOP * W:(TOP + H) * W], ef[:]).then_inc(s_hv.handle, 1)
                wait(e, s_hv, 2)

        for tp in taps:
            with nc.Block() as block:
                credit(sh, block, tp)

        SA = {n: [(a.sem if n in ("x", "w", "g", "st") else a.loop_sem)(f"{n}{g}") for g in range(G3)] for n in ("x", "w", "g", "h", "hp", "tr", "cv", "po", "tt", "fl", "st", "ev", "pw", "dc")}
        SC = {n: (a.sem if n in "xy" else a.loop_sem)(f"c{n}") for n in ("x", "r", "p", "a", "o", "y")}
        a.open()
        with nc.Fori(0, B // 2) as pr:
            for g, K in enumerate(KS):
                M, R = 2 * K * K, K // 2
                with Arena(nc, f"o{g}") as ao, nc.Block() as block:
                    PW = W + 2 * R
                    ow = ao.sb("ow", [P, K * K, M])
                    grid = ao.sb("grid", [M, N])
                    xs = ao.sb("xs", [P, 2, N])
                    h = ao.sb("h", [P, 2, N])
                    hp = ao.sb("hp", [P, 2, PW, PW])
                    hT = ao.sb("hT", [P, 2, NT, P])
                    pos = ao.sb("pos", [M, 2, N])
                    off = ao.sb("off", [M, 2, N])
                    mx = ao.sb("mx", [M, 2, 2])
                    mxm = ao.sb("mxm", [M, 2])
                    fm = ao.sb("fm", [1, 2, K])
                    S = {n: v[g] for n, v in SA.items()}

                    @block.sync
                    def _(e):
                        e.dma_start(xs[:], xv[:, ds(pr * 2, 2), g, :]).then_inc(S["x"].handle, 16)
                        e.dma_start(ow[:], t[f"b_ow{g}"]).then_inc(S["w"].handle, 16)
                        e.dma_start(grid[:], t[f"b_grid{g}"]).then_inc(S["g"].handle, 16)
                        wait(e, S["tr"], pr * 3 + 3)
                        for s in range(2):
                            e.dma_start(hTd[s, TOP * W:(TOP + H) * W, :].rearrange("(j p) c -> p j c", p=P), hT[:, s, :, :]).then_inc(S["st"].handle, 16)
                        wait(e, S["po"], pr * 8 + 8)
                        e.dma_start(posd[:, 0:M, :].rearrange("s m n -> m s n"), pos[:]).then_inc(S["st"].handle, 16)
                        hold(sh, e, S["st"], (pr + 1) * 48)

                    @block.gpsimd
                    def _(e):
                        e.memset(hp[:], 0.0).then_inc(S["hp"].handle, 1)

                    @block.scalar
                    def _(e):
                        wait(e, S["hp"], pr * 2 + 1)
                        wait(e, S["h"], pr * 2 + 2)
                        for s in range(2):
                            last = e.copy(hp[:, s, R:R + H, R:R + W], h[:, s, :].rearrange("p (a b) -> p a b", a=H))
                        last.then_inc(S["hp"].handle, 1)
                        wait(e, S["tr"], pr * 3 + 1)
                        for s in range(2):
                            e.copy(hT[:, s, :, :], ps[2 + s][:].rearrange("p a (b c) -> p (a b) c", c=P)).then_inc(S["tr"].handle, 1)

                    @block.vector
                    def _(e):
                        wait(e, S["x"], (pr + 1) * 16)
                        for s in range(2):
                            gn = sh["gn"][:, g, ds(pr * 2 + s, 1), :].rearrange("p b s -> p (b s)")
                            e.tensor_scalar(h[:, s, :], xs[:, s, :], gn[:, 0:1], gn[:, 1:2], ALU.subtract, ALU.mult).then_inc(S["h"].handle, 1)
                        wait(e, S["g"], (pr + 1) * 16)
                        for s in range(2):
                            for n in range(2):
                                wait(e, S["cv"], pr * 4 + s * 2 + n + 1)
                                part = slice(n * HALF, (n + 1) * HALF)
                                e.tensor_scalar(off[:, s, part], acc[s][0:M, n, :], ob[0:M, g:g + 1], None, ALU.add).then_inc(S["po"].handle, 1)
                        wait(e, S["po"], pr * 8 + 4)
                        e.tensor_reduce(mx[:, 0, :], off[:], AX, ALU.min, negate=True).then_inc(S["po"].handle, 1)
                        e.tensor_reduce(mx[:, 1, :], off[:], AX, ALU.max).then_inc(S["po"].handle, 1)
                        for s in range(2):
                            e.tensor_tensor(pos[:, s, :], off[:, s, :], grid[:], ALU.add).then_inc(S["po"].handle, 1)
                        wait(e, S["po"], pr * 8 + 8)
                        link = Chain(sh, e, S["fl"], pr, 5)
                        link(e.tensor_reduce(mxm[:], mx[:], AX, ALU.max))
                        link(e.tensor_scalar(mxm[:], mxm[:], ymask[0:M, :], None, ALU.mult))
                        wait(e, S["tt"], pr + 1)
                        for way in range(2):
                            last = e.tensor_reduce(fm[:, way, :], ps[2][0:1, way, 0:M].rearrange("p (ky m) -> p ky m", ky=K), AX, ALU.max)
                        link(last)
                        for f in range(2 * FAR):
                            steps = FAR - 1 - f if f < FAR else f - FAR
                            last = e.tensor_scalar(far[:, 1 + f * KS[-1]:1 + f * KS[-1] + K], fm[:, int(f >= FAR), :],
                                                   float(NEAR + steps * FAR_STEP), None, ALU.is_gt)
                        link(last)
                        n = 1 + (FAR - 1) * KS[-1]
                        link(e.tensor_reduce(far[:, 0:1], far[:, n:n + 2 * KS[-1]].rearrange("p (f k) -> p f k", f=2)[:, :, 0:K],
                                             mybir.AxisListType.XY, ALU.max))
                        link.end()

                    @block.tensor
                    def _(e):
                        wait(e, S["h"], pr * 2 + 2)
                        for s in range(2):
                            for i in range(NT):
                                last = e.transpose(ps[2 + s][:, i // 4, i % 4 * P:(i % 4 + 1) * P], h[:, s, i * P:(i + 1) * P], sh["ident"][:])
                        last.then_inc(S["tr"].handle, 1)
                        wait(e, S["w"], (pr + 1) * 16)
                        wait(e, S["hp"], pr * 2 + 2)
                        for s in range(2):
                            for n in range(2):
                                for k in range(K * K):
                                    dy, dx = divmod(k, K)
                                    last = e.matmul(acc[s][0:M, n, :].rearrange("p (a b) -> p a b", b=W), ow[:, k, :],
                                                    hp[:, s, n * 16 + dy:n * 16 + dy + 16, dx:dx + W], start=(k == 0), stop=(k == K * K - 1))
                                last.then_inc(S["cv"].handle, 1)
                        wait(e, S["tr"], pr * 3 + 3)
                        hold(sh, e, S["fl"], pr * 5 + 2)
                        for way in range(2):
                            last = e.matmul(ps[2][0:1, way, 0:M], mxm[:, way:way + 1], sh["ident"][0:M, 0:M], start=True, stop=True)
                        last.then_inc(S["tt"].handle, 1)

                with Arena(nc, f"m{g}") as am:
                    bf = {"hk": am.sb("hk", [P, 2, CHUNKS, P]), "wk": am.sb("wk", [P, K, P]), "py": am.sb("py", [P, NB, N]),
                          "px": am.sb("px", [P, NB, 2, N]), "hi": am.sb("hi", [P, N], F16), "stack": am.sb("stack", [P, NB, N], F16),
                          "y": am.sb("y", [P, NB, ITEMS, P]), "NS": 5, "S": am.sb("S", [P, 5, 3 * P]),
                          "hTd": hTd, "posd": posd, "dw": t[f"b_dw{g}"], "minus": minus, "low": low, "zero": zero, "E": E,
                          "acc": acc, "p_r": p_r}
                    smp = am.sb("smp", [P, 2, N])
                    first = TOP - ROWB - R

                    def near_loop(e):
                        with e.Fori(0, K) as ky:
                            yield pr * K + ky, ky, first

                    with nc.Block() as block:
                        deform(nc, sh, block, K, taps[g], bf, near_loop, True)
                    with nc.If(nc.values_load(far[0:1, 0:1], min_val=0, max_val=1) > 0):
                        with nc.Fori(0, 2 * FAR) as f, nc.Fori(0, K) as ky:
                            which = nc.values_load(far[0:1, ds(1 + f * KS[-1] + ky, 1)], min_val=0, max_val=1)
                            row = first + f * FAR_STEP + f // FAR * FAR_STEP - FAR * FAR_STEP
                            with nc.If(which > 0):
                                with nc.Block() as block:
                                    credit(sh, block, tfar)
                                with nc.Block() as block:
                                    deform(nc, sh, block, K, tfar, bf, lambda e: [(0, ky, row)], False)
                                clear(nc, [sem.handle for sem in tfar.all])
                    with nc.Block() as block:
                        S = {n: v[g] for n, v in SA.items()}

                        @block.scalar
                        def _(e):
                            for s in range(2):
                                e.copy(smp[:, s, :], acc[s][:].rearrange("p a n -> p (a n)")).then_inc(S["ev"].handle, 1)
                            for s in range(2):
                                wait(e, S["pw"], pr * 2 + s + 1)
                                e.activation(dcv[:, g, s, :], ps[2 + s][:].rearrange("p a n -> p (a n)"), ACT.Identity, bias=pb[:, g:g + 1]).then_inc(S["dc"].handle, 1)

                        @block.tensor
                        def _(e):
                            for s in range(2):
                                wait(e, S["ev"], pr * 2 + s + 1)
                                for n in range(2):
                                    last = e.matmul(ps[2 + s][:, n, :], pw[:, g, :], smp[:, s, n * HALF:(n + 1) * HALF], start=True, stop=True)
                                last.then_inc(S["pw"].handle, 1)

            with Arena(nc, "se") as ae, nc.Block() as block:
                xs = ae.sb("xs", [P, 2, G3, N])
                pool = ae.sb("pool", [P, G3, 2, 2])
                hid = ae.sb("hid", [HID, 4])
                z = ae.sb("z", [P, G3, 2])
                zz = ae.sb("zz", [P, G3, 4])

                @block.sync
                def _(e):
                    e.dma_start(xs[:], xv[:, ds(pr * 2, 2), :, :]).then_inc(SC["x"].handle, 16)
                    wait(e, SC["o"], pr * 7 + 6)
                    e.dma_start(yv[:, ds(pr * 2, 2), :, :], xs[:]).then_inc(SC["y"].handle, 16)
                    hold(sh, e, SC["y"], (pr + 1) * 16)

                @block.vector
                def _(e):
                    link = Chain(sh, e, SC["r"], pr, 7)
                    for g in range(G3):
                        e.tensor_reduce(pool[:, g, 0, :], dcv[:, g, :, :], AX, ALU.add)
                        last = e.tensor_reduce(pool[:, g, 1, :], dcv[:, g, :, :], AX, ALU.max)
                    link(last)
                    link(e.tensor_scalar(pool[:, :, 0, :], pool[:, :, 0, :], 1.0 / N, None, ALU.mult))
                    wait(e, SC["p"], pr * 2 + 1)
                    link(e.tensor_scalar(hid[:], ps[2][0:HID, 0, 0:4], 0.0, None, ALU.max))
                    wait(e, SC["p"], pr * 2 + 2)
                    link(e.tensor_copy(zz[:], ps[3][:, 0, 0:4 * G3].rearrange("p (g f) -> p g f", f=4)))
                    link(e.tensor_tensor(z[:], zz[:, :, 0:2], zz[:, :, 2:4], ALU.add))
                    wait(e, SC["a"], pr + 1)
                    link(e.tensor_scalar(z[:], z[:], 1.0, None, ALU.add))
                    link(e.reciprocal(z[:], z[:]))
                    wait(e, SC["x"], (pr + 1) * 16)
                    for g in range(G3):
                        for s in range(2):
                            e.scalar_tensor_tensor(xs[:, s, g, :], dcv[:, g, s, :], z[:, g, s:s + 1], xs[:, s, g, :], ALU.mult, ALU.add).then_inc(SC["o"].handle, 1)
                    wait(e, SC["o"], pr * 7 + 6)
                    for g in range(G3):
                        for s in range(2):
                            for n in range(2):
                                last = e.bn_stats(sh["stat"][:, g, ds(pr * 2 + s, 1), n, :].rearrange("p o s -> p (o s)"), xs[:, s, g, n * HALF:(n + 1) * HALF])
                    last.then_inc(SC["o"].handle, 1)
                    hold(sh, e, SC["o"], pr * 7 + 7)
                    link.end()

                @block.scalar
                def _(e):
                    wait(e, SC["r"], pr * 7 + 5)
                    e.activation(z[:], z[:], ACT.Exp, scale=-1.0).then_inc(SC["a"].handle, 1)

                @block.tensor
                def _(e):
                    hold(sh, e, SC["r"], pr * 7 + 2)
                    for g in range(G3):
                        last = e.matmul(ps[2][0:HID, 0, 0:4], f1[:, g, :], pool[:, g, :, :].rearrange("p a s -> p (a s)"), start=(g == 0), stop=(g == G3 - 1))
                    last.then_inc(SC["p"].handle, 1)
                    hold(sh, e, SC["r"], pr * 7 + 3)
                    for g in range(G3):
                        last = e.matmul(ps[3][:, 0, 4 * g:4 * g + 4], f2[:, g, :], hid[:], start=True, stop=True)
                    last.then_inc(SC["p"].handle, 1)


def program(nc, t):
    with ExitStack() as ctx:
        def shared(name, shape, dt=F32):
            return ctx.enter_context(nc.sbuf_tensor(name, shape, dt))

        sh = {
            "tick": ctx.enter_context(nc.semaphore("tick")),
            "ident": shared("ident", [P, P]),
            "gmat": shared("gmat", [P, G3, GROUPS]),
            "gmatT": shared("gmatT", [GROUPS, G3, P]),
            "stat": shared("stat", [P, G3, B, 2, 6]),
            "gn": shared("gn", [P, G3, B, 2]),
        }
        load_shared(nc, sh, t)
        x1, x2, x3 = (nc.dram_tensor(f"x{i}", [B, C, N], F32).ap() for i in (1, 2, 3))
        layer0(nc, sh, t["x"], t["a_wqk"], t["a_wv"], t["a_wp"], t["a_bp"], x1)
        layer1(nc, sh, x1, t, x2)
        layer2(nc, sh, x2, t["c_wqk"], t["c_wvT"], t["c_wo"], t["c_temp"], t["c_bo"], x3)
        layer3(nc, sh, x3, [t[f"d_w{k}"] for k in range(CONVS)], t["d_bn"], t["out"])


def laid_out(i, np):
    f = np.float32
    t = {"x": i["x"].reshape(B, C, N)}
    t["ident"] = np.eye(P, dtype=f)
    member = (np.arange(C)[:, None] // CPG == np.arange(GROUPS)[None, :]).astype(f)
    t["gmat"] = member.reshape(G3, P, GROUPS)
    t["gmatT"] = member.T.reshape(GROUPS, G3, P)
    w = i["L0_conv_w_qkv"].T.reshape(C, 3, PAIRS, 2, D)
    qk = np.zeros((PAIRS, C, 2, 2, 64), f)
    qk[..., 0:D] = w[:, 0:2].transpose(2, 0, 1, 3, 4)
    t["a_wqk"] = qk.reshape(PAIRS, C, 2, 128)[..., 0:TP]
    t["a_wv"] = w[:, 2].reshape(C, C)
    wp = np.zeros((PAIRS, 2, 64, C), f)
    wp[:, :, 0:D] = i["L0_conv_w_proj"].T.reshape(PAIRS, 2, D, C)
    t["a_wp"] = wp.reshape(PAIRS, 128, C)[:, 0:TP].transpose(1, 0, 2)
    t["a_bp"] = i["L0_conv_b_proj"]
    spread = np.zeros((2, 2, PARTS, H, H, W), f)
    for r in range(H):
        for u in range(2):
            spread[u, u, :, r, r, :] = -1.0
    t["b_E"] = spread.reshape(2, P, H * W)
    t["b_minus"] = -(np.arange(P) % H).astype(f)[:, None]
    t["b_low"] = (np.arange(P) // H % PARTS).astype(f)[:, None]
    M7 = 2 * KS[-1] ** 2
    t["b_ymask"] = ((np.arange(M7) + 1) % 2).astype(f)[:, None]
    t["b_pw"] = np.stack([i[f"L1_conv_pw_w{K}"].reshape(P, P).T for K in KS])
    t["b_pb"] = np.stack([i[f"L1_conv_pw_b{K}"] for K in KS], 1)
    ob = np.zeros((M7, G3), f)
    for g, K in enumerate(KS):
        M, R = 2 * K * K, K // 2
        ob[0:M, g] = i[f"L1_conv_offset_b{K}"]
        t[f"b_ow{g}"] = i[f"L1_conv_offset_w{K}"].transpose(1, 2, 3, 0).reshape(P, K * K, M)
        t[f"b_dw{g}"] = i[f"L1_conv_dw_w{K}"].reshape(P, K * K).T
        grid = np.zeros((K, K, 2, H, W), f)
        grid[:, :, 0] = (np.arange(K)[:, None, None, None] - R + np.arange(H)[None, None, :, None])
        grid[:, :, 1] = (np.arange(K)[None, :, None, None] - R + np.arange(W)[None, None, None, :])
        t[f"b_grid{g}"] = grid.reshape(M, N)
    t["b_ob"] = ob
    t["b_f1"] = i["L1_conv_fc1_w"].reshape(HID, G3, P).transpose(1, 2, 0)
    t["b_f2"] = i["L1_conv_fc2_w"].reshape(G3, P, HID).transpose(2, 0, 1)
    w = i["L2_conv_w_qkv"].reshape(C, 3, C)
    t["c_wqk"] = w[:, 1::-1]
    wv = np.zeros((PAIRS, 2, 64, C), f)
    wv[:, :, 0:D] = w[:, 2].T.reshape(PAIRS, 2, D, C)
    t["c_wvT"] = wv.reshape(PAIRS, 128, C)[:, 0:TP].transpose(1, 0, 2)
    t["c_wo"] = i["L2_conv_w_out"].reshape(HEADS, D, C).transpose(1, 0, 2)
    t["c_temp"] = i["L2_conv_temperature"].reshape(HEADS)
    t["c_bo"] = i["L2_conv_b_out"]
    for k, name in enumerate(("lk_w", "w5", "w7a", "w7b", "w3a", "w3b", "w3c")):
        t[f"d_w{k}"] = i[f"L3_conv_{name}"].reshape(C, -1)
    t["d_bn"] = np.concatenate([i["L3_conv_obn"][None], i["L3_conv_br_bn"]]).transpose(2, 0, 1)
    return t


def kernel(**inputs):
    import numpy as np
    import concourse.bacc as bacc
    from concourse.bass_utils import run_bass_kernel_spmd as run

    nc = bacc.Bacc("TRN2", target_bir_lowering=False, num_devices=1)
    arrays, t = {}, {}
    for name, a in laid_out({k: np.asarray(v) for k, v in inputs.items()}, np).items():
        a = np.ascontiguousarray(a)
        arrays[f"in_{name}"] = a
        t[name] = nc.dram_tensor(f"in_{name}", a.shape, mybir.dt.from_np(a.dtype), kind="ExternalInput").ap()
    t["out"] = nc.dram_tensor("out_dram", [B, C, N], F32, kind="ExternalOutput").ap()
    program(nc, t)
    r = run(nc, [arrays], core_ids=[0])
    return r.results[0]["out_dram"].reshape(B, C, H, W)
```

```python
from contextlib import ExitStack

import concourse.bass as bass
from concourse import mybir
from concourse.alu_op_type import AluOpType as ALU

F32 = mybir.dt.float32
F16 = mybir.dt.float16
BF16 = mybir.dt.bfloat16
I32 = mybir.dt.int32
ACT = mybir.ActivationFunctionType
AX = mybir.AxisListType.X

P = 128
B = 8
C = 384
G3 = C // P
H = W = 32
N = H * W
HALF = N // 2
GROUPS = 32
CPG = C // GROUPS
HEADS = 8
D = C // HEADS
PAIRS = HEADS // 2
TP = 64 + D
NT = N // P
ROWB = P // W


def ds(start, size):
    return bass.DynSlice(start, size)


class Arena:

    def __init__(self, nc, tag):
        self.nc, self.tag, self.stack, self.sems = nc, tag, ExitStack(), []
        self.ahead = []

    def __enter__(self):
        self.stack.__enter__()
        return self

    def __exit__(self, *e):
        if self.sems and e[0] is None:
            clear(self.nc, self.sems)
        return self.stack.__exit__(*e)

    def sb(self, name, shape, dt=F32):
        return self.stack.enter_context(self.nc.sbuf_tensor(f"{self.tag}_{name}", shape, dt))

    def ps(self, name, shape, dt=F32):
        return self.stack.enter_context(self.nc.psum_tensor(f"{self.tag}_{name}", shape, dt))

    def sem(self, name):
        self.sems.append(self.stack.enter_context(self.nc.semaphore(f"{self.tag}_{name}")))
        return Sem(self.sems[-1], 0)

    def loop_sem(self, name):
        sem = Sem(self.sem(name).handle, 1)
        self.ahead.append(sem.handle)
        return sem

    def open(self):
        with self.nc.Block() as block:

            @block.sync
            def _(e):
                for sem in self.ahead:
                    e.sem_inc(sem, 1)


class Sem:

    def __init__(self, handle, start):
        self.handle, self.start = handle, start


def wait(e, sem, count):
    e.wait_ge(sem.handle, count + sem.start)


def clear(nc, sems):
    with nc.Block() as block:

        @block.sync
        def _(e):
            for sem in sems:
                e.sem_clear(sem)


def at(i, per, k):
    return i * per + max(k, 0)


def hold(sh, e, sem, value):
    wait(e, sem, value)
    e.sem_inc(sh["tick"], 1)


class Chain:

    def __init__(self, sh, eng, sem, i=None, per=0):
        self.sh = sh
        self.eng, self.sem, self.i, self.per, self.n = eng, sem, i, per, 0

    def __call__(self, ins):
        ins.then_inc(self.sem.handle, 1)
        self.n += 1
        if self.i is None:
            wait(self.eng, self.sem, self.n)
        else:
            hold(self.sh, self.eng, self.sem, self.i * self.per + self.n)

    def end(self):
        assert self.i is None or self.n == self.per, (self.n, self.per)


def load_shared(nc, sh, consts):
    with Arena(nc, "ld") as a, nc.Block() as block:
        s = a.sem("s")

        @block.sync
        def _(e):
            e.dma_start(sh["ident"][:], consts["ident"]).then_inc(s.handle, 16)
            e.dma_start(sh["gmat"][:], consts["gmat"].rearrange("g p n -> p g n")).then_inc(s.handle, 16)
            e.dma_start(sh["gmatT"][:], consts["gmatT"]).then_inc(s.handle, 16)
            wait(e, s, 48)


def norm_params(nc, sh, tag):
    with Arena(nc, tag) as a:
        mv = a.sb("mv", [P, G3, B, 2])
        sq = a.sb("sq", [P, G3, B])
        grp = a.sb("grp", [GROUPS, B, 2])
        gsq = a.sb("gsq", [GROUPS, B])
        bank = a.ps("bank", [P, 1 + G3, B * 2])
        p_grp = bank[0:GROUPS, 0, :]
        p_ch = bank[:, 1:1 + G3, :]
        s_d, s_dc, s_pe, s_a = a.sem("d"), a.sem("dc"), a.sem("pe"), a.sem("a")
        with nc.Block() as block:

            @block.vector
            def _(e):
                link = Chain(sh, e, s_dc)
                for g in range(G3):
                    for b in range(B):
                        last = e.bn_aggr(mv[:, g, b, :], sh["stat"][:, g, b, :, :].rearrange("p a s -> p (a s)"))
                link(last)
                link(e.tensor_tensor(sq[:], mv[:, :, :, 0], mv[:, :, :, 0], ALU.mult))
                e.tensor_tensor(mv[:, :, :, 1], mv[:, :, :, 1], sq[:], ALU.add).then_inc(s_d.handle, 1)
                wait(e, s_pe, 1)
                link(e.tensor_scalar(grp[:].rearrange("p b s -> p (b s)"), p_grp, 1.0 / CPG, None, ALU.mult))
                link(e.tensor_tensor(gsq[:], grp[:, :, 0], grp[:, :, 0], ALU.mult))
                link(e.tensor_tensor(gsq[:], grp[:, :, 1], gsq[:], ALU.subtract))
                e.tensor_scalar(gsq[:], gsq[:], 1e-5, None, ALU.add).then_inc(s_d.handle, 1)
                wait(e, s_a, 1)
                e.reciprocal(grp[:, :, 1], gsq[:]).then_inc(s_d.handle, 1)
                wait(e, s_pe, 2)
                e.tensor_copy(sh["gn"][:].rearrange("p g b s -> p g (b s)"), p_ch).then_inc(s_d.handle, 1)
                wait(e, s_d, 4)

            @block.scalar
            def _(e):
                wait(e, s_d, 2)
                e.activation(gsq[:], gsq[:], ACT.Sqrt).then_inc(s_a.handle, 1)

            @block.tensor
            def _(e):
                wait(e, s_d, 1)
                for g in range(G3):
                    last = e.matmul(p_grp, sh["gmat"][:, g, :], mv[:, g, :, :].rearrange("p b s -> p (b s)"),
                                    start=(g == 0), stop=(g == G3 - 1))
                last.then_inc(s_pe.handle, 1)
                wait(e, s_d, 3)
                for g in range(G3):
                    last = e.matmul(p_ch[:, g, :], sh["gmatT"][:, g, :], grp[:].rearrange("p b s -> p (b s)"),
                                    start=True, stop=True)
                last.then_inc(s_pe.handle, 1)


def input_stats(nc, sh, x):
    with Arena(nc, "i") as a:
        xs = a.sb("xs", [P, B, G3, N])
        s_x = [a.sem(f"x{b}") for b in range(B)]
        s_st = a.sem("st")
        with nc.Block() as block:

            @block.sync
            def _(e):
                for b in range(B):
                    e.dma_start(xs[:, b, :, :], x.rearrange("b (g p) n -> p b g n", p=P)[:, b, :, :]).then_inc(s_x[b].handle, 16)

            @block.vector
            def _(e):
                for b in range(B):
                    wait(e, s_x[b], 16)
                    for g in range(G3):
                        for n in range(2):
                            last = e.bn_stats(sh["stat"][:, g, b, n, :], xs[:, b, g, n * HALF:(n + 1) * HALF])
                last.then_inc(s_st.handle, 1)
                wait(e, s_st, 1)


def layer0(nc, sh, x, w_qk, w_v, w_proj, b_proj, y):
    input_stats(nc, sh, x)
    norm_params(nc, sh, "n0")
    xv = x.rearrange("b (g p) n -> p b g n", p=P)
    yv = y.rearrange("b (g p) n -> p b g n", p=P)
    TH = NT
    TB = HEADS * TH
    SCALE = float(D) ** -0.5
    RING = 4
    UNITS = 6
    ROWS_OF = (0, 64)
    with Arena(nc, "a") as a:
        xh = a.sb("xh", [P, G3, N])
        xr = a.sb("xr", [P, G3, N])
        h = a.sb("h", [P, G3, N])
        wqk = a.sb("wqk", [P, PAIRS, G3, 2, TP])
        wv = a.sb("wv", [P, G3, C])
        wp = a.sb("wp", [TP, PAIRS, C])
        bp = a.sb("bp", [P, G3])
        idh = a.sb("idh", [P, P], F16)
        q = a.sb("q", [TP, 2, 2, N], F16)
        kh = a.sb("kh", [TP, 2, 2, N], F16)
        kl = a.sb("kl", [TP, 2, 2, N], F16)
        v = a.sb("v", [P, 2, NT, 2, TP], F16)
        att = a.sb("att", [P, RING, N])
        ah = a.sb("ah", [P, RING, N], F16)
        al = a.sb("al", [P, RING, N], F16)
        attT = a.sb("attT", [P, 2, 2 * NT, HALF], F16)
        nmax = a.sb("nmax", [P, RING])
        den = a.sb("den", [P, RING])
        rden = a.sb("rden", [P, RING])
        oh = a.sb("oh", [TP, HALF])
        o = a.sb("o", [TP, PAIRS, N])
        p_s = [a.ps(f"p_s{i}", [P, 2, HALF]) for i in range(2)]
        p_t = a.ps("p_t", [P, 2 * NT, P], F16)
        p_o = a.ps("p_o", [P, HALF])
        p_j = a.ps("p_j", [P, HALF])
        s_w, s_xh, s_xr, s_y = (a.sem(n) for n in ("w", "xh", "xr", "y"))
        s_z, s_h, s_pj, s_ja, s_jv = (a.loop_sem(n) for n in ("z", "h", "pj", "ja", "jv"))
        s_s, s_m, s_e, s_ri, s_hi, s_lo, s_t, s_ta, s_tv = (a.loop_sem(n) for n in ("s", "m", "e", "ri", "hi", "lo", "t", "ta", "tv"))
        s_o, s_oa, s_on, s_f, s_fo, s_st, s_yd = (a.loop_sem(n) for n in ("o", "oa", "on", "f", "fo", "st", "yd"))
        a.open()
        JA = (2, 2, 4, 4, 1, 1)
        PJA = sum(JA)

        with nc.Block() as block:

            @block.sync
            def _(e):
                e.dma_start(wqk[:], w_qk.rearrange("t (g p) s n -> p t g s n", p=P)).then_inc(s_w.handle, 16)
                e.dma_start(wv[:], w_v.rearrange("(g p) n -> p g n", p=P)).then_inc(s_w.handle, 16)
                e.dma_start(wp[:], w_proj).then_inc(s_w.handle, 16)
                e.dma_start(bp[:], b_proj.rearrange("(g p) -> p g", p=P), allow_slow_non_contiguous=True).then_inc(s_w.handle, 16)
                wait(e, s_w, 64)

            @block.vector
            def _(e):
                e.memset(q[:], 0.0).then_inc(s_z.handle, 1)
                e.memset(kh[:], 0.0).then_inc(s_z.handle, 1)
                e.memset(kl[:], 0.0).then_inc(s_z.handle, 1)
                e.tensor_copy(idh[:], sh["ident"][:]).then_inc(s_z.handle, 1)

            @block.gpsimd
            def _(e):
                e.memset(v[:], 0.0).then_inc(s_z.handle, 1)
                e.memset(o[:], 0.0).then_inc(s_z.handle, 1)

        def project(e, i, t, unit):
            if unit == 0 and t == 0:
                wait(e, s_h, i // PAIRS + 1 if not isinstance(i, int) else 1)
            prev = i * PJA + sum(JA[:unit])
            wait(e, s_ja, prev)
            wait(e, s_jv, prev)
            if unit < 4:
                s, n = divmod(unit, 2)
                for g in range(G3):
                    last = e.matmul(p_j[0:TP, :], wqk[:, t, g, s, :], h[:, g, n * HALF:(n + 1) * HALF], start=(g == 0), stop=(g == G3 - 1))
            else:
                for c in range(4):
                    for g in range(G3):
                        px = (4 * (unit - 4) + c) * P
                        last = e.matmul(p_j[:, c * 2 * D:(c + 1) * 2 * D], h[:, g, px:px + P], wv[:, g, t * 2 * D:(t + 1) * 2 * D],
                                        start=(g == 0), stop=(g == G3 - 1))
            last.then_inc(s_pj.handle, 1)

        def high(e, i, t, unit):
            if unit == 0 and not isinstance(i, int):
                wait(e, s_s, (i - 1) * 16)
            wait(e, s_pj, i * UNITS + unit + 1)
            u, n = t % 2, unit % 2
            cols = slice(n * HALF, (n + 1) * HALF)
            if unit < 2:
                for hd, r in enumerate(ROWS_OF):
                    e.activation(q[r:r + D, u, hd, cols], p_j[r:r + D, :], ACT.Copy, scale=SCALE).then_inc(s_ja.handle, 1)
            elif unit < 4:
                for hd, r in enumerate(ROWS_OF):
                    for to in ROWS_OF:
                        e.copy(kh[to:to + D, u, hd, cols], p_j[r:r + D, :]).then_inc(s_ja.handle, 1)
            else:
                if unit == 4 and not isinstance(i, int):
                    wait(e, s_o, (i - 1) * 4)
                e.copy(v[:, u, 4 * n:4 * n + 4, :, 0:D], p_j[:, 0:8 * D].rearrange("p (c s d) -> p c s d", c=4, s=2)).then_inc(s_ja.handle, 1)

        def low(e, i, t, unit):
            wait(e, s_ja, i * PJA + sum(JA[:unit + 1]))
            u, n = t % 2, unit % 2
            cols = slice(n * HALF, (n + 1) * HALF)
            if unit < 2:
                for hd, r in enumerate(ROWS_OF):
                    z = 64 - r
                    e.scalar_tensor_tensor(q[z:z + D, u, hd, cols], p_j[r:r + D, :], SCALE, q[r:r + D, u, hd, cols],
                                           ALU.mult, ALU.subtract).then_inc(s_jv.handle, 1)
            elif unit < 4:
                for hd, r in enumerate(ROWS_OF):
                    for to in ROWS_OF:
                        e.tensor_tensor(kl[to:to + D, u, hd, cols], p_j[r:r + D, :], kh[r:r + D, u, hd, cols], ALU.subtract).then_inc(s_jv.handle, 1)
            else:
                e.tensor_tensor(v[:, u, 4 * n:4 * n + 4, :, 64:TP], p_j[:, 0:8 * D].rearrange("p (c s d) -> p c s d", c=4, s=2),
                                v[:, u, 4 * n:4 * n + 4, :, 0:D], ALU.subtract).then_inc(s_jv.handle, 1)

        def norm(e, b):
            wait(e, s_xh, (b + 1) * 16)
            wait(e, s_pj, b * (PAIRS * UNITS))
            bb = b % B if not isinstance(b, int) else b
            for g in range(G3):
                gn = sh["gn"][:, g, ds(bb, 1), :].rearrange("p o s -> p (o s)")
                last = e.tensor_scalar(h[:, g, :], xh[:, g, :], gn[:, 0:1], gn[:, 1:2], ALU.subtract, ALU.mult)
            last.then_inc(s_h.handle, 1)

        FIRST = 5
        UNIT_AT = (0, 2, 4, 6, 8, 10)

        def unit_in(m):
            t, r = divmod(m, 16)
            return (t + 1, UNIT_AT.index(r)) if t >= 0 and r in UNIT_AT else None

        with nc.Block() as block:

            @block.sync
            def _(e):
                e.dma_start(xh[:], xv[:, 0, :, :]).then_inc(s_xh.handle, 16)
                with e.Fori(0, B) as b:
                    wait(e, s_yd, b)
                    e.dma_start(xr[:].unsqueeze(1), xv[:, ds(b, 1), :, :]).then_inc(s_xr.handle, 16)
                    hold(sh, e, s_h, b + 1)
                    e.dma_start(xh[:].unsqueeze(1), xv[:, ds((b + 1) % B, 1), :, :]).then_inc(s_xh.handle, 16)
                    wait(e, s_fo, at(b, 6, 6))
                    e.dma_start(yv[:, ds(b, 1), :, :], xr[:].unsqueeze(1)).then_inc(s_y.handle, 16)
                    hold(sh, e, s_st, b + 1)
                    wait(e, s_y, (b + 1) * 16)
                    e.sem_inc(s_yd.handle, 1)
                wait(e, s_xh, 16 * (B + 1))

            @block.tensor
            def _(e):
                def scores(b, m):
                    pair, hd, c = m // 16, m // NT % 2, m % NT
                    if m % 16 == 0:
                        wait(e, s_jv, (b * PAIRS + pair) * PJA + sum(JA[0:4]))
                    wait(e, s_e, at(b, TB, m - 1))
                    for n in range(2):
                        for k, r in ((kh, 0), (kl, 1)):
                            last = e.matmul(p_s[m % 2][:, n, :], q[:, pair % 2, hd, c * P:(c + 1) * P],
                                            k[:, pair % 2, hd, n * HALF:(n + 1) * HALF], start=(r == 0), stop=(r == 1))
                    last.then_inc(s_s.handle, 1)

                def turn(b, m):
                    wait(e, s_ta, at(b, TB, m))
                    wait(e, s_tv, at(b, TB, m))
                    wait(e, s_lo, at(b, TB, m + 1))
                    for r, part in enumerate((ah, al)):
                        for c in range(NT):
                            last = e.transpose(p_t[:, r * NT + c, :], part[:, m % RING, c * P:(c + 1) * P], idh[:])
                    last.then_inc(s_t.handle, 1)

                def weigh(b, j):
                    pair, hd = j // 4, j // 2 % 2
                    if j % 4 == 0:
                        wait(e, s_jv, (b * PAIRS + pair) * PJA + PJA)
                    if j == 0:
                        wait(e, s_fo, b * 6)
                    wait(e, s_on, at(b, 16, j))
                    wait(e, s_ta, at(b, TB, 4 * j + 4))
                    wait(e, s_tv, at(b, TB, 4 * j + 4))
                    for c in range(2 * NT):
                        last = e.matmul(p_o[0:TP, :], v[:, pair % 2, c % NT, hd, :], attT[:, j % 2, c, :],
                                        start=(c == 0), stop=(c == 2 * NT - 1))
                    last.then_inc(s_o.handle, 1)

                def slot(b, m):
                    scores(b, m + 2)
                    if m - 2 >= 0:
                        turn(b, m - 2)
                    if unit_in(m):
                        pair, unit = unit_in(m)
                        project(e, b * PAIRS + pair, pair % PAIRS, unit)
                    if m >= 7 and (m - 7) % 4 == 0:
                        weigh(b, (m - 7) // 4)

                for unit in range(UNITS):
                    project(e, 0, 0, unit)
                for m in range(-2, FIRST):
                    slot(0, m)
                with e.Fori(0, B) as b:
                    for m in range(FIRST, FIRST + TB):
                        slot(b, m)
                    wait(e, s_on, (b + 1) * 16)
                    for m in range(2 * G3):
                        g, n = m // 2, m % 2
                        wait(e, s_fo, at(b, 6, m))
                        for t in range(PAIRS):
                            last = e.matmul(p_o[:], wp[:, t, g * P:(g + 1) * P],
                                            o[:, t, n * HALF:(n + 1) * HALF], start=(t == 0), stop=(t == PAIRS - 1))
                        last.then_inc(s_f.handle, 1)

            @block.gpsimd
            def _(e):
                def part(b, m):
                    r = m % RING
                    wait(e, s_t, at(b, TB, m + 1 - RING))
                    hold(sh, e, s_ri, at(b, TB, m + 1))
                    e.tensor_scalar(ah[:, r, :], att[:, r, :], rden[:, r:r + 1], None, ALU.mult).then_inc(s_hi.handle, 1)

                for m in range(FIRST - 1):
                    part(0, m)
                with e.Fori(0, B) as b:
                    for m in range(FIRST - 1, FIRST - 1 + TB):
                        part(b, m)

            @block.scalar
            def _(e):
                def slot(b, m):
                    if m + 1 >= 0:
                        k, r = m + 1, (m + 1) % RING
                        wait(e, s_m, at(b, TB, k + 1))
                        wait(e, s_lo, at(b, TB, k + 1 - RING))
                        e.activation(att[:, r, :], p_s[k % 2][:].rearrange("p a n -> p (a n)"), ACT.Exp,
                                     bias=nmax[:, r:r + 1], accum_out=den[:, r:r + 1]).then_inc(s_e.handle, 1)
                    if m - 2 >= 0:
                        k = m - 2
                        wait(e, s_t, at(b, TB, k + 1))
                        if k % 4 == 0:
                            wait(e, s_o, at(b, 16, k // 4 - 1))
                        e.copy(attT[:, k // 4 % 2, 0:NT, (k % 4) * P:(k % 4 + 1) * P], p_t[:, 0:NT, :]).then_inc(s_ta.handle, 1)
                    if unit_in(m - 1):
                        pair, unit = unit_in(m - 1)
                        high(e, b * PAIRS + pair, pair % PAIRS, unit)
                    if m >= 8 and (m - 8) % 4 == 0:
                        j = (m - 8) // 4
                        r = ROWS_OF[j // 2 % 2]
                        wait(e, s_o, at(b, 16, j + 1))
                        wait(e, s_on, at(b, 16, j))
                        e.copy(oh[r:r + D, :], p_o[0:D, :]).then_inc(s_oa.handle, 1)

                for unit in range(UNITS):
                    high(e, 0, 0, unit)
                for m in range(-2, FIRST):
                    slot(0, m)
                with e.Fori(0, B) as b:
                    for m in range(FIRST, FIRST + TB):
                        slot(b, m)

            @block.vector
            def _(e):
                def slot(b, m):
                    if m - 1 >= 0:
                        k, r = m - 1, (m - 1) % RING
                        wait(e, s_hi, at(b, TB, k + 1))
                        wait(e, s_t, at(b, TB, k + 1 - RING))
                        e.scalar_tensor_tensor(al[:, r, :], att[:, r, :], rden[:, r:r + 1], ah[:, r, :],
                                               ALU.mult, ALU.subtract).then_inc(s_lo.handle, 1)
                    k, r = m + 2, (m + 2) % RING
                    wait(e, s_s, at(b, TB, k + 1))
                    wait(e, s_e, at(b, TB, k + 1 - RING))
                    e.tensor_reduce(nmax[:, r:r + 1], p_s[k % 2][:].rearrange("p a n -> p (a n)"), AX, ALU.max,
                                    negate=True).then_inc(s_m.handle, 1)
                    if m + 1 >= 0:
                        k, r = m + 1, (m + 1) % RING
                        wait(e, s_e, at(b, TB, k + 1))
                        wait(e, s_lo, at(b, TB, k + 1 - RING))
                        e.reciprocal(rden[:, r:r + 1], den[:, r:r + 1]).then_inc(s_ri.handle, 1)
                    if m - 2 >= 0:
                        k = m - 2
                        wait(e, s_t, at(b, TB, k + 1))
                        if k % 4 == 0:
                            wait(e, s_o, at(b, 16, k // 4 - 1))
                        e.tensor_copy(attT[:, k // 4 % 2, NT:, (k % 4) * P:(k % 4 + 1) * P], p_t[:, NT:, :]).then_inc(s_tv.handle, 1)
                    if m == 3 * 16 - 3:
                        norm(e, b + 1)
                    if unit_in(m - 1):
                        pair, unit = unit_in(m - 1)
                        low(e, b * PAIRS + pair, pair % PAIRS, unit)
                    if m >= 8 and (m - 8) % 4 == 0:
                        j = (m - 8) // 4
                        r = ROWS_OF[j // 2 % 2]
                        t, n = j // 4, j % 2
                        wait(e, s_oa, at(b, 16, j + 1))
                        e.tensor_tensor(o[r:r + D, t, n * HALF:(n + 1) * HALF], p_o[64:TP, :], oh[r:r + D, :], ALU.add).then_inc(s_on.handle, 1)

                norm(e, 0)
                for unit in range(UNITS):
                    low(e, 0, 0, unit)
                for m in range(-2, FIRST):
                    slot(0, m)
                with e.Fori(0, B) as b:
                    for m in range(FIRST, FIRST + TB):
                        slot(b, m)
                    wait(e, s_xr, (b + 1) * 16)
                    for m in range(2 * G3):
                        g, n = m // 2, m % 2
                        wait(e, s_f, at(b, 6, m + 1))
                        part = xr[:, g, n * HALF:(n + 1) * HALF]
                        e.scalar_tensor_tensor(part, p_o[:], bp[:, g:g + 1], part, ALU.add, ALU.add).then_inc(s_fo.handle, 1)
                    wait(e, s_fo, at(b, 6, 6))
                    for m in range(2 * G3):
                        g, n = m // 2, m % 2
                        last = e.bn_stats(one(sh["stat"][:, g, ds(b, 1), n, :]), xr[:, g, n * HALF:(n + 1) * HALF])
                    last.then_inc(s_st.handle, 1)


def normalise(e, sh, h, xs, b):
    for g in range(G3):
        last = e.tensor_scalar(h[:, g, :], xs[:, g, :], one(sh["gn"][:, g, ds(b, 1), 0:1]), one(sh["gn"][:, g, ds(b, 1), 1:2]),
                               ALU.subtract, ALU.mult)
    return last


def one(ap):
    return ap.rearrange("p o n -> p (o n)")


def layer2(nc, sh, x, w_qk, w_vT, w_out, temp, b_out, y):
    xv = x.rearrange("b (g p) n -> p b g n", p=P)
    yv = y.rearrange("b (g p) n -> p b g n", p=P)
    norm_params(nc, sh, "n2")
    with Arena(nc, "c") as a:
        xs = a.sb("xs", [P, 2, G3, N])
        h = a.sb("h", [P, 2, G3, N])
        w = a.sb("w", [P, G3, 2, C])
        wvT = a.sb("wvT", [TP, PAIRS, C])
        wo = a.sb("wo", [D, HEADS, C])
        tmp = a.sb("temp", [D, HEADS])
        bo = a.sb("bo", [P, G3])
        ones = a.sb("ones", [P, D])
        kq = a.sb("kq", [P, NT, HEADS, TP])
        dk = a.sb("dk", [D, HEADS, D])
        dq = a.sb("dq", [P, HEADS, D])
        rk = a.sb("rk", [D, HEADS])
        rq = a.sb("rq", [D, HEADS, D])
        at2 = a.sb("att", [D, HEADS, D])
        mx = a.sb("mx", [D, HEADS])
        attT = a.sb("attT", [D, HEADS, D])
        m = a.sb("m", [TP, PAIRS, C])
        f = a.sb("f", [P, G3, C])
        xo = a.sb("xo", [P, G3, N])
        p_a = [a.ps(f"p_a{i}", [P, 512]) for i in range(4)]
        p_g = a.ps("p_g", [P, 2, 512])
        p_m = a.ps("p_m", [P, 2, 512])
        gram = p_g[:, :, 0:4 * TP].rearrange("p u (h c) -> p u h c", h=4)
        s_w, s_y, s_z = (a.sem(n) for n in ("w", "y", "z"))
        s_x = [a.sem(f"x{u}") for u in range(2)]
        s_h, s_a, s_ae, s_g, s_dq, s_qq, s_c, s_sq, s_ex, s_yd = (a.loop_sem(n) for n in ("h", "a", "ae", "g", "dq", "qq", "c", "sq", "ex", "yd"))
        s_sub, s_an, s_tt, s_te, s_m, s_me, s_f, s_fe, s_o, s_oe, s_st = (
            a.loop_sem(n) for n in ("sub", "an", "tt", "te", "m", "me", "f", "fe", "o", "oe", "st"))
        a.open()
        BEFORE = (3, 9, 11, 12)
        with nc.Block() as block:

            @block.sync
            def _(e):
                e.dma_start(w[:], w_qk.rearrange("(g p) s n -> p g s n", p=P)).then_inc(s_w.handle, 16)
                e.dma_start(wvT[:], w_vT).then_inc(s_w.handle, 16)
                e.dma_start(wo[:], w_out).then_inc(s_w.handle, 16)
                e.dma_start(tmp[:], temp.partition_broadcast(D)).then_inc(s_w.handle, 16)
                e.dma_start(bo[:], b_out.rearrange("(g p) -> p g", p=P), allow_slow_non_contiguous=True).then_inc(s_w.handle, 16)
                wait(e, s_w, 80)

            @block.gpsimd
            def _(e):
                e.memset(kq[:], 0.0).then_inc(s_z.handle, 1)
                e.memset(ones[:], 1.0).then_inc(s_z.handle, 1)
                e.memset(m[:], 0.0).then_inc(s_z.handle, 1)
                wait(e, s_z, 3)

        with nc.Block() as block:

            @block.sync
            def _(e):
                e.dma_start(xs[:, 0, :, :], xv[:, 0, :, :]).then_inc(s_x[0].handle, 16)
                with e.Fori(0, B // 2) as b2:
                    for u in range(2):
                        b = b2 * 2 + u
                        hold(sh, e, s_oe, b * 6)
                        e.dma_start(xs[:, 1 - u, :, :].unsqueeze(1), xv[:, ds((b + 1) % B, 1), :, :]).then_inc(s_x[1 - u].handle, 16)
                        wait(e, s_oe, b * 6 + 6)
                        e.dma_start(yv[:, ds(b, 1), :, :], xo[:].unsqueeze(1)).then_inc(s_y.handle, 16)
                        wait(e, s_y, (b + 1) * 16)
                        e.sem_inc(s_yd.handle, 1)
                for u in range(2):
                    wait(e, s_x[u], 16 * (B // 2 + 1 - u))

            @block.vector
            def _(e):
                wait(e, s_x[0], 16)
                normalise(e, sh, h[:, 0, :, :], xs[:, 0, :, :], 0).then_inc(s_h.handle, 1)
                with e.Fori(0, B // 2) as b2:
                    for u in range(2):
                        b = b2 * 2 + u
                        link = Chain(sh, e, s_c, b, 5)
                        wait(e, s_x[1 - u], (b2 + 1 + u) * 16)
                        wait(e, s_o, b * 6)
                        normalise(e, sh, h[:, 1 - u, :, :], xs[:, 1 - u, :, :], (b + 1) % B).then_inc(s_h.handle, 1)
                        wait(e, s_g, b + 1)
                        idk = sh["ident"][0:D, 0:D].unsqueeze(1).broadcast_to([D, 4, D])
                        idq = sh["ident"][64:TP, 64:TP].unsqueeze(1).broadcast_to([D, 4, D])
                        for v in range(2):
                            e.tensor_tensor(dq[64:TP, 4 * v:4 * v + 4, :], gram[64:TP, v, :, 64:TP], idq, ALU.mult).then_inc(s_dq.handle, 1)
                        for v in range(2):
                            last = e.tensor_tensor(dk[:, 4 * v:4 * v + 4, :], gram[0:D, v, :, 0:D], idk, ALU.mult)
                        link(last)
                        e.tensor_reduce(rk[:], dk[:], AX, ALU.add).then_inc(s_dq.handle, 1)
                        wait(e, s_sq, b * 2 + 1)
                        e.tensor_scalar(rk[:], rk[:], 1e-12, None, ALU.max)
                        wait(e, s_sq, b * 2 + 2)
                        link(e.tensor_scalar(rq[:], rq[:], 1e-12, None, ALU.max))
                        e.reciprocal(rk[:], rk[:])
                        link(e.reciprocal(rq[:], rq[:]))
                        e.tensor_tensor(rk[:], rk[:], tmp[:], ALU.mult)
                        for v in range(2):
                            last = e.tensor_tensor(at2[:, 4 * v:4 * v + 4, :], gram[0:D, v, :, 64:TP], rq[:, 4 * v:4 * v + 4, :], ALU.mult)
                        link(last)
                        link(e.tensor_tensor(at2[:], at2[:], rk[:].unsqueeze(2).broadcast_to([D, HEADS, D]), ALU.mult))
                        e.tensor_reduce(mx[:], at2[:], AX, ALU.max).then_inc(s_sub.handle, 1)
                        wait(e, s_sub, b * 4 + 1)
                        e.tensor_tensor(at2[:], at2[:], mx[:].unsqueeze(2).broadcast_to([D, HEADS, D]), ALU.subtract).then_inc(s_sub.handle, 1)
                        wait(e, s_ex, b + 1)
                        e.tensor_reduce(mx[:], at2[:], AX, ALU.add).then_inc(s_sub.handle, 1)
                        wait(e, s_sub, b * 4 + 3)
                        e.reciprocal(mx[:], mx[:]).then_inc(s_sub.handle, 1)
                        wait(e, s_sub, b * 4 + 4)
                        e.tensor_tensor(at2[:], at2[:], mx[:].unsqueeze(2).broadcast_to([D, HEADS, D]), ALU.mult).then_inc(s_an.handle, 1)
                        wait(e, s_tt, b + 1)
                        e.tensor_copy(attT[:].rearrange("p h d -> p (h d)"), p_m[0:D, 0, 0:C]).then_inc(s_te.handle, 1)
                        for v in range(PAIRS):
                            wait(e, s_m, b * 4 + v + 1)
                            for r in (0, 64):
                                last = e.tensor_copy(m[r:r + D, v, :], p_m[r:r + D, v % 2, 0:C])
                            last.then_inc(s_me.handle, 1)
                        for g in range(G3):
                            wait(e, s_f, b * 3 + g + 1)
                            e.tensor_copy(f[:, g, :], p_a[g][:, 0:C]).then_inc(s_fe.handle, 1)
                        wait(e, s_yd, b)
                        for i in range(2 * G3):
                            g, n = i // 2, i % 2
                            wait(e, s_o, b * 6 + i + 1)
                            e.scalar_tensor_tensor(xo[:, g, n * HALF:(n + 1) * HALF], p_a[i % 4][:], bo[:, g:g + 1],
                                                   xs[:, u, g, n * HALF:(n + 1) * HALF], ALU.add, ALU.add).then_inc(s_oe.handle, 1)
                        wait(e, s_oe, b * 6 + 6)
                        for i in range(2 * G3):
                            g, n = i // 2, i % 2
                            last = e.bn_stats(one(sh["stat"][:, g, ds(b, 1), n, :]), xo[:, g, n * HALF:(n + 1) * HALF])
                        last.then_inc(s_st.handle, 1)
                        link.end()
                wait(e, s_st, B)

            @block.scalar
            def _(e):
                def leave(n, steps):
                    for i in steps:
                        c, s = i // 2, i % 2
                        wait(e, s_a, n * (2 * NT) + i + 1)
                        if i == 0:
                            wait(e, s_g, n)
                        e.copy(kq[:, c, :, 64 * s:64 * s + D], p_a[i % 4][:, 0:C].rearrange("p (h d) -> p h d", h=HEADS)).then_inc(s_ae.handle, 1)

                leave(0, range(2 * NT))
                with e.Fori(0, B) as b:
                    leave(b + 1, range(0, BEFORE[0]))
                    wait(e, s_dq, b * 3 + 3)
                    e.activation(rk[:], rk[:], ACT.Sqrt).then_inc(s_sq.handle, 1)
                    wait(e, s_qq, b + 1)
                    e.activation(rq[:].rearrange("p h d -> p (h d)"), p_m[0:D, 0, 0:C], ACT.Sqrt).then_inc(s_sq.handle, 1)
                    leave(b + 1, range(BEFORE[0], BEFORE[1] - 2))
                    wait(e, s_sub, b * 4 + 2)
                    e.activation(at2[:], at2[:], ACT.Exp).then_inc(s_ex.handle, 1)
                    leave(b + 1, range(BEFORE[1] - 2, 2 * NT))

            @block.tensor
            def _(e):
                def project(n, u, steps):
                    for i in steps:
                        c, s = i // 2, i % 2
                        if i == 0:
                            wait(e, s_h, n + 1)
                            if not isinstance(n, int):
                                wait(e, s_oe, (n - 1) * 6)
                        if i >= 4:
                            wait(e, s_ae, n * (2 * NT) + i - 3)
                        for g in range(G3):
                            last = e.matmul(p_a[i % 4][:, 0:C], h[:, u, g, c * P:(c + 1) * P], w[:, g, s, :], start=(g == 0), stop=(g == G3 - 1))
                        last.then_inc(s_a.handle, 1)

                project(0, 0, range(2 * NT))
                with e.Fori(0, B // 2) as b2:
                    for u in range(2):
                        b = b2 * 2 + u
                        wait(e, s_ae, b * (2 * NT) + 2 * NT)
                        for hd in range(HEADS):
                            for c in range(NT):
                                last = e.matmul(gram[0:TP, hd // 4, hd % 4, :], kq[:, c, hd, :], kq[:, c, hd, :], start=(c == 0), stop=(c == NT - 1))
                        last.then_inc(s_g.handle, 1)
                        project(b + 1, 1 - u, range(0, BEFORE[0]))
                        hold(sh, e, s_dq, b * 3 + 2)
                        e.matmul(p_m[0:D, 0, 0:C], ones[64:TP, :], dq[64:TP, :, :].rearrange("p h d -> p (h d)"), start=True, stop=True).then_inc(s_qq.handle, 1)
                        project(b + 1, 1 - u, range(BEFORE[0], BEFORE[1]))
                        hold(sh, e, s_an, b + 1)
                        for hd in range(HEADS):
                            last = e.transpose(p_m[0:D, 0, hd * D:(hd + 1) * D], at2[:, hd, :], sh["ident"][0:D, 0:D])
                        last.then_inc(s_tt.handle, 1)
                        for v in range(PAIRS):
                            if v % 2 == 0:
                                project(b + 1, 1 - u, range(BEFORE[2 + v // 2 - 1], BEFORE[2 + v // 2]))
                            hold(sh, e, s_te, b + 1)
                            if v >= 2:
                                hold(sh, e, s_me, b * 4 + v - 1)
                            for s in range(2):
                                last = e.matmul(p_m[64 * s:64 * s + D, v % 2, 0:C], attT[:, 2 * v + s, :], wo[:, 2 * v + s, :], start=True, stop=True)
                            last.then_inc(s_m.handle, 1)
                        project(b + 1, 1 - u, range(BEFORE[3], 2 * NT))
                        wait(e, s_ae, (b + 2) * (2 * NT))
                        wait(e, s_me, b * 4 + 4)
                        for g in range(G3):
                            for v in range(PAIRS):
                                last = e.matmul(p_a[g][:, 0:C], wvT[:, v, g * P:(g + 1) * P], m[:, v, :], start=(v == 0), stop=(v == PAIRS - 1))
                            last.then_inc(s_f.handle, 1)
                        wait(e, s_fe, b * 3 + 3)
                        for i in range(2 * G3):
                            o, n = i // 2, i % 2
                            if i >= 4:
                                wait(e, s_oe, b * 6 + i - 3)
                            for g in range(G3):
                                last = e.matmul(p_a[i % 4][:], f[:, g, o * P:(o + 1) * P], h[:, u, g, n * HALF:(n + 1) * HALF], start=(g == 0), stop=(g == G3 - 1))
                            last.then_inc(s_o.handle, 1)


KB = 13
REACH = KB // 2
SHAPES = [(13, 1), (5, 1), (7, 1), (7, 2), (3, 3), (3, 4), (3, 5)]
CONVS = len(SHAPES)
TAPS3 = [k * k for k, _ in SHAPES]
PITCH = W + REACH
KROWS = 24
BANDS = 5
TLEN = BANDS * ROWB * PITCH
CH4 = 4


def layer3(nc, sh, x, weights, bn, y):
    xv = x.rearrange("b (g p) n -> p g b n", p=P)
    yv = y.rearrange("b (g p) n -> p g b n", p=P)
    NTAP = sum(TAPS3)
    wm_dram = nc.dram_tensor("merged_kernels", [C, KROWS * PITCH], F32).ap()
    norm_params(nc, sh, "n3")
    with Arena(nc, "d") as a:
        wr = a.sb("wr", [P, G3, NTAP])
        bnp = a.sb("bnp", [P, G3, CONVS, 4])
        dev = a.sb("dev", [P, G3, CONVS])
        scale = a.sb("scale", [P, G3, CONVS])
        shift = a.sb("shift", [P, G3, CONVS])
        sft = a.sb("sft", [P, G3])
        wm = a.sb("wm", [P, G3, KROWS, PITCH])
        xs = a.sb("xs", [P, B, N])
        h = a.sb("h", [P, 2, N])
        xT = a.sb("xT", [P, P, B * NT])
        yT = a.sb("yT", [P, B * NT, P])
        win = a.sb("win", [P, 2, CH4, TLEN])
        toe = a.sb("toe", [P, 4, CH4, BANDS * ROWB, W])
        xo = a.sb("xo", [P, 2, N])
        p_t = [a.ps(f"p_t{i}", [P, NT, P]) for i in range(2)]
        p_c = [a.ps(f"p_c{i}", [P, 8, B * NT]) for i in range(2)]
        s_w, s_wm, s_c, s_v = (a.sem(n) for n in ("w", "wm", "c", "v"))
        with nc.Block() as block:

            @block.sync
            def _(e):
                off = 0
                for i, wi in enumerate(weights):
                    e.dma_start(wr[:, :, off:off + TAPS3[i]], wi.rearrange("(g p) t -> p g t", p=P)).then_inc(s_w.handle, 16)
                    off += TAPS3[i]
                e.dma_start(bnp[:], bn.rearrange("(g p) i f -> p g i f", p=P)).then_inc(s_w.handle, 16)
                wait(e, s_wm, 1)
                e.dma_start(wm_dram.rearrange("(g p) n -> p g n", p=P), wm[:].rearrange("p g r c -> p g (r c)")).then_inc(s_w.handle, 16)
                wait(e, s_w, 16 * (CONVS + 2))

            @block.scalar
            def _(e):
                wait(e, s_v, 1)
                e.activation(dev[:], dev[:], ACT.Sqrt).then_inc(s_v.handle, 1)

            @block.vector
            def _(e):
                link = Chain(sh, e, s_c)
                link(e.memset(wm[:], 0.0))
                wait(e, s_w, 16 * (CONVS + 1))
                e.tensor_scalar(dev[:], bnp[:, :, :, 3], 1e-5, None, ALU.add).then_inc(s_v.handle, 1)
                wait(e, s_v, 2)
                link(e.reciprocal(dev[:], dev[:]))
                link(e.tensor_tensor(scale[:], bnp[:, :, :, 0], dev[:], ALU.mult))
                link(e.tensor_tensor(shift[:], bnp[:, :, :, 2], scale[:], ALU.mult))
                link(e.tensor_tensor(shift[:], bnp[:, :, :, 1], shift[:], ALU.subtract))
                link(e.tensor_reduce(sft[:], shift[:], AX, ALU.add))
                off = 0
                for i, (k, d) in enumerate(SHAPES):
                    first = REACH - d * (k - 1) // 2
                    span = d * (k - 1) + 1
                    for g in range(G3):
                        into = wm[:, g, REACH + first:REACH + first + span:d, first:first + span:d]
                        last = e.scalar_tensor_tensor(into, wr[:, g, off:off + k * k].rearrange("p (a b) -> p a b", a=k),
                                                      scale[:, g, i:i + 1], into, ALU.mult, ALU.add)
                    if i + 1 < CONVS:
                        link(last)
                    off += k * k
                last.then_inc(s_wm.handle, 1)
                wait(e, s_wm, 1)

        s_x = a.sem("x")
        s_h, s_t, s_te, s_p, s_pe, s_b, s_o, s_yd = (a.loop_sem(n) for n in ("h", "t", "te", "p", "pe", "b", "o", "yd"))
        s_y = [a.sem(f"y{u}") for u in range(2)]
        s_win = [a.sem(f"win{q}") for q in range(2)]
        s_toe = [a.loop_sem(f"toe{q}") for q in range(4)]
        a.open()
        CB = P // (4 * CH4)
        win_m = win[:].rearrange("p q c (r w) -> p q c r w", w=PITCH)
        xT_m = xT[:].rearrange("p c (b i) -> p c b i", b=B)
        with nc.Block() as block:

            @block.sync
            def _(e):
                with e.Fori(0, G3 * CB) as i:
                    for q in range(4):
                        wait(e, s_toe[(q - 2) % 4], i + 1)
                        for r in range(ROWB):
                            src = bass.AP(wm_dram.tensor, REACH * 2 + 1 + r * PITCH, [[KROWS * PITCH, C], [1, W], [1, TLEN - PITCH + W]])
                            e.dma_start(win[r * W:(r + 1) * W, q % 2, :, 0:TLEN - PITCH + W],
                                        src[ds(i * (4 * CH4) + q * CH4, CH4)].rearrange("c w n -> w c n")).then_inc(s_win[q % 2].handle, 16)

            def pack(e, copy, i, q):
                wait(e, s_win[q % 2], (i * 2 + q // 2 + 1) * (16 * ROWB))
                hold(sh, e, s_p, i * 4 + q + 1)
                copy(toe[:, q, :, :, :], win_m[:, q % 2, :, :, 0:W]).then_inc(s_toe[q].handle, 1)

            @block.gpsimd
            def _(e):
                with e.Fori(0, G3) as g:
                    with e.Fori(0, CB) as j:
                        pack(e, e.tensor_copy, g * CB + j, 1)
                    with e.Fori(0, B // 2) as b2:
                        for u in range(2):
                            wait(e, s_o, g * B + b2 * 2 + u + 1)
                            e.dma_start(yv[:, ds(g, 1), ds(b2 * 2 + u, 1), :], xo[:, u:u + 1, :].unsqueeze(1)).then_inc(s_y[u].handle, 16)
                        for u in range(2):
                            wait(e, s_y[u], (g * (B // 2) + b2 + 1) * 16)
                        e.sem_inc(s_yd.handle, 1)

            @block.scalar
            def _(e):
                with e.Fori(0, G3) as g:
                    wait(e, s_o, g * B)
                    e.dma_start(xs[:].unsqueeze(1), xv[:, ds(g, 1), :, :]).then_inc(s_x.handle, 16)
                    with e.Fori(0, B // 2) as b2:
                        for u in range(2):
                            n = g * B + b2 * 2 + u
                            wait(e, s_t, n + 1)
                            if u == 0:
                                e.copy(xT_m[:, :, ds(b2 * 2, 1), :].rearrange("p c o i -> p c (o i)"), p_t[0][:].rearrange("p i c -> p c i")).then_inc(s_te.handle, 1)
                    with e.Fori(0, CB) as j:
                        i = g * CB + j
                        pack(e, e.copy, i, 2)
                        wait(e, s_p, i * 4 + 2 + 4)
                        e.copy(yT[:, :, ds(j * 16, 8)], p_c[0][:].rearrange("p c n -> p n c")).then_inc(s_pe.handle, 1)

            @block.vector
            def _(e):
                with e.Fori(0, G3) as g:
                    with e.Fori(0, B // 2) as b2:
                        for u in range(2):
                            n = g * B + b2 * 2 + u
                            b = b2 * 2 + u
                            wait(e, s_x, g * 16 + 16)
                            gn = sh["gn"][:, ds(g, 1), ds(b, 1), :].rearrange("p g b s -> p (g b s)")
                            e.tensor_scalar(h[:, u, :], one(xs[:, ds(b, 1), :]), gn[:, 0:1], gn[:, 1:2], ALU.subtract, ALU.mult).then_inc(s_h.handle, 1)
                            wait(e, s_t, n + 1)
                            if u == 1:
                                e.tensor_copy(xT_m[:, :, ds(b, 1), :].rearrange("p c o i -> p c (o i)"), p_t[1][:].rearrange("p i c -> p c i")).then_inc(s_te.handle, 1)
                    with e.Fori(0, CB) as j:
                        i = g * CB + j
                        pack(e, e.tensor_copy, i, 0)
                        pack(e, e.tensor_copy, i, 3)
                        wait(e, s_p, i * 4 + 4 + 4)
                        e.tensor_copy(yT[:, :, ds(j * 16 + 8, 8)], p_c[1][:].rearrange("p c n -> p n c")).then_inc(s_pe.handle, 1)
                    for b in range(B):
                        wait(e, s_b, g * B + b + 1)
                        wait(e, s_yd, g * (B // 2) + b // 2)
                        e.scalar_tensor_tensor(xo[:, b % 2, :], p_t[b % 2][:].rearrange("p i w -> p (i w)").rearrange("p (i w) -> p i w", i=NT)[:, :, ::-1],
                                               sft[:, ds(g, 1)], xs[:, b, :].rearrange("p (i w) -> p i w", i=NT), ALU.add, ALU.add).then_inc(s_o.handle, 1)

            @block.tensor
            def _(e):
                e.sem_inc(s_p.handle, 4)
                for q in (2, 3):
                    e.sem_inc(s_toe[q].handle, 1)
                with e.Fori(0, G3) as g:
                    with e.Fori(0, B // 2) as b2:
                        for u in range(2):
                            n = g * B + b2 * 2 + u
                            wait(e, s_h, n + 1)
                            wait(e, s_te, g * B + b2 * 2)
                            for i in range(NT):
                                last = e.transpose(p_t[u][:, i, :], h[:, u, i * P:(i + 1) * P], sh["ident"][:])
                            last.then_inc(s_t.handle, 1)
                    with e.Fori(0, CB) as j:
                        i = g * CB + j
                        for q in range(4):
                            wait(e, s_toe[q], i + 1 + (q == 2 or q == 3))
                            if q == 0:
                                wait(e, s_te, g * B + B)
                            if q % 2 == 0:
                                wait(e, s_pe, i * 2)
                            for c in range(CH4):
                                ch = j * 16 + (q * CH4 + c)
                                for d in (0, -1, 1, -2, 2):
                                    lo, hi = max(0, -d), min(NT, NT - d)
                                    rows = ROWB * (d + 2)
                                    last = e.matmul(p_c[q // 2][:, (q % 2) * CH4 + c, :].rearrange("p (b i) -> p b i", b=B)[:, :, lo:hi],
                                                    toe[:, q, c, rows:rows + ROWB, :].rearrange("p r w -> p (r w)"),
                                                    xT_m[:, ds(ch, 1), :, lo + d:hi + d].rearrange("p o b i -> p (o b) i"),
                                                    start=(d == 0), stop=(d == 2), skip_group_check=True)
                            last.then_inc(s_p.handle, 1)
                    for b in range(B):
                        if b == 0:
                            wait(e, s_pe, (g + 1) * (2 * CB))
                        if b >= 2:
                            wait(e, s_o, g * B + b - 1)
                        for i in range(NT):
                            last = e.transpose(p_t[b % 2][:, i, :], yT[:, b * NT + i, :], sh["ident"][:])
                        last.then_inc(s_b.handle, 1)


KS = (3, 5, 7)
NEAR = ROWB
NARROW = {3: 2, 5: 3, 7: NEAR}
CHUNKS = NT + 2
FAR_STEP = 3 * ROWB
FAR = 3
TOP = FAR * FAR_STEP + 2 * ROWB
ROWS = 2 * TOP + H
PARTS = 2
SLOTS = {3: (0, 1, 2), 5: (0, 1, 2, 0, 1), 7: (0, 1, 2, 0, 1, 2, 1)}
NB = 3
BACK = 5
HID = C // 16


def last_use(K, kx):
    seq = SLOTS[K]
    return next(n for n in range(1, 2 * K) if seq[(kx - n) % K] == seq[kx])


def nth_use(K, kx):
    seq = SLOTS[K]
    return seq.count(seq[kx]), seq[:kx + 1].count(seq[kx])


def columns_of(j, reach):
    top = (j - 1) * ROWB
    return max(0, top - reach) * W, min(H, top + ROWB + reach) * W


class Taps:

    def __init__(self, a, tag):
        self.s_stack, self.s_y = (a.sem(f"{tag}_{n}") for n in ("stack", "y"))
        self.s_hk, self.s_row, self.s_col, self.s_acc = (a.sem(f"{tag}_{n}") for n in ("hk", "row", "col", "act"))
        self.s_py = [a.sem(f"{tag}_py{i}") for i in range(NB)]
        self.s_px = [a.sem(f"{tag}_px{i}") for i in range(NB)]
        self.s_hi, self.s_rep, self.s_s, self.s_m = (a.sem(f"{tag}_{n}") for n in ("hi", "rep", "s", "m"))
        self.all = [self.s_stack, self.s_y, self.s_hk, self.s_row, self.s_col, self.s_acc, self.s_hi, self.s_rep, self.s_s, self.s_m, *self.s_py, *self.s_px]


ITEMS = 2 * CHUNKS


def credit(sh, block, tp):
    @block.gpsimd
    def _(e):
        e.sem_inc(tp.s_y.handle, 1)

    for engine in (block.sync, block.scalar):

        @engine
        def _(e):
            e.sem_inc(sh["tick"], 1)

    @block.vector
    def _(e):
        e.sem_inc(tp.s_stack.handle, BACK)
        e.sem_inc(tp.s_s.handle, BACK * ITEMS)

    @block.tensor
    def _(e):
        e.sem_inc(tp.s_rep.handle, BACK * ITEMS)
        e.sem_inc(tp.s_m.handle, BACK * ITEMS)


def load_row(e, K, tp, bf, ky, first):
    for s in range(2):
        e.dma_start(bf["hk"][:, s, :, :], bf["hTd"][s, ds(first * W, CHUNKS * P), :].rearrange("(j p) c -> p j c", p=P)).then_inc(tp.s_hk.handle, 16)
    e.dma_start(bf["wk"][:, 0:K, :], bf["dw"][ds(ky * K, K), :].partition_broadcast(P)).then_inc(tp.s_hk.handle, 16)


def deform(nc, sh, block, K, tp, bf, loop, rows, ahead, zero_first, reach):
    def near(T, n, per):
        return (T - n + 1 + BACK) * per

    @block.sync
    def _(e):
        for it, ky, row, loaded in rows(e):
            for kx in range(K):
                T, b, back = it * K + kx, SLOTS[K][kx], last_use(K, kx)
                m = (ky * K + kx) * 2
                wait(e, tp.s_stack, near(T, back, 1))
                for s in range(2):
                    e.dma_start(bf["py"][64 * s:64 * s + 64, b, :], bf["posd"][s, ds(m, 1), :].partition_broadcast(64).rearrange("p o n -> p (o n)")).then_inc(tp.s_py[b].handle, 16)
                if kx == 0 and not loaded:
                    wait(e, tp.s_y, it * K + 1)
                    load_row(e, K, tp, bf, ky, row + ky)
                wait(e, tp.s_s, near(T, back, ITEMS))
                e.dma_start(bf["px"][:, b, :, :], bf["posd"][:, ds(m + 1, 1), :].rearrange("s o n -> (s o) n").partition_broadcast(P)).then_inc(tp.s_px[b].handle, 16)

    @block.scalar
    def _(e):
        for it, ky, row in loop(e):
            for kx in range(K):
                b = SLOTS[K][kx]
                uses, nth = nth_use(K, kx)
                T = it * K + kx
                for buf, sem, by, done in ((bf["py"][:, b, :], tp.s_py[b], 32, tp.s_row),
                                           (bf["px"][:, b, :, :].rearrange("p s n -> p (s n)"), tp.s_px[b], 16, tp.s_col)):
                    wait(e, sem, (it * uses + nth) * by)
                    e.activation(buf, buf, ACT.Abs, bias=bf["minus"][:]).then_inc(tp.s_acc.handle, 1)
                    wait(e, tp.s_acc, T * 2 + (1 if done is tp.s_row else 2))
                    e.activation(buf, buf, ACT.Relu, bias=1.0, scale=-1.0).then_inc(done.handle, 1)

    @block.gpsimd
    def _(e):
        for it, ky, row in loop(e):
            for kx in range(K):
                b = SLOTS[K][kx]
                T = it * K + kx
                if kx == 0:
                    wait(e, tp.s_hk, (it + 1) * 48)
                hold(sh, e, tp.s_m, near(T, last_use(K, kx), ITEMS))
                e.tensor_tensor(bf["y"][:, b, :, :], bf["hk"][:].rearrange("p s j c -> p (s j) c"),
                                bf["wk"][:, kx, :].unsqueeze(1).broadcast_to([P, ITEMS, P]), ALU.mult).then_inc(tp.s_y.handle, 1)

    @block.vector
    def _(e):
        def split(it, kx):
            T, b = it * K + kx, SLOTS[K][kx]
            wait(e, tp.s_row, T + 1)
            e.tensor_copy(bf["hi"][:], bf["py"][:, b, :]).then_inc(tp.s_hi.handle, 1)
            wait(e, tp.s_hi, T + 1)
            wait(e, tp.s_rep, near(T, last_use(K, kx), ITEMS))
            e.scalar_tensor_tensor(bf["stack"][:, b, :], bf["hi"][:], bf["low"][:], bf["py"][:, b, :], ALU.mult, ALU.subtract).then_inc(tp.s_stack.handle, 1)

        def multiply(it, ky, row, more):
            for kx in range(K):
                T, b = it * K + kx, SLOTS[K][kx]
                for i in range(ITEMS):
                    s, j = divmod(i, CHUNKS)
                    lo, hi = columns_of(j, reach)
                    n = hi - lo
                    if i == 0:
                        wait(e, tp.s_col, T + 1)
                    if i == CHUNKS:
                        if kx + 1 < K:
                            split(it, kx + 1)
                        elif more:
                            split(it + 1, 0)
                    wait(e, tp.s_rep, (T + BACK) * ITEMS + i + 1)
                    wait(e, tp.s_m, (T + BACK) * ITEMS + i + 1 - bf["NS"])
                    e.tensor_tensor(bf["S"][:, i % bf["NS"], 0:n], bf["p_r"][i % 4][:, 0:n],
                                    bf["px"][:, b, s, lo:hi], ALU.mult).then_inc(tp.s_s.handle, 1)

        ahead(e, lambda it, ky, row: split(it, 0), multiply)

    @block.tensor
    def _(e):
        if zero_first:
            for s in range(2):
                for n in range(2):
                    e.matmul(bf["acc"][s][:, n, :], bf["zero"][:, 0:P], bf["zero"][:], start=True, stop=False, skip_group_check=True)

        def spread(it, ky, row, k):
            kx, i = divmod(k, ITEMS)
            s, j = divmod(i, CHUNKS)
            T, b = it * K + kx, SLOTS[K][kx]
            lo, hi = columns_of(j, reach)
            if i == 0:
                wait(e, tp.s_stack, T + 1 + BACK)
            wait(e, tp.s_s, (T + BACK) * ITEMS + i + 1 - 4)
            e.matmul(bf["p_r"][i % 4][:, 0:hi - lo], bf["E"][:, s, ds((row + ky + j * ROWB) * W, P)],
                     bf["stack"][:, b, lo:hi], start=True, stop=True).then_inc(tp.s_rep.handle, 1)

        def product(it, k):
            kx, i = divmod(k, ITEMS)
            s, j = divmod(i, CHUNKS)
            T, b = it * K + kx, SLOTS[K][kx]
            lo, hi = columns_of(j, reach)
            if i == 0:
                wait(e, tp.s_y, T + 2)
            wait(e, tp.s_s, (T + BACK) * ITEMS + i + 1)
            for n in range(2):
                a, z = max(lo, n * HALF), min(hi, (n + 1) * HALF)
                if a < z:
                    last = e.matmul(bf["acc"][s][:, n, a - n * HALF:z - n * HALF], bf["y"][:, b, i, :],
                                    bf["S"][:, i % bf["NS"], a - lo:z - lo], start=False, stop=False, skip_group_check=True)
            last.then_inc(tp.s_m.handle, 1)

        AHEAD = 3

        def start(it, ky, row):
            for k in range(AHEAD):
                spread(it, ky, row, k)

        def multiply(it, ky, row, more):
            for k in range(K * ITEMS):
                if k + AHEAD < K * ITEMS:
                    spread(it, ky, row, k + AHEAD)
                elif more:
                    spread(it + 1, ky + 1, row, k + AHEAD - K * ITEMS)
                product(it, k)

        ahead(e, start, multiply)


def layer1(nc, sh, x, t, y):
    xv = x.rearrange("b (g p) n -> p b g n", p=P)
    yv = y.rearrange("b (g p) n -> p b g n", p=P)
    M7 = 2 * KS[-1] ** 2
    posd = nc.dram_tensor("sampling_positions", [2, M7, N], F32).ap()
    hTd = nc.dram_tensor("turned_image", [2, ROWS * W, P], F32).ap()
    PADT = TOP * W // P
    norm_params(nc, sh, "n1")
    with Arena(nc, "b") as a:
        E = a.sb("E", [P, 2, ROWS * W], F16)
        zero = a.sb("zero", [P, HALF], F16)
        minus = a.sb("minus", [P, 1])
        low = a.sb("low", [P, 1])
        ymask = a.sb("ymask", [M7, 1])
        pw = a.sb("pw", [P, G3, P])
        pb = a.sb("pb", [P, G3])
        ob = a.sb("ob", [M7, G3])
        f1 = a.sb("f1", [P, G3, HID])
        f2 = a.sb("f2", [HID, G3, P])
        dcv = a.sb("dcv", [P, G3, 2, N])
        xs = a.sb("xs", [P, 2, G3, N])
        h = a.sb("h", [P, 2, N])
        hk = a.sb("hk", [P, 2, CHUNKS, P])
        wk = a.sb("wk", [P, KS[-1], P])
        pool = a.sb("pool", [P, G3, 2, 2])
        far = a.sb("far", [1, 1 + 2 * FAR * KS[-1]], I32)
        wide = a.sb("wide", [1, 1], I32)
        ps = [a.ps(f"p{i}", [P, 2, HALF]) for i in range(4)]
        acc = ps[0:2]
        p_r = [ps[2 + i // 2][:, i % 2, :] for i in range(4)]
        taps = [Taps(a, f"t{g}") for g in range(G3)]
        tfar = Taps(a, "far")
        s_i, s_iv, s_hv, s_iz = (a.sem(n) for n in ("i", "iv", "hv", "iz"))
        with Arena(nc, "bi") as ai, nc.Block() as block:
            ef = ai.sb("ef", [P, 2, H * W])
            zt = ai.sb("zt", [P, PADT, P])

            @block.sync
            def _(e):
                e.dma_start(ef[:], t["b_E"].rearrange("s p n -> p s n")).then_inc(s_i.handle, 16)
                for dst, src in ((minus[:], t["b_minus"]), (low[:], t["b_low"]), (ymask[:], t["b_ymask"]),
                                 (pw[:], t["b_pw"].rearrange("g c o -> c g o")), (f1[:], t["b_f1"].rearrange("g c o -> c g o")), (f2[:], t["b_f2"]),
                                 (pb[:], t["b_pb"]), (ob[:], t["b_ob"])):
                    e.dma_start(dst, src, allow_slow_non_contiguous=True).then_inc(s_i.handle, 16)
                wait(e, s_iv, 2)
                for s in range(2):
                    for r0 in (0, (TOP + H) * W):
                        e.dma_start(hTd[s, r0:r0 + TOP * W, :].rearrange("(j p) c -> p j c", p=P), zt[:]).then_inc(s_iz.handle, 16)
                wait(e, s_iz, 16 * 4)
                wait(e, s_i, 16 * 9)

            @block.gpsimd
            def _(e):
                e.memset(zt[:], 0.0).then_inc(s_iv.handle, 1)
                e.memset(zero[:], 0.0).then_inc(s_iv.handle, 1)

            @block.vector
            def _(e):
                e.memset(E[:], 0.0).then_inc(s_hv.handle, 1)
                wait(e, s_hv, 1)
                wait(e, s_i, 16 * 9)
                e.tensor_copy(E[:, :, TOP * W:(TOP + H) * W], ef[:]).then_inc(s_hv.handle, 1)
                wait(e, s_hv, 2)

        for tp in taps:
            with nc.Block() as block:
                credit(sh, block, tp)

        SA = {n: [(a.sem if n in ("x", "w", "g", "st") else a.loop_sem)(f"{n}{g}") for g in range(G3)] for n in ("x", "w", "g", "h", "hp", "tr", "cv", "po", "tt", "fl", "st", "ev", "pw", "dc")}
        SC = {n: a.loop_sem(f"c{n}") for n in ("r", "p", "a", "o")}
        s_cy = [a.sem(f"cy{g}") for g in range(G3)]
        a.open()
        with nc.Block() as block:

            @block.sync
            def _(e):
                for g in range(G3):
                    e.dma_start(xs[:, :, g, :], xv[:, 0:2, g, :]).then_inc(SA["x"][g].handle, 16)

        with nc.Fori(0, B // 2) as pr:
            def normalise_group(e, g):
                wait(e, SA["x"][g], (pr + 1) * 16)
                for s in range(2):
                    gn = sh["gn"][:, g, ds(pr * 2 + s, 1), :].rearrange("p b s -> p (b s)")
                    e.tensor_scalar(h[:, s, :], xs[:, s, g, :], gn[:, 0:1], gn[:, 1:2], ALU.subtract, ALU.mult).then_inc(SA["h"][g].handle, 1)

            for g, K in enumerate(KS):
                M, R = 2 * K * K, K // 2
                first = TOP - ROWB - R
                row_bf = {"hk": hk, "wk": wk, "hTd": hTd, "dw": t[f"b_dw{g}"]}
                with Arena(nc, f"o{g}") as ao, nc.Block() as block:
                    PW = W + 2 * R
                    ow = ao.sb("ow", [P, K * K, M])
                    grid = ao.sb("grid", [M, N])
                    hp = ao.sb("hp", [P, 2, PW, PW])
                    hT = ao.sb("hT", [P, 2, NT, P])
                    pos = ao.sb("pos", [M, 2, N])
                    off = ao.sb("off", [M, 2, N])
                    mx = ao.sb("mx", [M, 2, 4])
                    mxm = ao.sb("mxm", [M, 2])
                    fm = ao.sb("fm", [1, 2, K])
                    fw = ao.sb("fw", [1, 1])
                    S = {n: v[g] for n, v in SA.items()}

                    @block.sync
                    def _(e):
                        e.dma_start(ow[:], t[f"b_ow{g}"]).then_inc(S["w"].handle, 16)
                        e.dma_start(grid[:], t[f"b_grid{g}"]).then_inc(S["g"].handle, 16)
                        wait(e, S["tr"], pr * 3 + 3)
                        for s in range(2):
                            e.dma_start(hTd[s, TOP * W:(TOP + H) * W, :].rearrange("(j p) c -> p j c", p=P), hT[:, s, :, :]).then_inc(S["st"].handle, 16)
                        hold(sh, e, S["st"], pr * 48 + 32)
                        load_row(e, K, taps[g], row_bf, 0, first)
                        wait(e, S["po"], pr * 16 + 16)
                        e.dma_start(posd[:, 0:M, :].rearrange("s m n -> m s n"), pos[:]).then_inc(S["st"].handle, 16)
                        hold(sh, e, S["st"], (pr + 1) * 48)

                    @block.gpsimd
                    def _(e):
                        e.memset(hp[:], 0.0).then_inc(S["hp"].handle, 1)

                    @block.scalar
                    def _(e):
                        wait(e, S["hp"], pr * 2 + 1)
                        wait(e, S["h"], pr * 2 + 2)
                        for s in range(2):
                            last = e.copy(hp[:, s, R:R + H, R:R + W], h[:, s, :].rearrange("p (a b) -> p a b", a=H))
                        last.then_inc(S["hp"].handle, 1)
                        wait(e, S["tr"], pr * 3 + 1)
                        for s in range(2):
                            e.copy(hT[:, s, :, :], ps[2 + s][:].rearrange("p a (b c) -> p (a b) c", c=P)).then_inc(S["tr"].handle, 1)

                    @block.vector
                    def _(e):
                        if g == 0:
                            normalise_group(e, g)
                        wait(e, S["g"], (pr + 1) * 16)
                        for s in range(2):
                            for n in range(2):
                                wait(e, S["cv"], pr * 4 + s * 2 + n + 1)
                                part = slice(n * HALF, (n + 1) * HALF)
                                e.tensor_scalar(off[:, s, part], acc[s][0:M, n, :], ob[0:M, g:g + 1], None, ALU.add).then_inc(S["po"].handle, 1)
                                hold(sh, e, S["po"], pr * 16 + (s * 2 + n) * 4 + 1)
                                for dst, red, neg in ((0, ALU.min, True), (1, ALU.max, False)):
                                    e.tensor_reduce(mx[:, dst, s * 2 + n:s * 2 + n + 1], off[:, s, part], AX, red, negate=neg).then_inc(S["po"].handle, 1)
                                e.tensor_tensor(pos[:, s, part], off[:, s, part], grid[:, part], ALU.add).then_inc(S["po"].handle, 1)
                        hold(sh, e, S["po"], pr * 16 + 16)
                        link = Chain(sh, e, S["fl"], pr, 7)
                        link(e.tensor_reduce(mxm[:], mx[:], AX, ALU.max))
                        link(e.tensor_scalar(mxm[:], mxm[:], ymask[0:M, :], None, ALU.mult))
                        wait(e, S["tt"], pr + 1)
                        for way in range(2):
                            last = e.tensor_reduce(fm[:, way, :], ps[2][0:1, way, 0:M].rearrange("p (ky m) -> p ky m", ky=K), AX, ALU.max)
                        link(last)
                        for f in range(2 * FAR):
                            steps = FAR - 1 - f if f < FAR else f - FAR
                            last = e.tensor_scalar(far[:, 1 + f * KS[-1]:1 + f * KS[-1] + K], fm[:, int(f >= FAR), :],
                                                   float(NEAR + steps * FAR_STEP), None, ALU.is_gt)
                        link(last)
                        n = 1 + (FAR - 1) * KS[-1]
                        link(e.tensor_reduce(far[:, 0:1], far[:, n:n + 2 * KS[-1]].rearrange("p (f k) -> p f k", f=2)[:, :, 0:K],
                                             mybir.AxisListType.XY, ALU.max))
                        link(e.tensor_reduce(fw[:], fm[:], mybir.AxisListType.XY, ALU.max))
                        link(e.tensor_scalar(wide[:], fw[:], float(NARROW[K]), None, ALU.is_gt))
                        link.end()

                    @block.tensor
                    def _(e):
                        wait(e, S["h"], pr * 2 + 2)
                        for s in range(2):
                            for i in range(NT):
                                last = e.transpose(ps[2 + s][:, i // 4, i % 4 * P:(i % 4 + 1) * P], h[:, s, i * P:(i + 1) * P], sh["ident"][:])
                        last.then_inc(S["tr"].handle, 1)
                        wait(e, S["w"], (pr + 1) * 16)
                        wait(e, S["hp"], pr * 2 + 2)
                        for s in range(2):
                            for n in range(2):
                                for k in range(K * K):
                                    dy, dx = divmod(k, K)
                                    last = e.matmul(acc[s][0:M, n, :].rearrange("p (a b) -> p a b", b=W), ow[:, k, :],
                                                    hp[:, s, n * 16 + dy:n * 16 + dy + 16, dx:dx + W], start=(k == 0), stop=(k == K * K - 1))
                                last.then_inc(S["cv"].handle, 1)
                        wait(e, S["tr"], pr * 3 + 3)
                        hold(sh, e, S["fl"], pr * 7 + 2)
                        for way in range(2):
                            last = e.matmul(ps[2][0:1, way, 0:M], mxm[:, way:way + 1], sh["ident"][0:M, 0:M], start=True, stop=True)
                        last.then_inc(S["tt"].handle, 1)

                with Arena(nc, f"m{g}") as am:
                    bf = {**row_bf, "py": am.sb("py", [P, NB, N]),
                          "px": am.sb("px", [P, NB, 2, N]), "hi": am.sb("hi", [P, N], F16), "stack": am.sb("stack", [P, NB, N], F16),
                          "y": am.sb("y", [P, NB, ITEMS, P]), "NS": 5, "S": am.sb("S", [P, 5, 3 * P]),
                          "posd": posd, "minus": minus, "low": low, "zero": zero, "E": E,
                          "acc": acc, "p_r": p_r}
                    smp = am.sb("smp", [P, 2, N])
                    def near_loop(e):
                        with e.Fori(0, K) as ky:
                            yield pr * K + ky, ky, first

                    def near_rows(e):
                        yield pr * K, 0, first, True
                        with e.Fori(1, K) as ky:
                            yield pr * K + ky, ky, first, False

                    def near_ahead(e, start, row_of_taps):
                        start(pr * K, 0, first)
                        with e.Fori(0, K - 1) as ky:
                            row_of_taps(pr * K + ky, ky, first, True)
                        row_of_taps(pr * K + K - 1, K - 1, first, False)

                    if NARROW[K] == NEAR:
                        with nc.Block() as block:
                            deform(nc, sh, block, K, taps[g], bf, near_loop, near_rows, near_ahead, True, NEAR)
                    else:
                        with nc.If(nc.values_load(wide[0:1, 0:1], min_val=0, max_val=1) < 1):
                            with nc.Block() as block:
                                deform(nc, sh, block, K, taps[g], bf, near_loop, near_rows, near_ahead, True, NARROW[K])
                        with nc.If(nc.values_load(wide[0:1, 0:1], min_val=0, max_val=1) > 0):
                            with nc.Block() as block:
                                deform(nc, sh, block, K, taps[g], bf, near_loop, near_rows, near_ahead, True, NEAR)
                    with nc.If(nc.values_load(far[0:1, 0:1], min_val=0, max_val=1) > 0):
                        with nc.Fori(0, 2 * FAR) as f, nc.Fori(0, K) as ky:
                            which = nc.values_load(far[0:1, ds(1 + f * KS[-1] + ky, 1)], min_val=0, max_val=1)
                            row = first + f * FAR_STEP + f // FAR * FAR_STEP - FAR * FAR_STEP
                            with nc.If(which > 0):
                                with nc.Block() as block:
                                    credit(sh, block, tfar)
                                def far_ahead(e, start, row_of_taps):
                                    start(0, ky, row)
                                    row_of_taps(0, ky, row, False)

                                with nc.Block() as block:
                                    deform(nc, sh, block, K, tfar, bf, lambda e: [(0, ky, row)], lambda e: [(0, ky, row, False)], far_ahead, False, NEAR)
                                clear(nc, [sem.handle for sem in tfar.all])
                    with nc.Block() as block:
                        S = {n: v[g] for n, v in SA.items()}

                        @block.scalar
                        def _(e):
                            for s in range(2):
                                e.copy(smp[:, s, :], acc[s][:].rearrange("p a n -> p (a n)")).then_inc(S["ev"].handle, 1)
                            for s in range(2):
                                wait(e, S["pw"], pr * 2 + s + 1)
                                e.activation(dcv[:, g, s, :], ps[2 + s][:].rearrange("p a n -> p (a n)"), ACT.Identity, bias=pb[:, g:g + 1],
                                             accum_out=pool[:, g, 0, s:s + 1]).then_inc(S["dc"].handle, 1)

                        @block.vector
                        def _(e):
                            if g + 1 < G3:
                                normalise_group(e, g + 1)
                            for s in range(2):
                                wait(e, S["dc"], pr * 2 + s + 1)
                                e.tensor_reduce(pool[:, g, 1, s:s + 1], dcv[:, g, s, :], AX, ALU.max)

                        @block.tensor
                        def _(e):
                            for s in range(2):
                                wait(e, S["ev"], pr * 2 + s + 1)
                                for n in range(2):
                                    last = e.matmul(ps[2 + s][:, n, :], pw[:, g, :], smp[:, s, n * HALF:(n + 1) * HALF], start=True, stop=True)
                                last.then_inc(S["pw"].handle, 1)

            with Arena(nc, "se") as ae, nc.Block() as block:
                hid = ae.sb("hid", [HID, 4])
                z = ae.sb("z", [P, G3, 2])
                zz = ae.sb("zz", [P, G3, 4])

                @block.sync
                def _(e):
                    for g in range(G3):
                        wait(e, SC["o"], pr * 9 + 2 * g + 2)
                        e.dma_start(yv[:, ds(pr * 2, 2), g, :], xs[:, :, g, :]).then_inc(s_cy[g].handle, 16)
                    for g in range(G3):
                        hold(sh, e, s_cy[g], (pr + 1) * 16)
                        hold(sh, e, SC["o"], pr * 9 + 7 + g)
                        e.dma_start(xs[:, :, g, :], xv[:, ds((pr + 1) % (B // 2) * 2, 2), g, :]).then_inc(SA["x"][g].handle, 16)

                @block.vector
                def _(e):
                    link = Chain(sh, e, SC["r"], pr, 6)
                    link(e.tensor_scalar(pool[:, :, 0, :], pool[:, :, 0, :], 1.0 / N, None, ALU.mult))
                    wait(e, SC["p"], pr * 2 + 1)
                    link(e.tensor_scalar(hid[:], ps[2][0:HID, 0, 0:4], 0.0, None, ALU.max))
                    wait(e, SC["p"], pr * 2 + 2)
                    link(e.tensor_copy(zz[:], ps[3][:, 0, 0:4 * G3].rearrange("p (g f) -> p g f", f=4)))
                    link(e.tensor_tensor(z[:], zz[:, :, 0:2], zz[:, :, 2:4], ALU.add))
                    wait(e, SC["a"], pr + 1)
                    link(e.tensor_scalar(z[:], z[:], 1.0, None, ALU.add))
                    link(e.reciprocal(z[:], z[:]))
                    for g in range(G3):
                        for s in range(2):
                            e.scalar_tensor_tensor(xs[:, s, g, :], dcv[:, g, s, :], z[:, g, s:s + 1], xs[:, s, g, :], ALU.mult, ALU.add).then_inc(SC["o"].handle, 1)
                    for g in range(G3):
                        wait(e, SC["o"], pr * 9 + 2 * g + 2)
                        for s in range(2):
                            for n in range(2):
                                last = e.bn_stats(sh["stat"][:, g, ds(pr * 2 + s, 1), n, :].rearrange("p o s -> p (o s)"), xs[:, s, g, n * HALF:(n + 1) * HALF])
                        last.then_inc(SC["o"].handle, 1)
                    hold(sh, e, SC["o"], pr * 9 + 9)
                    link.end()

                @block.scalar
                def _(e):
                    wait(e, SC["r"], pr * 6 + 4)
                    e.activation(z[:], z[:], ACT.Exp, scale=-1.0).then_inc(SC["a"].handle, 1)

                @block.tensor
                def _(e):
                    hold(sh, e, SC["r"], pr * 6 + 1)
                    for g in range(G3):
                        last = e.matmul(ps[2][0:HID, 0, 0:4], f1[:, g, :], pool[:, g, :, :].rearrange("p a s -> p (a s)"), start=(g == 0), stop=(g == G3 - 1))
                    last.then_inc(SC["p"].handle, 1)
                    hold(sh, e, SC["r"], pr * 6 + 2)
                    for g in range(G3):
                        last = e.matmul(ps[3][:, 0, 4 * g:4 * g + 4], f2[:, g, :], hid[:], start=True, stop=True)
                    last.then_inc(SC["p"].handle, 1)

        with nc.Block() as block:

            @block.sync
            def _(e):
                for g in range(G3):
                    wait(e, SA["x"][g], 16 * (B // 2 + 1))


def program(nc, t):
    with ExitStack() as ctx:
        def shared(name, shape, dt=F32):
            return ctx.enter_context(nc.sbuf_tensor(name, shape, dt))

        sh = {
            "tick": ctx.enter_context(nc.semaphore("tick")),
            "ident": shared("ident", [P, P]),
            "gmat": shared("gmat", [P, G3, GROUPS]),
            "gmatT": shared("gmatT", [GROUPS, G3, P]),
            "stat": shared("stat", [P, G3, B, 2, 6]),
            "gn": shared("gn", [P, G3, B, 2]),
        }
        load_shared(nc, sh, t)
        x1, x2, x3 = (nc.dram_tensor(f"x{i}", [B, C, N], F32).ap() for i in (1, 2, 3))
        layer0(nc, sh, t["x"], t["a_wqk"], t["a_wv"], t["a_wp"], t["a_bp"], x1)
        layer1(nc, sh, x1, t, x2)
        layer2(nc, sh, x2, t["c_wqk"], t["c_wvT"], t["c_wo"], t["c_temp"], t["c_bo"], x3)
        layer3(nc, sh, x3, [t[f"d_w{k}"] for k in range(CONVS)], t["d_bn"], t["out"])


def laid_out(i, np):
    f = np.float32
    t = {"x": i["x"].reshape(B, C, N)}
    t["ident"] = np.eye(P, dtype=f)
    member = (np.arange(C)[:, None] // CPG == np.arange(GROUPS)[None, :]).astype(f)
    t["gmat"] = member.reshape(G3, P, GROUPS)
    t["gmatT"] = member.T.reshape(GROUPS, G3, P)
    w = i["L0_conv_w_qkv"].T.reshape(C, 3, PAIRS, 2, D)
    qk = np.zeros((PAIRS, C, 2, 2, 64), f)
    qk[..., 0:D] = w[:, 0:2].transpose(2, 0, 1, 3, 4)
    t["a_wqk"] = qk.reshape(PAIRS, C, 2, 128)[..., 0:TP]
    t["a_wv"] = w[:, 2].reshape(C, C)
    wp = np.zeros((PAIRS, 2, 64, C), f)
    wp[:, :, 0:D] = i["L0_conv_w_proj"].T.reshape(PAIRS, 2, D, C)
    t["a_wp"] = wp.reshape(PAIRS, 128, C)[:, 0:TP].transpose(1, 0, 2)
    t["a_bp"] = i["L0_conv_b_proj"]
    spread = np.zeros((2, 2, PARTS, H, H, W), f)
    for r in range(H):
        for u in range(2):
            spread[u, u, :, r, r, :] = -1.0
    t["b_E"] = spread.reshape(2, P, H * W)
    t["b_minus"] = -(np.arange(P) % H).astype(f)[:, None]
    t["b_low"] = (np.arange(P) // H % PARTS).astype(f)[:, None]
    M7 = 2 * KS[-1] ** 2
    t["b_ymask"] = ((np.arange(M7) + 1) % 2).astype(f)[:, None]
    t["b_pw"] = np.stack([i[f"L1_conv_pw_w{K}"].reshape(P, P).T for K in KS])
    t["b_pb"] = np.stack([i[f"L1_conv_pw_b{K}"] for K in KS], 1)
    ob = np.zeros((M7, G3), f)
    for g, K in enumerate(KS):
        M, R = 2 * K * K, K // 2
        ob[0:M, g] = i[f"L1_conv_offset_b{K}"]
        t[f"b_ow{g}"] = i[f"L1_conv_offset_w{K}"].transpose(1, 2, 3, 0).reshape(P, K * K, M)
        t[f"b_dw{g}"] = i[f"L1_conv_dw_w{K}"].reshape(P, K * K).T
        grid = np.zeros((K, K, 2, H, W), f)
        grid[:, :, 0] = (np.arange(K)[:, None, None, None] - R + np.arange(H)[None, None, :, None])
        grid[:, :, 1] = (np.arange(K)[None, :, None, None] - R + np.arange(W)[None, None, None, :])
        t[f"b_grid{g}"] = grid.reshape(M, N)
    t["b_ob"] = ob
    t["b_f1"] = i["L1_conv_fc1_w"].reshape(HID, G3, P).transpose(1, 2, 0)
    t["b_f2"] = i["L1_conv_fc2_w"].reshape(G3, P, HID).transpose(2, 0, 1)
    w = i["L2_conv_w_qkv"].reshape(C, 3, C)
    t["c_wqk"] = w[:, 1::-1]
    wv = np.zeros((PAIRS, 2, 64, C), f)
    wv[:, :, 0:D] = w[:, 2].T.reshape(PAIRS, 2, D, C)
    t["c_wvT"] = wv.reshape(PAIRS, 128, C)[:, 0:TP].transpose(1, 0, 2)
    t["c_wo"] = i["L2_conv_w_out"].reshape(HEADS, D, C).transpose(1, 0, 2)
    t["c_temp"] = i["L2_conv_temperature"].reshape(HEADS)
    t["c_bo"] = i["L2_conv_b_out"]
    for k, name in enumerate(("lk_w", "w5", "w7a", "w7b", "w3a", "w3b", "w3c")):
        t[f"d_w{k}"] = i[f"L3_conv_{name}"].reshape(C, -1)
    t["d_bn"] = np.concatenate([i["L3_conv_obn"][None], i["L3_conv_br_bn"]]).transpose(2, 0, 1)
    return t


def kernel(**inputs):
    import numpy as np
    import concourse.bacc as bacc
    from concourse.bass_utils import run_bass_kernel_spmd as run

    nc = bacc.Bacc("TRN2", target_bir_lowering=False, num_devices=1)
    arrays, t = {}, {}
    for name, a in laid_out({k: np.asarray(v) for k, v in inputs.items()}, np).items():
        a = np.ascontiguousarray(a)
        arrays[f"in_{name}"] = a
        t[name] = nc.dram_tensor(f"in_{name}", a.shape, mybir.dt.from_np(a.dtype), kind="ExternalInput").ap()
    t["out"] = nc.dram_tensor("out_dram", [B, C, N], F32, kind="ExternalOutput").ap()
    program(nc, t)
    r = run(nc, [arrays], core_ids=[0])
    return r.results[0]["out_dram"].reshape(B, C, H, W)
```
